# Optimizing a Trainium2 kernel written in Bass

```python
import numpy as np
import jax
import jax.numpy as jnp

def _softmax(x, axis=-1):
    return jax.nn.softmax(x, axis=axis)

def _gelu(x):
    return jax.nn.gelu(x, approximate=True)

def _silu(x):
    return jax.nn.silu(x)

def _sigmoid(x):
    return jax.nn.sigmoid(x)

def _layernorm(x, axis=-1, eps=1e-05):
    m = jnp.mean(x, axis=axis, keepdims=True)
    v = jnp.var(x, axis=axis, keepdims=True)
    return (x - m) / jnp.sqrt(v + eps)

def _scatter_add(tgt, idx, src, axis=0):
    return tgt.at[idx].add(src)

def _segment_sum(src, seg, n):
    return jax.ops.segment_sum(src, seg, n)
kernel_name = 'mk_gnn_resnorm_d4_gnn_r32_1967af'

def setup_inputs(seed: int=0):
    np.random.seed(seed)
    _w = jnp.asarray

    def _rec_inputs():
        import jax
        import jax.numpy as jnp
        _gk = jax.random.key(seed)
        x = -0.0003713 + 1 * jax.random.normal(jax.random.fold_in(_gk, 1), (3125, 128), jnp.float32)
        _s = jax.random.randint(jax.random.fold_in(_gk, 2), (25000,), 0, 3125, jnp.int32)
        _d = jax.random.randint(jax.random.fold_in(_gk, 3), (25000,), 0, 3125, jnp.int32)
        _loop = jnp.arange(3125, dtype=jnp.int32)
        src = jnp.concatenate([_s, _d, _loop])
        dst = jnp.concatenate([_d, _s, _loop])
        _o = jnp.argsort(dst, stable=True)
        src = src[_o]
        dst = dst[_o]
        edge_type_4 = jax.random.randint(jax.random.fold_in(_gk, 13), (53125,), 0, 4, jnp.int32)
        edge_type_8 = jax.random.randint(jax.random.fold_in(_gk, 14), (53125,), 0, 8, jnp.int32)
        edge_weight = jax.random.uniform(jax.random.fold_in(_gk, 15), (53125,), jnp.float32, 0.0, 0.0625)
        return (x, src, dst, edge_type_4, edge_type_8, edge_weight)
    x, src, dst, edge_type_4, edge_type_8, edge_weight = _rec_inputs()

    def _L0_gnn_setup():
        import jax, jax.numpy as jnp
        import numpy as np
        N = 3125
        E = 50000
        D = 128
        NEG_SLOPE = 0.2
        EPS = 1e-12
        key = jax.random.key(seed)
        k1, k2, k3, k4, k5, k6 = jax.random.split(key, 6)
        ego = jax.random.normal(k1, (N, D), dtype=jnp.float32)
        std = float(np.sqrt(2.0 / (D + D)))
        W1 = jax.random.normal(k2, (D, D), dtype=jnp.float32) * std
        W2 = jax.random.normal(k3, (D, D), dtype=jnp.float32) * std
        b1 = jnp.zeros((1, D), dtype=jnp.float32)
        b2 = jnp.zeros((1, D), dtype=jnp.float32)
        src = jax.random.randint(k4, (E,), 0, N)
        dst = jax.random.randint(k5, (E,), 0, N)
        adj_vals = jax.random.uniform(k6, (E,), dtype=jnp.float32) * (1.0 / 16.0)
        return {'ego_embeddings': ego, 'W1': W1, 'W2': W2, 'b1': b1, 'b2': b2, 'adj_vals': adj_vals, 'src': src, 'dst': dst}
    _L0_gnn_all = _L0_gnn_setup()
    _L0_gnn_in = {k: v for k, v in _L0_gnn_all.items() if k in ('W1', 'W2', 'b1', 'b2')}
    del _L0_gnn_all

    def _L1_gnn_setup():
        import jax, jax.numpy as jnp
        import numpy as np
        N = 50000
        E = 25000
        DIN = 128
        H = 4
        C = 32
        EPS = 1e-05
        NEG_SLOPE = 0.2

        def layer_norm(x, g, b):
            m = jnp.mean(x, axis=-1, keepdims=True)
            v = jnp.mean((x - m) ** 2, axis=-1, keepdims=True)
            return (x - m) * jax.lax.rsqrt(v + EPS) * g + b

        def gat_conv(h, src, dst, W, att_src, att_dst, gat_b, n):
            xh = (h @ W).reshape(n, H, C)
            a_src = jnp.einsum('nhc,hc->nh', xh, att_src)
            a_dst = jnp.einsum('nhc,hc->nh', xh, att_dst)
            alpha = jax.nn.leaky_relu(a_src[src] + a_dst[dst], NEG_SLOPE)
            amax = jax.ops.segment_max(alpha, dst, num_segments=n)
            alpha = jnp.exp(alpha - amax[dst])
            denom = jax.ops.segment_sum(alpha, dst, num_segments=n)
            alpha = alpha / denom[dst]
            msg = xh[src] * alpha[:, :, None]
            out = jax.ops.segment_sum(msg, dst, num_segments=n)
            return out.reshape(n, H * C) + gat_b
        key = jax.random.key(seed)
        ks = jax.random.split(key, 14)
        s = 1.0 / np.sqrt(DIN)
        return {'x': jax.random.normal(ks[0], (N, DIN), dtype=jnp.float32), 'edge_index': jax.random.randint(ks[1], (2, E), 0, N, dtype=jnp.int64), 'ln1_g': jnp.ones((DIN,), jnp.float32), 'ln1_b': jnp.zeros((DIN,), jnp.float32), 'W': jax.random.normal(ks[2], (DIN, H * C), jnp.float32) * s, 'att_src': jax.random.normal(ks[3], (H, C), jnp.float32) * (1.0 / np.sqrt(C)), 'att_dst': jax.random.normal(ks[4], (H, C), jnp.float32) * (1.0 / np.sqrt(C)), 'gat_b': jnp.zeros((H * C,), jnp.float32), 'ln2_g': jnp.ones((H * C,), jnp.float32), 'ln2_b': jnp.zeros((H * C,), jnp.float32), 'w1': jax.random.normal(ks[5], (H * C, 2 * H * C), jnp.float32) * (1.0 / np.sqrt(H * C)), 'b1': jnp.zeros((2 * H * C,), jnp.float32), 'w2': jax.random.normal(ks[6], (2 * H * C, H * C), jnp.float32) * (1.0 / np.sqrt(2 * H * C)), 'b2': jnp.zeros((H * C,), jnp.float32)}
    _L1_gnn_all = _L1_gnn_setup()
    _L1_gnn_in = {k: v for k, v in _L1_gnn_all.items() if k in ('ln1_g', 'ln1_b', 'W', 'att_src', 'att_dst', 'gat_b', 'ln2_g', 'ln2_b', 'w1', 'b1', 'w2', 'b2')}
    del _L1_gnn_all

    def _L2_gnn_setup():
        import jax, jax.numpy as jnp
        import numpy as np
        N = 3125
        E = 20000
        D = 128
        R = 4
        ALPHA = 0.2

        def _lrelu(x):
            return jax.nn.leaky_relu(x, negative_slope=ALPHA)
        key = jax.random.key(seed)
        ks = jax.random.split(key, 14)
        s = 0.05
        return {'node_features': jax.random.normal(ks[0], (N, D), jnp.float32), 'edge_index': jax.random.randint(ks[1], (2, E), 0, N), 'edge_type': jax.random.randint(ks[2], (E,), 0, R), 'W_R': jax.random.normal(ks[3], (R, 2 * D, D), jnp.float32) * s, 'b_R': jax.random.normal(ks[4], (R, D), jnp.float32) * s, 'W_Q': jax.random.normal(ks[5], (R, D, D), jnp.float32) * s, 'b_Q': jax.random.normal(ks[6], (R, D), jnp.float32) * s, 'W_K': jax.random.normal(ks[7], (R, D, D), jnp.float32) * s, 'b_K': jax.random.normal(ks[8], (R, D), jnp.float32) * s, 'W_V': jax.random.normal(ks[9], (R, D, D), jnp.float32) * s, 'b_V': jax.random.normal(ks[10], (R, D), jnp.float32) * s, 'a_w': jax.random.normal(ks[11], (2 * D, 1), jnp.float32) * s, 'a_b': jax.random.normal(ks[12], (1,), jnp.float32) * s}
    _L2_gnn_all = _L2_gnn_setup()
    _L2_gnn_in = {k: v for k, v in _L2_gnn_all.items() if k in ('W_R', 'b_R', 'W_Q', 'b_Q', 'W_K', 'b_K', 'W_V', 'b_V', 'a_w', 'a_b')}
    del _L2_gnn_all

    def _L3_gnn_setup():
        import jax, jax.numpy as jnp
        import numpy as np
        N_NODES = 3125
        N_EDGES = 18750
        HID = 128
        N_ETYPES = 8
        key = jax.random.key(seed)
        ks = jax.random.split(key, 10)
        s = 1.0 / np.sqrt(HID)
        return {'h': jax.random.normal(ks[0], (N_NODES, HID), dtype=jnp.float32), 'edge_index': jax.random.randint(ks[1], (2, N_EDGES), 0, N_NODES, dtype=jnp.int64), 'edge_type': jax.random.randint(ks[2], (N_EDGES,), 0, N_ETYPES, dtype=jnp.int64), 'message_W': jax.random.uniform(ks[3], (N_ETYPES, HID, HID), jnp.float32, -s, s), 'message_b': jax.random.uniform(ks[4], (N_ETYPES, HID), jnp.float32, -s, s), 'gru_w_ih': jax.random.uniform(ks[5], (3 * HID, HID), jnp.float32, -s, s), 'gru_w_hh': jax.random.uniform(ks[6], (3 * HID, HID), jnp.float32, -s, s), 'gru_b_ih': jax.random.uniform(ks[7], (3 * HID,), jnp.float32, -s, s), 'gru_b_hh': jax.random.uniform(ks[8], (3 * HID,), jnp.float32, -s, s)}
    _L3_gnn_all = _L3_gnn_setup()
    _L3_gnn_in = {k: v for k, v in _L3_gnn_all.items() if k in ('message_W', 'message_b', 'gru_w_ih', 'gru_w_hh', 'gru_b_ih', 'gru_b_hh')}
    del _L3_gnn_all
    return {'x': x, 'src': src, 'dst': dst, 'edge_type_4': edge_type_4, 'edge_type_8': edge_type_8, 'edge_weight': edge_weight, 'L0_gnn_W1': _L0_gnn_in['W1'], 'L0_gnn_W2': _L0_gnn_in['W2'], 'L0_gnn_b1': _L0_gnn_in['b1'], 'L0_gnn_b2': _L0_gnn_in['b2'], 'L1_gnn_ln1_g': _L1_gnn_in['ln1_g'], 'L1_gnn_ln1_b': _L1_gnn_in['ln1_b'], 'L1_gnn_W': _L1_gnn_in['W'], 'L1_gnn_att_src': _L1_gnn_in['att_src'], 'L1_gnn_att_dst': _L1_gnn_in['att_dst'], 'L1_gnn_gat_b': _L1_gnn_in['gat_b'], 'L1_gnn_ln2_g': _L1_gnn_in['ln2_g'], 'L1_gnn_ln2_b': _L1_gnn_in['ln2_b'], 'L1_gnn_w1': _L1_gnn_in['w1'], 'L1_gnn_b1': _L1_gnn_in['b1'], 'L1_gnn_w2': _L1_gnn_in['w2'], 'L1_gnn_b2': _L1_gnn_in['b2'], 'L2_gnn_W_R': _L2_gnn_in['W_R'], 'L2_gnn_b_R': _L2_gnn_in['b_R'], 'L2_gnn_W_Q': _L2_gnn_in['W_Q'], 'L2_gnn_b_Q': _L2_gnn_in['b_Q'], 'L2_gnn_W_K': _L2_gnn_in['W_K'], 'L2_gnn_b_K': _L2_gnn_in['b_K'], 'L2_gnn_W_V': _L2_gnn_in['W_V'], 'L2_gnn_b_V': _L2_gnn_in['b_V'], 'L2_gnn_a_w': _L2_gnn_in['a_w'], 'L2_gnn_a_b': _L2_gnn_in['a_b'], 'L3_gnn_message_W': _L3_gnn_in['message_W'], 'L3_gnn_message_b': _L3_gnn_in['message_b'], 'L3_gnn_gru_w_ih': _L3_gnn_in['gru_w_ih'], 'L3_gnn_gru_w_hh': _L3_gnn_in['gru_w_hh'], 'L3_gnn_gru_b_ih': _L3_gnn_in['gru_b_ih'], 'L3_gnn_gru_b_hh': _L3_gnn_in['gru_b_hh']}

def reference(x, src, dst, edge_type_4, edge_type_8, edge_weight, L0_gnn_W1, L0_gnn_W2, L0_gnn_b1, L0_gnn_b2, L1_gnn_ln1_g, L1_gnn_ln1_b, L1_gnn_W, L1_gnn_att_src, L1_gnn_att_dst, L1_gnn_gat_b, L1_gnn_ln2_g, L1_gnn_ln2_b, L1_gnn_w1, L1_gnn_b1, L1_gnn_w2, L1_gnn_b2, L2_gnn_W_R, L2_gnn_b_R, L2_gnn_W_Q, L2_gnn_b_Q, L2_gnn_W_K, L2_gnn_b_K, L2_gnn_W_V, L2_gnn_b_V, L2_gnn_a_w, L2_gnn_a_b, L3_gnn_message_W, L3_gnn_message_b, L3_gnn_gru_w_ih, L3_gnn_gru_w_hh, L3_gnn_gru_b_ih, L3_gnn_gru_b_hh):
    import jax
    import jax.numpy as jnp

    def _L0_gnn_ref(ego_embeddings, W1, W2, b1, b2, adj_vals, src, dst):
        import jax, jax.numpy as jnp
        import numpy as np
        N = 3125
        E = 50000
        D = 128
        NEG_SLOPE = 0.2
        EPS = 1e-12
        msgs = ego_embeddings[src] * adj_vals[:, None]
        lap = jax.ops.segment_sum(msgs, dst, num_segments=ego_embeddings.shape[0])
        first = (ego_embeddings + lap) @ W1 + b1
        second = ego_embeddings * lap @ W2 + b2
        out = jax.nn.leaky_relu(first + second, negative_slope=NEG_SLOPE)
        norm = jnp.sqrt(jnp.sum(out * out, axis=1, keepdims=True))
        return out / jnp.maximum(norm, EPS)

    def _L1_gnn_ref(x, edge_index, ln1_g, ln1_b, W, att_src, att_dst, gat_b, ln2_g, ln2_b, w1, b1, w2, b2):
        import jax, jax.numpy as jnp
        import numpy as np
        N = 50000
        E = 25000
        DIN = 128
        H = 4
        C = 32
        EPS = 1e-05
        NEG_SLOPE = 0.2

        def layer_norm(x, g, b):
            m = jnp.mean(x, axis=-1, keepdims=True)
            v = jnp.mean((x - m) ** 2, axis=-1, keepdims=True)
            return (x - m) * jax.lax.rsqrt(v + EPS) * g + b

        def gat_conv(h, src, dst, W, att_src, att_dst, gat_b, n):
            xh = (h @ W).reshape(n, H, C)
            a_src = jnp.einsum('nhc,hc->nh', xh, att_src)
            a_dst = jnp.einsum('nhc,hc->nh', xh, att_dst)
            alpha = jax.nn.leaky_relu(a_src[src] + a_dst[dst], NEG_SLOPE)
            amax = jax.ops.segment_max(alpha, dst, num_segments=n)
            alpha = jnp.exp(alpha - amax[dst])
            denom = jax.ops.segment_sum(alpha, dst, num_segments=n)
            alpha = alpha / denom[dst]
            msg = xh[src] * alpha[:, :, None]
            out = jax.ops.segment_sum(msg, dst, num_segments=n)
            return out.reshape(n, H * C) + gat_b
        n = x.shape[0]
        loops = jnp.arange(n, dtype=edge_index.dtype)
        src = jnp.concatenate([edge_index[0], loops])
        dst = jnp.concatenate([edge_index[1], loops])
        h = layer_norm(x, ln1_g, ln1_b)
        h = gat_conv(h, src, dst, W, att_src, att_dst, gat_b, n)
        h = h + x
        hn = layer_norm(h, ln2_g, ln2_b)
        ffn = jax.nn.gelu(hn @ w1 + b1, approximate=False) @ w2 + b2
        return h + ffn

    def _L2_gnn_ref(node_features, edge_index, edge_type, W_R, b_R, W_Q, b_Q, W_K, b_K, W_V, b_V, a_w, a_b):
        import jax, jax.numpy as jnp
        import numpy as np
        N = 3125
        E = 20000
        D = 128
        R = 4
        ALPHA = 0.2

        def _lrelu(x):
            return jax.nn.leaky_relu(x, negative_slope=ALPHA)
        num_nodes = node_features.shape[0]
        src, tgt = (edge_index[0], edge_index[1])
        rel_in = jnp.concatenate([node_features[src], node_features[tgt]], axis=1)
        h = jnp.zeros_like(node_features)
        for r in range(R):
            mask = edge_type == r
            rel_t = _lrelu(rel_in @ W_R[r] + b_R[r])
            Q = rel_t @ W_Q[r] + b_Q[r]
            K = rel_t @ W_K[r] + b_K[r]
            V = rel_t @ W_V[r] + b_V[r]
            e = _lrelu(jnp.concatenate([Q, K], axis=1) @ a_w + a_b)[:, 0]
            e_m = jnp.where(mask, e, -1e+30)
            seg_max = jax.ops.segment_max(e_m, tgt, num_segments=num_nodes)
            seg_max = jnp.where(seg_max > -1e+29, seg_max, 0.0)
            ex = jnp.where(mask, jnp.exp(e - seg_max[tgt]), 0.0)
            denom = jax.ops.segment_sum(ex, tgt, num_segments=num_nodes)
            attn = ex / jnp.maximum(denom[tgt], 1e-16)
            h = h + jax.ops.segment_sum(V * attn[:, None], tgt, num_segments=num_nodes)
        return jax.nn.elu(h)

    def _L3_gnn_ref(h, edge_index, edge_type, message_W, message_b, gru_w_ih, gru_w_hh, gru_b_ih, gru_b_hh):
        import jax, jax.numpy as jnp
        import numpy as np
        N_NODES = 3125
        N_EDGES = 18750
        HID = 128
        N_ETYPES = 8
        num_nodes = h.shape[0]
        src, dst = (edge_index[0], edge_index[1])
        all_msgs = jnp.einsum('nh,thd->ntd', h, message_W) + message_b
        msg = all_msgs[src, edge_type]
        messages = jax.ops.segment_sum(msg, dst, num_segments=num_nodes)
        gi = messages @ gru_w_ih.T + gru_b_ih
        gh = h @ gru_w_hh.T + gru_b_hh
        i_r, i_z, i_n = jnp.split(gi, 3, axis=-1)
        h_r, h_z, h_n = jnp.split(gh, 3, axis=-1)
        r = jax.nn.sigmoid(i_r + h_r)
        z = jax.nn.sigmoid(i_z + h_z)
        n = jnp.tanh(i_n + r * h_n)
        return (1.0 - z) * n + z * h
    edge_index = jnp.stack([src, dst])
    x = _layernorm(x + _L0_gnn_ref(x, L0_gnn_W1, L0_gnn_W2, L0_gnn_b1, L0_gnn_b2, edge_weight, src, dst), axis=-1)
    x = _layernorm(x + _L1_gnn_ref(x, edge_index, L1_gnn_ln1_g, L1_gnn_ln1_b, L1_gnn_W, L1_gnn_att_src, L1_gnn_att_dst, L1_gnn_gat_b, L1_gnn_ln2_g, L1_gnn_ln2_b, L1_gnn_w1, L1_gnn_b1, L1_gnn_w2, L1_gnn_b2), axis=-1)
    x = _layernorm(x + _L2_gnn_ref(x, edge_index, edge_type_4, L2_gnn_W_R, L2_gnn_b_R, L2_gnn_W_Q, L2_gnn_b_Q, L2_gnn_W_K, L2_gnn_b_K, L2_gnn_W_V, L2_gnn_b_V, L2_gnn_a_w, L2_gnn_a_b), axis=-1)
    x = _layernorm(x + _L3_gnn_ref(x, edge_index, edge_type_8, L3_gnn_message_W, L3_gnn_message_b, L3_gnn_gru_w_ih, L3_gnn_gru_w_hh, L3_gnn_gru_b_ih, L3_gnn_gru_b_hh), axis=-1)
    return x

_drawn_inputs = setup_inputs


def setup_inputs(seed=0):
    import zlib

    import numpy as np

    out = dict(_drawn_inputs(seed))
    spreads = {'L0_gnn_b1': (0.0, 2.0),
     'L0_gnn_b2': (0.0, 2.0),
     'L1_gnn_ln1_g': (1.0, 0.2),
     'L1_gnn_ln1_b': (0.0, 0.1),
     'L1_gnn_gat_b': (0.0, 0.1),
     'L1_gnn_ln2_g': (1.0, 0.2),
     'L1_gnn_ln2_b': (0.0, 0.1),
     'L1_gnn_b1': (0.0, 0.1),
     'L1_gnn_b2': (0.0, 0.1)}
    factors = {'edge_weight': 6.264,
     'L0_gnn_W2': 4.301,
     'L2_gnn_W_Q': 4.601,
     'L2_gnn_b_Q': 46.726,
     'L2_gnn_W_K': 5.12,
     'L2_gnn_b_K': 50.058,
     'L2_gnn_a_w': 3.736,
     'L3_gnn_gru_b_ih': 4.521,
     'L3_gnn_gru_b_hh': 5.963}
    for name, (base, spread) in spreads.items():
        noise = np.random.default_rng([zlib.crc32(name.encode()), seed]).standard_normal(out[name].shape)
        drawn = base * np.exp(spread * noise) if base else spread * noise
        out[name] = jnp.asarray(drawn.astype(out[name].dtype))
    for name, factor in factors.items():
        out[name] = (out[name] * factor).astype(out[name].dtype)
    return out
```

```python
import concourse.bass as bass
from concourse import mybir
from contextlib import ExitStack


class Chain:

    def __init__(self, engine, sem):
        self.engine, self.sem, self.done, self.turn, self.per = engine, sem, 0, None, 0

    def begin(self, turn, per):
        self.turn, self.per, self.first = turn, per, self.done

    def end(self, turns):
        assert self.done - self.first == self.per, (self.done - self.first, self.per)
        self.done, self.turn = self.first + turns * self.per, None

    def link(self, ins):
        ins.then_inc(self.sem, 1)
        self.done += 1
        self.engine.wait_ge(self.sem, self.done if self.turn is None else self.turn * self.per + self.done)


def gnn_stack(nc, t, out, layers=4):
    f32, i32, bf16, f16 = mybir.dt.float32, mybir.dt.int32, mybir.dt.bfloat16, mybir.dt.float16
    ALU, ACT, AX = mybir.AluOpType, mybir.ActivationFunctionType, mybir.AxisListType

    P = 128
    N, D = t["x"].shape
    E = t["src"].shape[0]
    NJ = 26
    NV = -(-N // P)
    LASTN = N - (NV - 1) * P
    Q = -(-E // 512)
    LASTE = E - (Q - 1) * 512
    NI = 440
    assert NI >= 4 * Q + NV - 1 and NI % 8 == 0
    QI = NI // 4
    IT = NI // 8
    SL, G = 4, 2
    H, C = t["L1_gnn_att_src"].shape
    R = t["L2_gnn_W_R"].shape[0]
    T8 = t["L3_gnn_message_W"].shape[0]
    W1C = D + H
    BIG = 1e30
    FAR = 1e4

    with ExitStack() as ctx:
        sb = lambda name, shape, dt=f32: ctx.enter_context(nc.sbuf_tensor(name, shape, dt))
        sem = lambda name: ctx.enter_context(nc.semaphore(name))
        dram = lambda name, shape: nc.dram_tensor(name, shape, f32, kind="Internal").ap()

        table1 = dram("table1", [NJ * P, W1C])
        spill1 = dram("spill1", [NI // G, P, G * W1C])
        table2 = dram("table2", [NJ * P * R, D])
        spill2 = dram("spill2", [NI // G, P, G * D])
        table3 = dram("table3", [NJ * P * T8, D])

        X = sb("X", [P, NJ, D])
        Y = sb("Y", [P, NJ, D])
        wide = sb("wide", [P, NJ, R * (D + 1)])
        acc = wide
        Btab = wide[:, :, 0:R * D]
        acc0 = acc[:, :, 0:D]
        acc1 = acc[:, :, 0:W1C + H]
        xh = wide[:, :, 384:384 + W1C]
        own = sb("own", [P, 3, NJ, H])
        big = wide[:, :, 256:256 + D]
        ad = sb("ad", [P, NJ, H])
        stats = sb("stats", [P, NJ, 6])
        col = [sb(f"col{n}", [P, NJ]) for n in range(6)]

        ints = {n: sb(f"int_{n}", [QI, 512], i32) for n in ("src", "dst", "t4", "t8")}
        rows = {n: sb(f"row_{n}", [QI, 512]) for n in ("src", "dst", "t4", "t8", "w", "j")}
        tile_i = sb("tile_i", [Q, 8], i32)
        tile_f = sb("tile_f", [Q, 8, 4])
        spread = acc[0:Q, 0:4, 0:NI]
        iota = sb("iota", [P, 512])
        iota16 = sb("iota16", [P, 512], f16)
        ident = sb("ident", [P, P])
        ident16 = sb("ident16", [P, P], bf16)
        upper = sb("upper", [P, P])
        itab = {n: sb(f"item_{n}", [P, NI], i32) for n in ("j", "src", "src4", "src8")}
        fields = ("rel", "w", "key4", "dst", "ok", "t4", "jf")
        item_f = sb("item_f", [P, len(fields), NI])
        ftab = {n: item_f[:, m, :] for m, n in enumerate(fields)}
        late = item_f[:, 3:7, :].rearrange("p m i -> p (m i)")
        score = sb("score", [P, NI, H])
        weight = sb("weight", [P, NI, H])
        rdst, rok, rt4, rneg, rg, rscr = (rows[n][:, :] for n in ("src", "dst", "t4", "j", "t8", "w"))
        rkey = sb("rkey", [QI, 513])
        reset = sb("reset", [QI, 513])
        rv = [sb(f"rv{h}", [QI, 512]) for h in range(H)]
        rf = [ints[n][:, :].bitcast(f32) for n in ("src", "dst", "t4", "t8")]
        ends = sb("ends", [QI, 4])
        resets_row = sb("resets_row", [4, QI])
        before_row = sb("before_row", [4, QI + 1])
        after_row = sb("after_row", [4, QI + 1])
        carry = sb("carry", [QI, 4])

        ix = sb("ix", [P, SL, G], i32)
        ring = sb("ring", [P, SL, G, W1C + H])
        ring2 = sb("ring2", [P, SL, G, D + 1])
        oneh = sb("oneh", [P, SL, G, P])
        onehT = sb("onehT", [P, SL, G, P])
        oneh4 = sb("oneh4", [P, SL, G, R * P], bf16)
        y_flat, weight_flat = Y[:, :, :].rearrange("p j d -> p (j d)"), weight[:, :, :].rearrange("p i h -> p (i h)")
        wide4 = [(weight_flat[:, 0:G * R * P] if b == 3 else y_flat[:, b * G * R * P:(b + 1) * G * R * P])
                 .rearrange("p (g f) -> p g f", g=G) for b in range(SL)]
        stg = sb("stg", [P, 2, R + 1, D])
        tT = sb("tT", [P, 2, R + 1, D])
        W0 = sb("W0", [P, 2, D])
        bias0 = sb("bias0", [P, 2, D])
        WX = sb("WX", [P, D + 2 * H])
        pool1 = oneh4[:, :, :, :].rearrange("p s g f -> p (s g f)").bitcast(f32)
        rowv = {n: pool1[:, m * D:(m + 1) * D] for m, n in enumerate(("ln1_g", "ln1_b", "gat_b", "ln2_g", "ln2_b", "b2"))}
        att = pool1[:, 6 * D:8 * D].rearrange("p (n d) -> p n d", n=2)
        scaled_w = pool1[:, 8 * D:10 * D].rearrange("p (n d) -> p n d", n=2)
        w1 = pool1[:, 10 * D:12 * D]
        w2 = pool1[:, 12 * D:14 * D].rearrange("p (n d) -> p n d", n=2)
        b1 = sb("b1", [P, 2])
        gelT = sb("gelT", [P, 2, 2, D])
        trow = sb("trow", [P, 2, T8 * D])
        WRs, WRd = (late[:, n * R * D:(n + 1) * R * D].rearrange("p (r d) -> p r d", d=D) for n in range(2))
        bR = late[:, 2 * R * D:3 * R * D]
        WV = sb("WV", [P, R, D])
        bV = sb("bV", [R, D])
        attq = sb("attq", [P, 2, D])
        a_b = sb("a_b", [P, 1])
        u4 = sb("u4", [P, 2, R])
        c4 = sb("c4", [P, 2, R])
        c4q = trow[:, 1, :].rearrange("p (n f) -> p n f", n=2)
        W3 = pool1[:, 0:T8 * D].rearrange("p (t d) -> p t d", d=D)
        b3 = pool1[:, T8 * D:2 * T8 * D]
        gru_rows = ring2[:, :, :, :].rearrange("p s g f -> p (s g f)")[:, 0:6 * D].rearrange("p (n d) -> p n d", d=D)
        gruT = weight_flat[:, 0:6 * D].rearrange("p (n d) -> p n d", n=2)
        gru_b = weight_flat[:, 6 * D:10 * D]
        gru_b2 = weight_flat[:, 10 * D:12 * D]

        PS = ctx.enter_context(nc.psum_tensor("PS", [P, 8, 512], f32))

        s_in = sem("edges_in")
        s_w = sem("weights_in")
        s_pad = sem("pads_set")
        s_const = sem("constants_made")
        s_const2 = sem("constants_shaped")
        s_chain = sem("vector_step")
        s_first = sem("tile_counts_summed")
        s_pre = sem("tile_prefix")
        s_spread = sem("spread_ready")
        s_items = sem("items_spread")
        s_tabs = sem("item_tables_ready")
        s_ix = [sem(f"indices_staged{b}") for b in range(SL)]
        s_rows = [sem(f"rows_gathered{b}") for b in range(SL)]
        s_oh = [sem(f"onehot_built{b}") for b in range(SL)]
        s_scat = [sem(f"rows_scattered{b}") for b in range(SL)]
        s_acc = sem("sums_added")
        s_staged = [sem(f"tile_staged{b}") for b in range(2)]
        s_turned = [sem(f"tile_turned{b}") for b in range(2)]
        s_tcopy = [sem(f"turned_copied{b}") for b in range(2)]
        s_prod = [sem(f"tile_product{b}") for b in range(2)]
        s_take = [sem(f"product_taken{b}") for b in range(2)]
        s_sq = sem("square_in")
        s_sqd = sem("squared")
        s_var = sem("root_in")
        s_std = sem("root_out")
        s_out = sem("out_written")
        s_w1 = sem("layer1_weights_in")
        s_ready = sem("node_rows_ready")
        s_written = [sem(f"table_rows_written{b}") for b in range(2)]
        s_tfree = [sem(f"table_rows_free{b}") for b in range(2)]
        s_table = sem("table_complete")
        s_ohturn = [sem(f"onehot_turned{b}") for b in range(SL)]
        s_ohT = [sem(f"turned_onehot_copied{b}") for b in range(SL)]
        s_spread1 = [sem(f"dst_values_spread{b}") for b in range(SL)]
        s_scored = [sem(f"scores_stored{b}") for b in range(SL)]
        s_spill = [sem(f"rows_spilled{b}") for b in range(SL)]
        s_spfree = [sem(f"spilled_rows_free{b}") for b in range(SL)]
        s_back = [sem(f"rows_back{b}") for b in range(SL)]
        s_scaled = [sem(f"rows_weighted{b}") for b in range(SL)]
        s_torow = sem("values_for_rows")
        s_inrow = sem("values_in_rows")
        s_ends = sem("row_ends")
        s_endsT = sem("row_ends_turned")
        s_scan = sem("rows_scanned")
        s_scanT = sem("row_carries")
        s_exin = sem("exponents")
        s_max = sem("maxima_at_starts")
        s_maxT = sem("maxima_turned")
        s_own = sem("own_exponents")
        s_w2 = sem("layer2_weights_in")
        s_w3 = sem("layer3_weights_in")
        s_added = [sem(f"relation_sums{b}") for b in range(SL)]
        s_relu = [sem(f"relation_rows{b}") for b in range(SL)]
        s_relT = [sem(f"relation_rows_turned{b}") for b in range(SL)]
        s_relTc = [sem(f"turned_relation_rows_copied{b}") for b in range(SL)]
        s_s4 = [sem(f"relation_scores{b}") for b in range(SL)]
        s_elu = sem("elu_in")
        s_elud = sem("elu_exponential")
        s_gruT = sem("gru_weights_turned")
        s_gate = sem("gates_in")
        s_gated = sem("gates_out")
        s_ownx = sem("own_exponentials")
        s_ex = sem("exponentials")
        s_exT = sem("exponentials_turned")
        s_mid = [sem(f"gelu_done{b}") for b in range(2)]
        s_prod2 = [sem(f"second_product{b}") for b in range(2)]
        s_final = sem("x_final")

        def window(b, it):
            return it * (SL * G) + b * G

        with nc.Block() as block:

            @block.sync
            def _(sp):
                sp.wait_ge(s_pad, 1)
                for name, key in (("src", "src"), ("dst", "dst"), ("t4", "edge_type_4"), ("t8", "edge_type_8")):
                    a = t[key]
                    sp.dma_start(ints[name][0:Q - 1, :], a[0:(Q - 1) * 512].rearrange("(q e) -> q e", e=512)).then_inc(s_in, 16)
                    sp.dma_start(ints[name][Q - 1:Q, 0:LASTE], a[(Q - 1) * 512:E].rearrange("(q e) -> q e", q=1)).then_inc(s_in, 16)
                a = t["edge_weight"]
                sp.dma_start(rows["w"][0:Q - 1, :], a[0:(Q - 1) * 512].rearrange("(q e) -> q e", e=512)).then_inc(s_in, 16)
                sp.dma_start(rows["w"][Q - 1:Q, 0:LASTE], a[(Q - 1) * 512:E].rearrange("(q e) -> q e", q=1)).then_inc(s_in, 16)
                sp.dma_start(X[:, 0:NV - 1, :], t["x"][0:(NV - 1) * P, :].rearrange("(j p) d -> p j d", p=P)).then_inc(s_w, 16)
                sp.dma_start(X[0:LASTN, NV - 1, :], t["x"][(NV - 1) * P:N, :]).then_inc(s_w, 16)
                sp.dma_start(W0[:, 0, :], t["L0_gnn_W1"]).then_inc(s_w, 16)
                sp.dma_start(W0[:, 1, :], t["L0_gnn_W2"]).then_inc(s_w, 16)
                sp.dma_start(bias0[:, 0, :], t["L0_gnn_b1"][0, :].partition_broadcast(P)).then_inc(s_w, 16)
                sp.dma_start(bias0[:, 1, :], t["L0_gnn_b2"][0, :].partition_broadcast(P)).then_inc(s_w, 16)
                if layers > 1:
                    sp.dma_start(WX[:, 0:D], t["L1_gnn_W"]).then_inc(s_w1, 16)
                    for n, name in enumerate(("L1_gnn_att_src", "L1_gnn_att_dst")):
                        sp.dma_start(att[:, n, :], t[name].rearrange("h c -> (h c)").partition_broadcast(P)).then_inc(s_w1, 16)
                    for name, tile in rowv.items():
                        sp.dma_start(tile, t["L1_gnn_" + name].partition_broadcast(P)).then_inc(s_w1, 16)
                    sp.dma_start(w1[:, :], t["L1_gnn_w1"]).then_inc(s_w1, 16)
                    sp.dma_start(w2[:, :, :], t["L1_gnn_w2"].rearrange("(a p) d -> p a d", p=P)).then_inc(s_w1, 16)
                    sp.dma_start(b1[:, :], t["L1_gnn_b1"].rearrange("(a p) -> p a", p=P),
                                 allow_slow_non_contiguous=True).then_inc(s_w1, 16)

                    def write_table(phase, base, table, width, row=None):
                        view = table.rearrange("(j p) d -> j p d", p=P)
                        with sp.Fori(0, NJ // 2) as it:
                            for b in range(2):
                                sp.wait_ge(s_take[b], it + (base + 2))
                                sp.dma_start(view[bass.ds(it * 2 + b, 1), :, :].rearrange("o p d -> (o p) d"),
                                             trow[:, b, 0:width] if row is None else
                                             row[:, bass.ds(it * 2 + b, 1), :].rearrange("p o d -> p (o d)")).then_inc(s_written[b], 16)
                            for b in range(2):
                                sp.wait_ge(s_written[b], it * 16 + (phase * (NJ // 2) * 16 + 16))
                                sp.sem_inc(s_tfree[b], 1)
                        sp.sem_inc(s_table, 1)

                    def spill(base, gathered, ring_tile, width, store):
                        with sp.Fori(0, IT) as it:
                            for b in range(SL):
                                sp.wait_ge(*gathered(b, it))
                                sp.dma_start(store[bass.ds(it * SL + b, 1), :, :].rearrange("o p d -> (o p) d").rearrange("p (g d) -> p g d", g=G),
                                             ring_tile[:, b, :, 0:width]).then_inc(s_spill[b], 16)
                            for b in range(SL):
                                sp.wait_ge(s_spill[b], it * 16 + (base * 16 + 16))
                                sp.sem_inc(s_spfree[b], 1)

                    def unspill(base, ring_tile, width, store):
                        with sp.Fori(0, IT) as it:
                            for b in range(SL):
                                sp.wait_ge(s_scat[b], it + (base + 1))
                                sp.dma_start(ring_tile[:, b, :, 0:width],
                                             store[bass.ds(it * SL + b, 1), :, :].rearrange("o p d -> (o p) d").rearrange("p (g d) -> p g d", g=G)).then_inc(s_back[b], 16)

                    write_table(0, 13, table1, W1C, xh)
                    spill(0, lambda b, it: (s_rows[b], it * (16 * G) + (IT + 1) * 16 * G), ring, W1C, spill1)
                    for b in range(SL):
                        sp.wait_ge(s_scored[b], 1 + IT)
                    unspill(IT, ring, W1C, spill1)
                if layers > 2:
                    sp.wait_ge(s_inrow, 1)
                    flat2 = lambda a: a.rearrange("a d -> (a d)").partition_broadcast(P)
                    sp.dma_start(WRs[:, :, :], t["L2_gnn_W_R"][:, 0:D, :].rearrange("r k d -> k r d")).then_inc(s_w2, 16)
                    sp.dma_start(WRd[:, :, :], t["L2_gnn_W_R"][:, D:2 * D, :].rearrange("r k d -> k r d")).then_inc(s_w2, 16)
                    sp.dma_start(WV[:, :, :], t["L2_gnn_W_V"].rearrange("r k d -> k r d")).then_inc(s_w2, 16)
                    sp.dma_start(trow[:, 0, 0:R * D].rearrange("p (r d) -> p r d", d=D), t["L2_gnn_W_Q"].rearrange("r k d -> k r d")).then_inc(s_w2, 16)
                    sp.dma_start(trow[:, 0, R * D:2 * R * D].rearrange("p (r d) -> p r d", d=D), t["L2_gnn_W_K"].rearrange("r k d -> k r d")).then_inc(s_w2, 16)
                    sp.dma_start(c4q[:, 0, :], flat2(t["L2_gnn_b_Q"])).then_inc(s_w2, 16)
                    sp.dma_start(c4q[:, 1, :], flat2(t["L2_gnn_b_K"])).then_inc(s_w2, 16)
                    sp.dma_start(bR[:, :], flat2(t["L2_gnn_b_R"])).then_inc(s_w2, 16)
                    sp.dma_start(bV[:, :], t["L2_gnn_b_V"]).then_inc(s_w2, 16)
                    sp.dma_start(attq[:, 0, :], flat2(t["L2_gnn_a_w"][0:D, :])).then_inc(s_w2, 16)
                    sp.dma_start(attq[:, 1, :], flat2(t["L2_gnn_a_w"][D:2 * D, :])).then_inc(s_w2, 16)
                    sp.dma_start(a_b[:, :], t["L2_gnn_a_b"].partition_broadcast(P)).then_inc(s_w2, 16)
                    write_table(1, 39, table2.rearrange("(n r) d -> n (r d)", r=R), R * D)
                    spill(IT, lambda b, it: (s_relu[b], it + 1), ring2, D, spill2)
                    for b in range(SL):
                        sp.wait_ge(s_scored[b], 1 + 2 * IT)
                    unspill(2 * IT, ring2, D, spill2)
                if layers > 3:
                    sp.wait_ge(s_acc, 9 + 3 * NI)
                    sp.dma_start(W3[:, :, :], t["L3_gnn_message_W"].rearrange("t k d -> k t d")).then_inc(s_w3, 16)
                    sp.dma_start(b3[:, :], flat2(t["L3_gnn_message_b"])).then_inc(s_w3, 16)
                    sp.dma_start(gru_rows[:, 0:3, :], t["L3_gnn_gru_w_ih"].rearrange("(a p) d -> p a d", p=P)).then_inc(s_w3, 16)
                    sp.dma_start(gru_rows[:, 3:6, :], t["L3_gnn_gru_w_hh"].rearrange("(a p) d -> p a d", p=P)).then_inc(s_w3, 16)
                    sp.dma_start(gru_b[:, 0:3 * D], t["L3_gnn_gru_b_ih"].partition_broadcast(P)).then_inc(s_w3, 16)
                    sp.dma_start(gru_b[:, 3 * D:4 * D], t["L3_gnn_gru_b_hh"][2 * D:3 * D].partition_broadcast(P)).then_inc(s_w3, 16)
                    sp.dma_start(gru_b2[:, :], t["L3_gnn_gru_b_hh"][0:2 * D].partition_broadcast(P)).then_inc(s_w3, 16)
                    write_table(2, 65, table3.rearrange("(n t) d -> n (t d)", t=T8), T8 * D)
                sp.wait_ge(s_final, 1)
                sp.dma_start(out[0:(NV - 1) * P, :].rearrange("(j p) d -> p j d", p=P), X[:, 0:NV - 1, :]).then_inc(s_out, 16)
                sp.dma_start(out[(NV - 1) * P:N, :], X[0:LASTN, NV - 1, :]).then_inc(s_out, 16)
                sp.wait_ge(s_out, 32)

            @block.gpsimd
            def _(pool):
                pool.iota(iota[:, :], [[1, 512]], base=0, channel_multiplier=0,
                          allow_small_or_imprecise_dtypes=True)
                pool.iota(iota16[:, :], [[1, 512]], base=0, channel_multiplier=0,
                          allow_small_or_imprecise_dtypes=True)
                pool.memset(ident[:, :], 0.0)
                pool.memset(ident16[:, :], 0.0)
                pool.memset(upper[:, :], 1.0).then_inc(s_const, 1)
                pool.wait_ge(s_const, 1)
                for m in (ident, ident16):
                    pool.affine_select(out=m[:, :], in_=m[:, :], compare_op=ALU.not_equal, fill=1.0,
                                       base=0, pattern=[[-1, P]], channel_multiplier=1)
                pool.affine_select(out=upper[:, :], in_=upper[:, :], compare_op=ALU.is_gt, fill=0.0,
                                   base=0, pattern=[[1, P]], channel_multiplier=-1).then_inc(s_const2, 1)

                def gather_loop(turns0, table, ring_tile, width, tables=0):
                    if tables:
                        pool.wait_ge(s_table, tables)
                    arm = [pool.alloc_register(f"gather_turn{turns0}_{b}") for b in range(SL)]
                    for b in range(SL):
                        pool.reg_mov(arm[b], turns0)
                    with pool.Fori(0, IT) as it:
                        for b in range(SL):
                            pool.reg_add(arm[b], arm[b], 1)
                            pool.wait_ge(s_const2, 1)
                            pool.wait_ge(s_ix[b], arm[b])
                            for k in range(G):
                                pool.indirect_dma_start(
                                    ring_tile[:, b, k, 0:width], None, table,
                                    bass.IndirectOffsetOnAxis(ap=ix[:, b, k:k + 1], axis=0)).then_inc(s_rows[b], 16)

                gather_loop(0, t["x"], ring, D)
                if layers > 1:
                    gather_loop(IT, table1, ring, W1C, 1)
                if layers > 2:
                    gather_loop(2 * IT, table2, ring, D, 2)
                if layers > 3:
                    gather_loop(3 * IT, table3, ring, D, 3)

            @block.scalar
            def _(act):
                chain = 0

                def stage_indices(table, turns0, it, b):
                    act.wait_ge(s_scat[b], it + (turns0 + 1))
                    act.copy(ix[:, b, :], table[:, bass.ds(window(b, it), G)]).then_inc(s_ix[b], 1)

                def copy_turned(base, it, b, width, n=1):
                    act.wait_ge(s_turned[b], it + (base + 2))
                    act.wait_ge(s_prod[b], it + (base + 1))
                    act.copy(tT[:, b, 0:n, :], PS[:, 4 + b, 0:n * D].rearrange("p (n d) -> p n d", d=D)).then_inc(s_tcopy[b], 1)

                def roots(n):
                    act.wait_ge(s_var, n + 1)
                    act.activation(col[1][:, :], col[0][:, :], ACT.Sqrt).then_inc(s_std, 1)

                act.wait_ge(s_tabs, 1)
                with act.Fori(0, IT) as it:
                    for b in range(SL):
                        stage_indices(itab["src"], 0, it, b)
                with act.Fori(0, NJ // 2) as it:
                    for b in range(2):
                        copy_turned(0, it, b, D, 2)
                act.wait_ge(s_sq, 1)
                act.activation(big, Y[:, :, :], ACT.Square).then_inc(s_sqd, 1)
                roots(0)
                roots(1)
                if layers > 1:
                    def stage_tile(source, base, it, b):
                        act.wait_ge(s_turned[b], it + (base + 1))
                        act.copy(stg[:, b, 0, :], source[:, bass.ds(it * 2 + b, 1), :].rearrange("p o d -> p (o d)")).then_inc(s_staged[b], 1)

                    roots(2)
                    act.wait_ge(s_ready, 1)
                    with act.Fori(0, NJ // 2) as it:
                        for b in range(2):
                            stage_tile(Y, 13, it, b)
                        for b in range(2):
                            copy_turned(13, it, b, D)
                    with act.Fori(0, IT) as it:
                        for b in range(SL):
                            act.wait_ge(s_scored[b], it + 1)
                            act.wait_ge(s_spfree[b], it + 1)
                            act.copy(ix[:, b, :], itab["src"][:, bass.ds(window(b, it), G)]).then_inc(s_ix[b], 1)
                        for b in range(SL):
                            act.wait_ge(s_ohturn[b], it + 2)
                            act.wait_ge(s_spread1[b], it + 1)
                            act.copy(onehT[:, b, :, :], PS[:, b, 0:G * P].rearrange("p (g d) -> p g d", g=G)).then_inc(s_ohT[b], 1)

                    def exponentials(n, tiles):
                        for h in range(H):
                            act.wait_ge(s_exin, n * H + h + 1)
                            act.activation(tiles[h][:, :], tiles[h][:, :], ACT.Exp, scale=-1.0).then_inc(s_ex, 1)

                    exponentials(0, rv)
                    act.wait_ge(s_own, 1)
                    act.activation(own[:, 0:2, :, :], own[:, 0:2, :, :], ACT.Exp, scale=-1.0).then_inc(s_ownx, 1)
                    roots(3)
                    act.wait_ge(s_ready, 2)
                    with act.Fori(0, NJ // 2) as it:
                        for b in range(2):
                            stage_tile(big, 26, it, b)
                        for b in range(2):
                            copy_turned(26, it, b, D)
                        for b in range(2):
                            act.wait_ge(s_prod[b], it + 28)
                            act.wait_ge(s_prod2[b], it + 1)
                            act.activation(gelT[:, b, 0, :], PS[:, 6 + b, 0:D], ACT.Gelu, bias=b1[:, 0:1])
                            act.activation(gelT[:, b, 1, :], PS[:, 6 + b, D:2 * D], ACT.Gelu, bias=b1[:, 1:2]).then_inc(s_mid[b], 1)
                    roots(4)
                if layers > 2:
                    act.wait_ge(s_ready, 3)
                    with act.Fori(0, NJ // 2) as it:
                        for b in range(2):
                            stage_tile(X, 39, it, b)
                        for b in range(2):
                            copy_turned(39, it, b, D)
                    with act.Fori(0, IT) as it:
                        for b in range(SL):
                            act.wait_ge(s_added[b], it + 1)
                            act.copy(ix[:, b, :], itab["src4"][:, bass.ds(window(b, it), G)]).then_inc(s_ix[b], 1)
                        for b in range(SL):
                            act.wait_ge(s_ohturn[b], it + (IT + 2))
                            act.wait_ge(s_spread1[b], it + (IT + 1))
                            act.copy(wide4[b], PS[:, b, :].bitcast(bf16).rearrange("p (g f) -> p g f", g=G)).then_inc(s_ohT[b], 1)
                        for b in range(SL):
                            act.wait_ge(s_relT[b], it + 1)
                            act.copy(onehT[:, b, :, :], PS[:, 4 + b, G * P:2 * G * P].rearrange("p (g d) -> p g d", g=G)).then_inc(s_relTc[b], 1)
                    exponentials(1, rv)
                    with act.Fori(0, NJ // 2) as it:
                        for b in range(2):
                            act.wait_ge(s_turned[b], it + 54)
                            act.wait_ge(s_prod[b], it + 53)
                            act.copy(tT[:, b, 0:R, :], PS[:, 4 + b, :].rearrange("p (n d) -> p n d", d=D))
                            act.copy(tT[0:R, b, R, :], PS[0:R, 2 + b, 0:D]).then_inc(s_tcopy[b], 1)
                    act.wait_ge(s_elu, 1)
                    act.activation(big, big, ACT.Exp).then_inc(s_elud, 1)
                    roots(5)
                if layers > 3:
                    act.wait_ge(s_gruT, 1)
                    for n in range(2):
                        ins = act.copy(gruT[:, n, :], PS[:, n, 0:3 * D])
                    act.wait_ge(s_ready, 4)
                    with act.Fori(0, NJ // 2) as it:
                        for b in range(2):
                            stage_tile(X, 65, it, b)
                        for b in range(2):
                            copy_turned(65, it, b, D)
                    with act.Fori(0, IT) as it:
                        for b in range(SL):
                            stage_indices(itab["src8"], 3 * IT, it, b)
                    act.wait_ge(s_ready, 5)
                    with act.Fori(0, NJ // 2) as it:
                        for b in range(2):
                            act.wait_ge(s_turned[b], it + 79)
                            act.copy(stg[:, b, 0, :], X[:, bass.ds(it * 2 + b, 1), :].rearrange("p o d -> p (o d)"))
                            act.copy(stg[:, b, 1, :], acc0[:, bass.ds(it * 2 + b, 1), :].rearrange("p o d -> p (o d)")).then_inc(s_staged[b], 1)
                        for b in range(2):
                            copy_turned(78, it, b, D, 2)
                    act.wait_ge(s_gate, 1)
                    act.activation(wide[:, :, 0:2 * D], wide[:, :, 0:2 * D], ACT.Sigmoid).then_inc(s_gated, 1)
                    act.wait_ge(s_gate, 2)
                    act.activation(wide[:, :, 2 * D:3 * D], wide[:, :, 2 * D:3 * D], ACT.Tanh).then_inc(s_gated, 1)
                    roots(6)

            @block.tensor
            def _(pe):
                pe.wait_ge(s_const2, 1)
                for b in range(2):
                    pe.sem_inc(s_turned[b], 1)
                    pe.sem_inc(s_prod[b], 1)
                    pe.sem_inc(s_prod2[b], 1)
                for b in range(SL):
                    pe.sem_inc(s_scat[b], 1)
                    pe.sem_inc(s_ohturn[b], 1)
                    pe.sem_inc(s_spread1[b], 1)
                pe.wait_ge(s_first, 1)
                pe.matmul(PS[0:Q, 6, 0:1], upper[0:Q, 0:Q], tile_f[:, 4, 3:4], start=True, stop=True).then_inc(s_pre, 1)
                pe.wait_ge(s_spread, 1)
                for n, name in enumerate(("src", "dst", "t4", "t8", "w", "j")):
                    for k in range(4):
                        mm = pe.matmul(PS[:, n, 0:NI], rows[name][0:Q, k * P:(k + 1) * P], spread[:, k, :],
                                       start=k == 0, stop=k == 3)
                mm.then_inc(s_items, 1)

                def scatter(first, arrived, ohs, it, b, width):
                    pe.wait_ge(*arrived)
                    pe.wait_ge(s_oh[b], it + (ohs + 1))
                    pe.wait_ge(s_acc, it * (SL * G) + (first + b * G + G - SL * G))
                    for k in range(G):
                        mm = pe.matmul(PS[:, b, k * 256:k * 256 + width], oneh[:, b, k, :], ring[:, b, k, 0:width],
                                       start=True, stop=True)
                    mm.then_inc(s_scat[b], 1)

                def turn(base, it, b, n=1):
                    pe.wait_ge(s_staged[b], it + (base + 2))
                    pe.wait_ge(s_tcopy[b], it + (base + 1))
                    for m in range(n):
                        mm = pe.transpose(PS[:, 4 + b, m * D:(m + 1) * D], stg[:, b, m, :], ident[:, :])
                    mm.then_inc(s_turned[b], 1)

                def product(base, it, b, outs):
                    pe.wait_ge(s_tcopy[b], it + (base + 2))
                    pe.wait_ge(s_take[b], it + (base + 1))
                    for to, pairs in outs:
                        for n, (lhs, rhs) in enumerate(pairs):
                            mm = pe.matmul(to, lhs, rhs, start=n == 0, stop=n == len(pairs) - 1)
                    mm.then_inc(s_prod[b], 1)

                pe.wait_ge(s_tabs, 1)
                with pe.Fori(0, IT) as it:
                    for b in range(SL):
                        scatter(9, (s_rows[b], it * (16 * G) + 16 * G), 0, it, b, D)
                pe.wait_ge(s_w, 96)
                with pe.Fori(0, NJ // 2) as it:
                    for b in range(2):
                        turn(0, it, b, 2)
                    for b in range(2):
                        product(0, it, b, [(PS[:, 6 + b, 0:D], [(tT[:, b, 0, :], W0[:, 0, :]), (tT[:, b, 1, :], W0[:, 1, :])])])
                if layers > 1:
                    def to_rows(n, first_bank, tables):
                        pe.wait_ge(s_torow, n + 1)
                        for m, table in enumerate(tables):
                            for k in range(4):
                                mm = pe.transpose(PS[0:QI, first_bank + m, k * P:(k + 1) * P], table[:, k:NI:4], ident[:, :])
                        mm.then_inc(s_inrow, 1)

                    def turn_ends(n):
                        pe.wait_ge(s_ends, n + 1)
                        pe.transpose(PS[0:4, 4, 0:QI], ends[:, :], ident[0:QI, 0:QI]).then_inc(s_endsT, 1)

                    def turn_carries(n, row):
                        pe.wait_ge(s_scan, n + 1)
                        pe.transpose(PS[0:QI, 4, 256:260], row, ident[0:4, 0:4]).then_inc(s_scanT, 1)

                    def to_items(n, tiles):
                        for h in range(H):
                            pe.wait_ge(s_ex, n * H + h + 1)
                            for k in range(4):
                                mm = pe.transpose(PS[:, h, k * QI:(k + 1) * QI], tiles[h][:, k * P:(k + 1) * P], ident[0:QI, 0:QI])
                            mm.then_inc(s_exT, 1)

                    to_rows(0, 0, [ftab[n] for n in ("dst", "ok", "t4")])
                    turn_ends(0)
                    turn_carries(0, before_row[:, 0:QI])
                    turn_ends(1)
                    pe.wait_ge(s_ready, 1)
                    with pe.Fori(0, NJ // 2) as it:
                        for b in range(2):
                            turn(13, it, b)
                        for b in range(2):
                            product(13, it, b, [(PS[:, 6 + b, 0:D + 2 * H], [(tT[:, b, 0, :], WX[:, :])])])
                    with pe.Fori(0, IT) as it:
                        for b in range(SL):
                            pe.wait_ge(s_oh[b], it + (IT + 1))
                            pe.wait_ge(s_ohT[b], it + 1)
                            for k in range(G):
                                mm = pe.transpose(PS[:, b, k * P:(k + 1) * P], oneh[:, b, k, :], ident[:, :])
                            mm.then_inc(s_ohturn[b], 1)
                        for b in range(SL):
                            j = [pe.value_load(itab["j"][0:1, bass.ds(window(b, it) + k, 1)], min_val=0, max_val=NV - 1) for k in range(G)]
                            pe.wait_ge(s_ohT[b], it + 2)
                            pe.wait_ge(s_scored[b], it + 1)
                            for k in range(G):
                                mm = pe.matmul(PS[:, 4 + b, k * H:(k + 1) * H], onehT[:, b, k, :],
                                               ad[:, bass.ds(j[k], 1), :].rearrange("p o h -> p (o h)"), start=True, stop=True)
                            mm.then_inc(s_spread1[b], 1)
                    to_rows(1, 0, [score[:, :, h] for h in range(H)])
                    turn_ends(2)
                    turn_carries(1, before_row[:, 0:QI])
                    turn_ends(3)
                    turn_carries(2, after_row[:, 1:QI + 1])
                    to_items(0, rv)
                    pe.wait_ge(s_max, 1)
                    for h in range(H):
                        for k in range(4):
                            mm = pe.transpose(PS[:, 4 + h, k * QI:(k + 1) * QI], rf[h][:, k * P:(k + 1) * P], ident[0:QI, 0:QI])
                    mm.then_inc(s_maxT, 1)
                    with pe.Fori(0, IT) as it:
                        for b in range(SL):
                            scatter(9 + NI, (s_scaled[b], it + 1), 2 * IT, it, b, W1C + H)
                    pe.wait_ge(s_ready, 2)
                    with pe.Fori(0, NJ // 2) as it:
                        for b in range(2):
                            turn(26, it, b)
                        for b in range(2):
                            pe.wait_ge(s_mid[b], it + 1)
                            product(26, it, b, [(PS[:, 6 + b, a * D:(a + 1) * D], [(w1[:, a * D:(a + 1) * D], tT[:, b, 0, :])]) for a in range(2)])
                        for b in range(2):
                            pe.wait_ge(s_mid[b], it + 2)
                            for a in range(2):
                                mm = pe.matmul(PS[:, 2 + b, 0:D], gelT[:, b, a, :], w2[:, a, :], start=a == 0, stop=a == 1)
                            mm.then_inc(s_prod2[b], 1)

                if layers > 2:
                    pe.wait_ge(s_ready, 3)
                    with pe.Fori(0, NJ // 2) as it:
                        for b in range(2):
                            turn(39, it, b)
                        for b in range(2):
                            product(39, it, b, [(PS[:, 6 + b, :], [(tT[:, b, 0, :], WRs[:, :, :].rearrange("p r d -> p (r d)"))]),
                                                (PS[:, 2 + b, :], [(tT[:, b, 0, :], WRd[:, :, :].rearrange("p r d -> p (r d)"))])])
                    with pe.Fori(0, IT) as it:
                        for b in range(SL):
                            pe.wait_ge(s_oh[b], it + (3 * IT + 1))
                            pe.wait_ge(s_ohT[b], it + (IT + 1))
                            for k in range(G):
                                for r in range(R):
                                    mm = pe.transpose(PS[:, b, :].bitcast(bf16)[:, (k * R + r) * P:(k * R + r + 1) * P],
                                                      oneh4[:, b, k, r * P:(r + 1) * P], ident16[:, :])
                            mm.then_inc(s_ohturn[b], 1)
                        for b in range(SL):
                            j = [pe.value_load(itab["j"][0:1, bass.ds(window(b, it) + k, 1)], min_val=0, max_val=NV - 1) for k in range(G)]
                            pe.wait_ge(s_ohT[b], it + (IT + 2))
                            pe.wait_ge(s_scored[b], it + (IT + 1))
                            for k in range(G):
                                for r in range(R):
                                    mm = pe.matmul(PS[:, 4 + b, k * D:(k + 1) * D], wide4[b][:, k, r * P:(r + 1) * P],
                                                   Btab[:, bass.ds(j[k], 1), r * D:(r + 1) * D].rearrange("p o d -> p (o d)"),
                                                   start=r == 0, stop=r == R - 1)
                            mm.then_inc(s_spread1[b], 1)
                        for b in range(SL):
                            pe.wait_ge(s_relu[b], it + 1)
                            for k in range(G):
                                mm = pe.transpose(PS[:, 4 + b, (G + k) * P:(G + k + 1) * P], ring2[:, b, k, 0:D], ident[:, :])
                            mm.then_inc(s_relT[b], 1)
                        for b in range(SL):
                            pe.wait_ge(s_relTc[b], it + 1)
                            for k in range(G):
                                mm = pe.matmul(PS[:, 4 + b, k * R:(k + 1) * R], onehT[:, b, k, :], u4[:, 0, :], start=True, stop=True)
                            mm.then_inc(s_s4[b], 1)
                    to_rows(2, 0, [score[:, :, r] for r in range(R)])
                    turn_ends(4)
                    turn_carries(3, before_row[:, 0:QI])
                    turn_ends(5)
                    turn_carries(4, after_row[:, 1:QI + 1])
                    pe.wait_ge(s_max, 2)
                    for k in range(4):
                        mm = pe.transpose(PS[:, 0, k * QI:(k + 1) * QI], rv[0][:, k * P:(k + 1) * P], ident[0:QI, 0:QI])
                    mm.then_inc(s_maxT, 1)
                    with pe.Fori(0, IT) as it:
                        for b in range(SL):
                            pe.wait_ge(s_back[b], it * 16 + (IT + 1) * 16)
                            pe.wait_ge(s_oh[b], it + (4 * IT + 1))
                            pe.wait_ge(s_acc, it * (SL * G) + (9 + 2 * NI + b * G - G))
                            for k in range(G):
                                for r in range(R):
                                    mm = pe.matmul(PS[:, 4 * (b % 2) + 2 * k + r // 2, (r % 2) * 256:(r % 2) * 256 + D + 1],
                                                   wide4[b][:, k, r * P:(r + 1) * P], ring2[:, b, k, :], start=True, stop=True)
                            mm.then_inc(s_scat[b], 1)
                    with pe.Fori(0, NJ // 2) as it:
                        for b in range(2):
                            pe.wait_ge(s_staged[b], it + 54)
                            pe.wait_ge(s_tcopy[b], it + 53)
                            for r in range(R):
                                pe.transpose(PS[:, 4 + b, r * D:(r + 1) * D], stg[:, b, r, :], ident[:, :])
                            pe.transpose(PS[0:R, 2 + b, 0:D], stg[:, b, R, 0:R], ident[:, :]).then_inc(s_turned[b], 1)
                        for b in range(2):
                            product(52, it, b, [(PS[:, 6 + b, 0:D], [(tT[:, b, r, :], WV[:, r, :]) for r in range(R)] + [(tT[0:R, b, R, :], bV[:, :])])])
                if layers > 3:
                    pe.wait_ge(s_w3, 7 * 16)
                    pe.wait_ge(s_acc, 9 + 3 * NI)
                    for n in range(2):
                        for a in range(3):
                            mm = pe.transpose(PS[:, n, a * D:(a + 1) * D], gru_rows[:, 3 * n + a, :], ident[:, :])
                    mm.then_inc(s_gruT, 1)
                    pe.wait_ge(s_ready, 4)
                    with pe.Fori(0, NJ // 2) as it:
                        for b in range(2):
                            turn(65, it, b)
                        for b in range(2):
                            product(65, it, b, [(PS[:, (6, 2)[a] + b, :], [(tT[:, b, 0, :], W3[:, 4 * a:4 * a + 4, :].rearrange("p r d -> p (r d)"))]) for a in range(2)])
                    with pe.Fori(0, IT) as it:
                        for b in range(SL):
                            scatter(9 + 3 * NI, (s_rows[b], it * (16 * G) + (3 * IT + 1) * 16 * G), 5 * IT, it, b, D)
                    pe.wait_ge(s_ready, 5)
                    with pe.Fori(0, NJ // 2) as it:
                        for b in range(2):
                            turn(78, it, b, 2)
                        for b in range(2):
                            hT, mT = tT[:, b, 0, :], tT[:, b, 1, :]
                            product(78, it, b, [(PS[:, 6 + b, 0:2 * D], [(mT, gruT[:, 0, 0:2 * D]), (hT, gruT[:, 1, 0:2 * D])]),
                                                (PS[:, 6 + b, 2 * D:3 * D], [(mT, gruT[:, 0, 2 * D:3 * D])]),
                                                (PS[:, 6 + b, 3 * D:4 * D], [(hT, gruT[:, 1, 2 * D:3 * D])])])

            @block.vector
            def _(dve):
                ch = Chain(dve, s_chain)
                for name, value in (("src", 0), ("dst", 1000000), ("t4", 0), ("t8", 0)):
                    dve.memset(ints[name][96:Q, :], value)
                dve.memset(X[:, NV - 1:NJ, :], 0.0)
                dve.memset(rows["w"][96:Q, :], 0.0).then_inc(s_pad, 1)
                for b in range(2):
                    dve.sem_inc(s_staged[b], 1)
                    dve.sem_inc(s_take[b], 1)
                    dve.sem_inc(s_tcopy[b], 1)
                    dve.sem_inc(s_mid[b], 1)
                    dve.sem_inc(s_tfree[b], 1)
                for b in range(SL):
                    dve.sem_inc(s_ohT[b], 1)
                    dve.sem_inc(s_scored[b], 1)
                    dve.sem_inc(s_added[b], 1)
                    dve.sem_inc(s_spfree[b], 1)
                dve.wait_ge(s_const2, 1)
                dve.wait_ge(s_in, 160)
                for name in ("src", "dst", "t4", "t8"):
                    dve.tensor_copy(rows[name][0:Q, :], ints[name][0:Q, :])
                dve.tensor_single_scalar(tile_i[:, 0:4], ints["dst"][0:Q, 0:512:P], 7, ALU.arith_shift_right)
                ch.link(dve.tensor_single_scalar(tile_i[:, 4:8], ints["dst"][0:Q, P - 1:512:P], 7, ALU.arith_shift_right))
                first, last, cnt, ones, incl, off, end, delta = (tile_f[:, n, :] for n in range(8))
                dve.tensor_copy(first, tile_i[:, 0:4])
                dve.memset(ones, 1.0)
                ch.link(dve.tensor_single_scalar(last, tile_i[:, 4:8], float(NV - 1), ALU.min))
                ch.link(dve.scalar_tensor_tensor(cnt, last, 1.0, first, ALU.add, ALU.subtract))
                dve.tensor_tensor_scan(incl, ones, cnt, 0.0, ALU.mult, ALU.add).then_inc(s_first, 1)
                dve.wait_ge(s_first, 1)
                ch.link(dve.tensor_tensor(off, incl, cnt, ALU.subtract))
                dve.wait_ge(s_pre, 1)
                ch.link(dve.tensor_scalar(off, off, PS[0:Q, 6, 0:1], None, ALU.add))
                dve.tensor_tensor(end, off, cnt, ALU.add)
                ch.link(dve.tensor_tensor(delta, first, off, ALU.subtract))
                for k in range(4):
                    dve.tensor_scalar(spread[:, k, :], iota[0:Q, 0:NI], off[:, k:k + 1], None, ALU.is_ge)
                ch.link(dve.tensor_copy(rows["j"][0:Q, :].rearrange("q (k e) -> q k e", e=P),
                                        delta.unsqueeze(2).to_broadcast([Q, 4, P])))
                for k in range(4):
                    ins = dve.scalar_tensor_tensor(spread[:, k, :], iota[0:Q, 0:NI], end[:, k:k + 1], spread[:, k, :],
                                                   ALU.is_lt, ALU.mult)
                ins.then_inc(s_spread, 1)
                dve.wait_ge(s_items, 1)
                src, dst, t4, t8, w, dj = (PS[:, n, 0:NI] for n in range(6))
                F = ftab
                dve.tensor_copy(F["w"], w)
                dve.tensor_copy(F["t4"], t4)
                dve.tensor_copy(itab["src"][:, :], src)
                dve.tensor_copy(score[:, :, 0], src)
                ch.link(dve.tensor_tensor(F["jf"], iota[:, 0:NI], dj, ALU.add))
                dve.tensor_single_scalar(itab["j"][:, :], F["jf"], float(NV - 1), ALU.min)
                dve.scalar_tensor_tensor(itab["src8"][:, :], score[:, :, 0], float(T8), t8, ALU.mult, ALU.add)
                dve.scalar_tensor_tensor(itab["src4"][:, :], score[:, :, 0], float(R), F["t4"], ALU.mult, ALU.add)
                ch.link(dve.scalar_tensor_tensor(F["rel"], F["jf"], -float(P), dst, ALU.mult, ALU.add))
                ch.link(dve.tensor_single_scalar(F["ok"], F["rel"], 0.0, ALU.is_ge))
                ch.link(dve.scalar_tensor_tensor(F["ok"], F["rel"], float(P), F["ok"], ALU.is_lt, ALU.mult))
                ch.link(dve.scalar_tensor_tensor(F["rel"], F["rel"], FAR, F["ok"], ALU.add, ALU.mult))
                ch.link(dve.tensor_single_scalar(F["rel"], F["rel"], -FAR, ALU.add))
                dve.scalar_tensor_tensor(F["key4"], F["t4"], float(P), F["rel"], ALU.mult, ALU.add)
                ch.link(dve.scalar_tensor_tensor(F["dst"], dst, 1.0, F["ok"], ALU.add, ALU.mult))
                dve.sem_inc(s_acc, 8)
                ch.link(dve.memset(acc[:, :, :], 0.0))
                dve.tensor_single_scalar(F["dst"], F["dst"], -1.0, ALU.add).then_inc(s_tabs, 1)
                dve.wait_ge(s_tabs, 1)
                dve.memset(col[0][:, :], 0.0).then_inc(s_acc, 1)

                def add_sums(first, turns0, it, b, width, target):
                    dve.wait_ge(s_scat[b], it + (turns0 + 2))
                    for k in range(G):
                        j = dve.value_load(itab["j"][0:1, bass.ds(window(b, it) + k, 1)], min_val=0, max_val=NV - 1)
                        a = target[:, bass.ds(j, 1), :].rearrange("p o d -> p (o d)")
                        dve.wait_ge(s_acc, it * (SL * G) + (first + b * G + k))
                        dve.tensor_tensor(a, a, PS[:, b, k * 256:k * 256 + width], ALU.add).then_inc(s_acc, 1)

                def layer_norm(n, source, target):
                    with dve.Fori(0, NJ) as j:
                        dve.bn_stats(stats[:, bass.ds(j, 1), :].rearrange("p o d -> p (o d)"),
                                     source[:, bass.ds(j, 1), :].rearrange("p o d -> p (o d)"))
                    ch.link(dve.memset(col[5][:, :], 0.0))
                    me, ve, mo, vo = (stats[:, :, m] for m in (1, 2, 4, 5))
                    dve.tensor_tensor(col[2][:, :], me, mo, ALU.add)
                    dve.tensor_tensor(col[3][:, :], me, mo, ALU.subtract)
                    ch.link(dve.tensor_tensor(col[0][:, :], ve, vo, ALU.add))
                    ch.link(dve.tensor_tensor(col[3][:, :], col[3][:, :], col[3][:, :], ALU.mult))
                    dve.tensor_single_scalar(col[2][:, :], col[2][:, :], 0.5, ALU.mult)
                    ch.link(dve.tensor_scalar(col[3][:, :], col[3][:, :], 0.25, 1e-5, ALU.mult, ALU.add))
                    dve.scalar_tensor_tensor(col[0][:, :], col[0][:, :], 1.0 / D, col[3][:, :], ALU.mult, ALU.add).then_inc(s_var, 1)
                    ch.link(dve.tensor_tensor(target, source, col[2][:, :].unsqueeze(2).to_broadcast([P, NJ, D]), ALU.subtract))
                    dve.wait_ge(s_std, n + 1)
                    ch.link(dve.reciprocal(col[1][:, :], col[1][:, :]))
                    ch.link(dve.tensor_tensor(target, target, col[1][:, :].unsqueeze(2).to_broadcast([P, NJ, D]), ALU.mult))

                def build_onehot(free, it, b, weighted):
                    dve.wait_ge(*free)
                    for k in range(G):
                        i = window(b, it) + k
                        if weighted:
                            ins = dve.tensor_scalar(oneh[:, b, k, :], iota[:, 0:P], ftab["rel"][:, bass.ds(i, 1)],
                                                    ftab["w"][:, bass.ds(i, 1)], ALU.is_equal, ALU.mult)
                        else:
                            ins = dve.tensor_scalar(oneh[:, b, k, :], iota[:, 0:P], ftab["rel"][:, bass.ds(i, 1)],
                                                    None, ALU.is_equal)
                    ins.then_inc(s_oh[b], 1)

                with dve.Fori(0, IT) as it:
                    for b in range(SL):
                        build_onehot((s_scat[b], it + 1), it, b, True)
                    for b in range(SL):
                        add_sums(9, 0, it, b, D, acc0)
                dve.wait_ge(s_acc, 9 + NI)
                dve.wait_ge(s_w, 96)
                ch.link(dve.tensor_tensor(bias0[:, 0, :], bias0[:, 0, :], bias0[:, 1, :], ALU.add))

                with dve.Fori(0, NJ // 2) as it:
                    ch.begin(it, 2)
                    for b in range(2):
                        j = it * 2 + b
                        xj = X[:, bass.ds(j, 1), :].rearrange("p o d -> p (o d)")
                        lj = acc0[:, bass.ds(j, 1), :].rearrange("p o d -> p (o d)")
                        dve.wait_ge(s_turned[b], it + 1)
                        dve.tensor_tensor(stg[:, b, 0, :], xj, lj, ALU.add)
                        dve.tensor_tensor(stg[:, b, 1, :], xj, lj, ALU.mult).then_inc(s_staged[b], 1)
                    for b in range(2):
                        j = it * 2 + b
                        yj = Y[:, bass.ds(j, 1), :].rearrange("p o d -> p (o d)")
                        dve.wait_ge(s_prod[b], it + 2)
                        ch.link(dve.tensor_tensor(yj, PS[:, 6 + b, 0:D], bias0[:, 0, :], ALU.add))
                        dve.scalar_tensor_tensor(yj, yj, 0.2, yj, ALU.mult, ALU.max).then_inc(s_take[b], 1)
                    ch.end(NJ // 2)
                dve.wait_ge(s_take[0], 1 + NJ // 2)
                dve.wait_ge(s_take[1], 1 + NJ // 2)
                dve.sem_inc(s_sq, 1)
                dve.wait_ge(s_sqd, 1)
                ch.link(dve.tensor_reduce(col[0][:, :], big, AX.X, ALU.add))
                dve.tensor_single_scalar(col[0][:, :], col[0][:, :], 1e-24, ALU.max).then_inc(s_var, 1)
                dve.wait_ge(s_std, 1)
                ch.link(dve.reciprocal(col[1][:, :], col[1][:, :]))
                ch.link(dve.tensor_tensor(Y[:, :, :], Y[:, :, :], col[1][:, :].unsqueeze(2).to_broadcast([P, NJ, D]), ALU.mult))
                ch.link(dve.tensor_tensor(Y[:, :, :], Y[:, :, :], X[:, :, :], ALU.add))
                layer_norm(1, Y[:, :, :], X[:, :, :])
                if layers > 1:
                    everyone = lambda v: v.unsqueeze(1).to_broadcast([P, NJ, D])
                    dve.wait_ge(s_w1, 12 * 16)

                    def scale_shift(target, gain, shift):
                        ch.link(dve.tensor_tensor(target, target, everyone(gain), ALU.mult))
                        ch.link(dve.tensor_tensor(target, target, everyone(shift), ALU.add))

                    for n in range(2):
                        dve.tensor_tensor(scaled_w[:, n, :], WX[:, 0:D], att[:, n, :], ALU.mult)
                    ch.link(dve.memset(before_row[:, :], -BIG))
                    for n in range(2):
                        dve.tensor_reduce(WX[:, D + n * H:D + (n + 1) * H], scaled_w[:, n, :].rearrange("p (h c) -> p h c", c=C), AX.X, ALU.add)
                    ch.link(dve.memset(after_row[:, :], -BIG))
                    dve.sem_inc(s_torow, 1)
                    dve.wait_ge(s_inrow, 1)
                    dve.tensor_copy(rt4, PS[0:QI, 2, :])
                    dve.tensor_copy(rok, PS[0:QI, 1, :])
                    dve.tensor_scalar(rneg, PS[0:QI, 1, :], BIG, -BIG, ALU.mult, ALU.add)
                    ch.link(dve.tensor_copy(rdst, PS[0:QI, 0, :]))
                    ch.link(dve.memset(ends[:, :], 0.0))
                    dve.tensor_reduce(ends[:, 0:1], rdst, AX.X, ALU.max).then_inc(s_ends, 1)
                    dve.wait_ge(s_endsT, 1)
                    ch.link(dve.tensor_copy(resets_row[:, :], PS[0:4, 4, 0:QI]))
                    dve.tensor_tensor_scan(before_row[:, 1:QI + 1], resets_row[:, :], resets_row[:, :], -1.0, ALU.max, ALU.max).then_inc(s_scan, 1)
                    dve.wait_ge(s_scanT, 1)
                    ch.link(dve.tensor_single_scalar(rkey[:, 0:1], PS[0:QI, 4, 256:257], -1.0, ALU.max))
                    ch.link(dve.tensor_tensor_scan(rkey[:, 1:513], rdst, rdst, rkey[:, 0:1], ALU.max, ALU.max))
                    ch.link(dve.tensor_tensor(reset[:, 0:512], rdst, rkey[:, 0:512], ALU.is_gt))
                    dve.memset(reset[:, 512:513], 0.0)
                    ch.link(dve.tensor_single_scalar(reset[:, 0:512], reset[:, 0:512], -BIG, ALU.mult))
                    for n in range(4):
                        ins = dve.tensor_reduce(ends[:, n:n + 1], reset[:, 0:512], AX.X, ALU.add)
                    ins.then_inc(s_ends, 1)
                    dve.wait_ge(s_endsT, 2)
                    ch.link(dve.tensor_copy(resets_row[:, :], PS[0:4, 4, 0:QI]))

                    def segment_max(n, values):
                        for h in range(H):
                            ch.link(dve.tensor_tensor_scan(rscr, reset[:, 0:512], values[h], -BIG, ALU.add, ALU.max))
                            ch.link(dve.tensor_copy(ends[:, h:h + 1], rscr[:, 511:512]))
                        dve.sem_inc(s_ends, 1)
                        dve.wait_ge(s_endsT, 2 * n + 3)
                        dve.tensor_tensor_scan(before_row[:, 1:QI + 1], resets_row[:, :], PS[0:4, 4, 0:QI], -BIG, ALU.add, ALU.max).then_inc(s_scan, 1)
                        dve.wait_ge(s_scanT, 2 * n + 2)
                        ch.link(dve.tensor_copy(carry[:, :], PS[0:QI, 4, 256:260]))
                        for h in range(H):
                            ch.link(dve.tensor_tensor_scan(rf[h], reset[:, 0:512], values[h], carry[:, h:h + 1], ALU.add, ALU.max))
                        for h in range(H):
                            ch.link(dve.tensor_tensor_scan(rscr[:, ::-1], reset[:, 1:513][:, ::-1], rf[h][:, ::-1], -BIG, ALU.add, ALU.max))
                            ch.link(dve.tensor_tensor(ends[:, h:h + 1], rscr[:, 0:1], reset[:, 0:1], ALU.add))
                        dve.sem_inc(s_ends, 1)
                        dve.wait_ge(s_endsT, 2 * n + 4)
                        dve.tensor_tensor_scan(after_row[:, 0:QI][:, ::-1], resets_row[:, ::-1], PS[0:4, 4, 0:QI][:, ::-1], -BIG, ALU.add, ALU.max).then_inc(s_scan, 1)
                        dve.wait_ge(s_scanT, 2 * n + 3)
                        ch.link(dve.tensor_copy(carry[:, :], PS[0:QI, 4, 256:260]))
                        for h in range(H):
                            ch.link(dve.tensor_tensor_scan(rg[:, ::-1], reset[:, 1:513][:, ::-1], rf[h][:, ::-1], carry[:, h:h + 1], ALU.add, ALU.max))
                            dve.scalar_tensor_tensor(values[h], rg, -0.1 * BIG, values[h], ALU.max, ALU.subtract).then_inc(s_exin, 1)
                            dve.wait_ge(s_exin, n * H + h + 1)
                            if n == 0:
                                ch.link(dve.scalar_tensor_tensor(rf[h], reset[:, 0:512], 0.0, rg, ALU.is_lt, ALU.mult))

                    layer_norm(2, X[:, :, :], Y[:, :, :])
                    scale_shift(Y[:, :, :], rowv["ln1_g"][:, :], rowv["ln1_b"])
                    dve.sem_inc(s_ready, 1)
                    with dve.Fori(0, NJ // 2) as it:
                        for b in range(2):
                            dve.wait_ge(s_prod[b], it + 15)
                            dve.tensor_copy(ad[:, bass.ds(it * 2 + b, 1), :].rearrange("p o h -> p (o h)"), PS[:, 6 + b, W1C:W1C + H])
                            dve.tensor_copy(xh[:, bass.ds(it * 2 + b, 1), :].rearrange("p o d -> p (o d)"), PS[:, 6 + b, 0:W1C]).then_inc(s_take[b], 1)
                    with dve.Fori(0, IT) as it:
                        for b in range(SL):
                            build_onehot((s_ohturn[b], it + 1), it, b, False)
                        for b in range(SL):
                            dve.wait_ge(s_spread1[b], it + 2)
                            dve.wait_ge(s_rows[b], it * (16 * G) + (IT + 1) * 16 * G)
                            dve.tensor_tensor(score[:, bass.ds(window(b, it), G), :],
                                              PS[:, 4 + b, 0:G * H].rearrange("p (g h) -> p g h", g=G),
                                              ring[:, b, :, D:W1C], ALU.add).then_inc(s_scored[b], 1)
                    dve.wait_ge(s_scored[0], 1 + IT)
                    dve.wait_ge(s_scored[1], 1 + IT)
                    dve.wait_ge(s_scored[2], 1 + IT)
                    dve.wait_ge(s_scored[3], 1 + IT)
                    dve.memset(acc1, 0.0)
                    dve.scalar_tensor_tensor(score[:, :, :], score[:, :, :], 0.2, score[:, :, :], ALU.mult, ALU.max).then_inc(s_torow, 1)
                    dve.wait_ge(s_inrow, 2)
                    for h in range(H):
                        ins = dve.tensor_tensor(rv[h][:, :], PS[0:QI, h, :], rneg, ALU.add)
                    ch.link(ins)
                    segment_max(0, [v[:, :] for v in rv])
                    dve.sem_inc(s_max, 1)
                    dve.wait_ge(s_maxT, 1)
                    for h in range(H):
                        ins = dve.tensor_copy(score[:, :, h].rearrange("p (q k) -> p k q", k=4),
                                              PS[:, 4 + h, 0:NI].rearrange("p (k q) -> p k q", k=4))
                    for h in range(H):
                        dve.wait_ge(s_exT, h + 1)
                        ins = dve.tensor_copy(weight[:, :, h].rearrange("p (q k) -> p k q", k=4),
                                              PS[:, h, 0:NI].rearrange("p (k q) -> p k q", k=4))
                    ch.link(ins)
                    with dve.Fori(0, IT) as it:
                        for b in range(SL):
                            build_onehot((s_scat[b], it + (IT + 1)), it, b, False)
                            dve.wait_ge(s_back[b], it * 16 + 16)
                            feats = ring[:, b, :, 0:D].rearrange("p g (h c) -> p g h c", c=C)
                            wb = weight[:, bass.ds(window(b, it), G), :]
                            for k in range(G):
                                wk = weight[:, bass.ds(window(b, it) + k, 1), :].rearrange("p o h -> p (o h)")
                                fk = ring[:, b, k, 0:D].rearrange("p (h c) -> p h c", c=C)
                                dve.tensor_tensor(fk, fk, wk.unsqueeze(2).to_broadcast([P, H, C]), ALU.mult)
                            dve.tensor_copy(ring[:, b, :, D:W1C], wb)
                            dve.tensor_copy(ring[:, b, :, W1C:W1C + H], score[:, bass.ds(window(b, it), G), :]).then_inc(s_scaled[b], 1)
                        for b in range(SL):
                            add_sums(9 + NI, IT, it, b, W1C + H, acc1)
                    dve.wait_ge(s_acc, 9 + 2 * NI)
                    sums, peak = acc1[:, :, D:W1C], acc1[:, :, W1C:W1C + H]
                    edge_exp, own_exp, top = (own[:, n, :, :] for n in range(3))
                    ch.link(dve.tensor_tensor(own_exp, xh[:, :, D:W1C], ad[:, :, :], ALU.add))
                    ch.link(dve.scalar_tensor_tensor(own_exp, own_exp, 0.2, own_exp, ALU.mult, ALU.max))
                    ch.link(dve.tensor_scalar(edge_exp, sums, 0.5, -BIG, ALU.is_lt, ALU.mult))
                    ch.link(dve.tensor_tensor(edge_exp, edge_exp, peak, ALU.add))
                    ch.link(dve.tensor_tensor(top, edge_exp, own_exp, ALU.max))
                    dve.tensor_tensor(edge_exp, top, edge_exp, ALU.subtract)
                    dve.tensor_tensor(own_exp, top, own_exp, ALU.subtract).then_inc(s_own, 1)
                    dve.wait_ge(s_ownx, 1)
                    ch.link(dve.tensor_tensor(top, sums, edge_exp, ALU.mult))
                    ch.link(dve.tensor_tensor(top, top, own_exp, ALU.add))
                    ch.link(dve.reciprocal(top, top))
                    dve.tensor_tensor(edge_exp, edge_exp, top, ALU.mult)
                    ch.link(dve.tensor_tensor(own_exp, own_exp, top, ALU.mult))
                    for h in range(H):
                        part = slice(h * C, (h + 1) * C)
                        dve.tensor_tensor(Y[:, :, part], acc1[:, :, part], edge_exp[:, :, h:h + 1].to_broadcast([P, NJ, C]), ALU.mult)
                        ins = dve.tensor_tensor(xh[:, :, part], xh[:, :, part], own_exp[:, :, h:h + 1].to_broadcast([P, NJ, C]), ALU.mult)
                    ch.link(ins)
                    ch.link(dve.tensor_tensor(Y[:, :, :], Y[:, :, :], xh[:, :, 0:D], ALU.add))
                    ch.link(dve.tensor_tensor(Y[:, :, :], Y[:, :, :], everyone(rowv["gat_b"]), ALU.add))
                    ch.link(dve.tensor_tensor(Y[:, :, :], Y[:, :, :], X[:, :, :], ALU.add))
                    layer_norm(3, Y[:, :, :], big)
                    scale_shift(big, rowv["ln2_g"][:, :], rowv["ln2_b"])
                    dve.sem_inc(s_ready, 1)
                    with dve.Fori(0, NJ // 2) as it:
                        for b in range(2):
                            yj = Y[:, bass.ds(it * 2 + b, 1), :].rearrange("p o d -> p (o d)")
                            dve.wait_ge(s_prod2[b], it + 2)
                            dve.tensor_tensor(yj, yj, PS[:, 2 + b, 0:D], ALU.add).then_inc(s_take[b], 1)
                    dve.wait_ge(s_take[0], 1 + 3 * (NJ // 2))
                    dve.wait_ge(s_take[1], 1 + 3 * (NJ // 2))
                    ch.link(dve.tensor_tensor(Y[:, :, :], Y[:, :, :], everyone(rowv["b2"]), ALU.add))
                    ch.link(dve.tensor_tensor(Y[:, :, :], Y[:, :, :], X[:, :, :], ALU.add))
                    layer_norm(4, Y[:, :, :], X[:, :, :])
                if layers > 2:
                    dve.wait_ge(s_w2, 12 * 16)
                    for n in range(2):
                        for r in range(R):
                            ch.link(dve.tensor_tensor(scaled_w[:, 0, :], trow[:, 0, (n * R + r) * D:(n * R + r + 1) * D], attq[:, n, :], ALU.mult))
                            dve.tensor_tensor(c4q[:, n, r * D:(r + 1) * D], c4q[:, n, r * D:(r + 1) * D], attq[:, n, :], ALU.mult)
                            ch.link(dve.tensor_reduce(u4[:, n, r:r + 1], scaled_w[:, 0, :], AX.X, ALU.add))
                        ch.link(dve.tensor_reduce(c4[:, n, :], c4q[:, n, :].rearrange("p (r d) -> p r d", d=D), AX.X, ALU.add))
                    dve.tensor_tensor(u4[:, 0, :], u4[:, 0, :], u4[:, 1, :], ALU.add)
                    ch.link(dve.tensor_tensor(c4[:, 0, :], c4[:, 0, :], c4[:, 1, :], ALU.add))
                    dve.memset(ring2[:, :, :, D:D + 1], 1.0)
                    ch.link(dve.tensor_scalar(c4[:, 0, :], c4[:, 0, :], a_b[:, 0:1], None, ALU.add))
                    dve.sem_inc(s_ready, 1)
                    with dve.Fori(0, NJ // 2) as it:
                        for b in range(2):
                            dve.wait_ge(s_prod[b], it + 41)
                            dve.wait_ge(s_tfree[b], it + (NJ // 2 + 1))
                            dve.tensor_copy(trow[:, b, 0:R * D], PS[:, 6 + b, :])
                            dve.tensor_tensor(Btab[:, bass.ds(it * 2 + b, 1), :].rearrange("p o d -> p (o d)"), PS[:, 2 + b, :], bR[:, :], ALU.add).then_inc(s_take[b], 1)
                    with dve.Fori(0, IT) as it:
                        for b in range(SL):
                            dve.wait_ge(s_ohturn[b], it + (IT + 1))
                            for k in range(G):
                                ins = dve.tensor_scalar(oneh4[:, b, k, :], iota16[:, :], ftab["key4"][:, bass.ds(window(b, it) + k, 1)], None, ALU.is_equal)
                            ins.then_inc(s_oh[b], 1)
                        for b in range(SL):
                            dve.wait_ge(s_spread1[b], it + (IT + 2))
                            dve.wait_ge(s_rows[b], it * (16 * G) + (2 * IT + 1) * 16 * G)
                            dve.wait_ge(s_spfree[b], it + (IT + 1))
                            dve.tensor_tensor(ring2[:, b, :, 0:D], PS[:, 4 + b, 0:G * D].rearrange("p (g d) -> p g d", g=G),
                                              ring[:, b, :, 0:D], ALU.add).then_inc(s_added[b], 1)
                        for b in range(SL):
                            dve.wait_ge(s_added[b], it + 2)
                            dve.scalar_tensor_tensor(ring2[:, b, :, 0:D], ring2[:, b, :, 0:D], 0.2, ring2[:, b, :, 0:D],
                                                     ALU.mult, ALU.max).then_inc(s_relu[b], 1)
                        for b in range(SL):
                            dve.wait_ge(s_s4[b], it + 1)
                            dve.tensor_copy(score[:, bass.ds(window(b, it), G), :],
                                            PS[:, 4 + b, 0:G * R].rearrange("p (g r) -> p g r", g=G)).then_inc(s_scored[b], 1)
                    for b in range(SL):
                        dve.wait_ge(s_scored[b], 1 + 2 * IT)
                    dve.memset(wide[:, :, :], 0.0)
                    ch.link(dve.tensor_tensor(score[:, :, :], score[:, :, :], c4[:, 0, :].unsqueeze(1).to_broadcast([P, NI, R]), ALU.add))
                    dve.scalar_tensor_tensor(score[:, :, :], score[:, :, :], 0.2, score[:, :, :], ALU.mult, ALU.max).then_inc(s_torow, 1)
                    dve.wait_ge(s_inrow, 3)
                    for r in range(R):
                        ch.link(dve.scalar_tensor_tensor(rscr, rt4, float(r), rok, ALU.is_equal, ALU.mult))
                        ch.link(dve.tensor_scalar(rscr, rscr, BIG, -BIG, ALU.mult, ALU.add))
                        ch.link(dve.tensor_tensor(rv[r][:, :], PS[0:QI, r, :], rscr, ALU.add))
                    segment_max(1, [v[:, :] for v in rv])
                    dve.wait_ge(s_ex, 2 * H)
                    dve.tensor_tensor(rv[2][:, :], rv[2][:, :], rv[3][:, :], ALU.add)
                    ch.link(dve.tensor_tensor(rv[0][:, :], rv[0][:, :], rv[1][:, :], ALU.add))
                    dve.tensor_tensor(rv[0][:, :], rv[0][:, :], rv[2][:, :], ALU.add).then_inc(s_max, 1)
                    dve.wait_ge(s_maxT, 2)
                    ch.link(dve.tensor_copy(ftab["w"].rearrange("p (q k) -> p k q", k=4),
                                            PS[:, 0, 0:NI].rearrange("p (k q) -> p k q", k=4)))
                    with dve.Fori(0, IT) as it:
                        for b in range(SL):
                            dve.wait_ge(s_scat[b], it + (2 * IT + 1))
                            for k in range(G):
                                i = window(b, it) + k
                                ins = dve.tensor_scalar(wide4[b][:, k, :], iota[:, :], ftab["key4"][:, bass.ds(i, 1)],
                                                        ftab["w"][:, bass.ds(i, 1)], ALU.is_equal, ALU.mult)
                            ins.then_inc(s_oh[b], 1)
                        for b in range(SL):
                            dve.wait_ge(s_scat[b], it + (2 * IT + 2))
                            for k in range(G):
                                j = dve.value_load(itab["j"][0:1, bass.ds(window(b, it) + k, 1)], min_val=0, max_val=NV - 1)
                                a = wide[:, bass.ds(j, 1), :].rearrange("p o (r f) -> p (o r) f", r=R)
                                q = 4 * (b % 2) + 2 * k
                                dve.wait_ge(s_acc, it * (SL * G) + (9 + 2 * NI + b * G + k))
                                dve.tensor_tensor(a, a, PS[:, q:q + 2, :].rearrange("p q (r f) -> p (q r) f", f=256)[:, :, 0:D + 1], ALU.add).then_inc(s_acc, 1)
                    dve.wait_ge(s_acc, 9 + 3 * NI)
                    sums = wide[:, :, :].rearrange("p j (r f) -> p j r f", r=R)[:, :, :, D]
                    rden, flag = own[:, 0, :, :], own[:, 1, :, :]
                    ch.link(dve.tensor_single_scalar(rden, sums, 1e-16, ALU.max))
                    ch.link(dve.reciprocal(rden, rden))
                    ch.link(dve.tensor_tensor(flag, rden, sums, ALU.mult))
                    with dve.Fori(0, NJ // 2) as it:
                        for b in range(2):
                            j = it * 2 + b
                            dve.wait_ge(s_turned[b], it + 53)
                            dve.tensor_copy(stg[:, b, R, 0:R], own[:, 1, bass.ds(j, 1), :].rearrange("p o r -> p (o r)"))
                            dve.tensor_tensor(stg[:, b, 0:R, :], wide[:, bass.ds(j, 1), :].rearrange("p o (r f) -> p (o r) f", r=R)[:, :, 0:D],
                                              own[:, 0, bass.ds(j, 1), :].rearrange("p o r -> p (o r)").unsqueeze(2).to_broadcast([P, R, D]), ALU.mult).then_inc(s_staged[b], 1)
                        for b in range(2):
                            dve.wait_ge(s_prod[b], it + 54)
                            dve.tensor_copy(Y[:, bass.ds(it * 2 + b, 1), :].rearrange("p o d -> p (o d)"), PS[:, 6 + b, 0:D]).then_inc(s_take[b], 1)
                    for b in range(2):
                        dve.wait_ge(s_take[b], 66)
                    dve.tensor_single_scalar(big, Y[:, :, :], 0.0, ALU.min).then_inc(s_elu, 1)
                    ch.link(dve.scalar_tensor_tensor(Y[:, :, :], Y[:, :, :], 0.0, X[:, :, :], ALU.max, ALU.add))
                    dve.wait_ge(s_elud, 1)
                    ch.link(dve.scalar_tensor_tensor(Y[:, :, :], big, -1.0, Y[:, :, :], ALU.add, ALU.add))
                    layer_norm(5, Y[:, :, :], X[:, :, :])
                if layers > 3:
                    dve.memset(acc0, 0.0)
                    dve.wait_ge(s_w3, 7 * 16)
                    ch.link(dve.tensor_tensor(gru_b[:, 0:2 * D], gru_b[:, 0:2 * D], gru_b2[:, :], ALU.add))
                    dve.sem_inc(s_ready, 1)
                    with dve.Fori(0, NJ // 2) as it:
                        for b in range(2):
                            dve.wait_ge(s_prod[b], it + 67)
                            dve.wait_ge(s_tfree[b], it + (NJ + 1))
                            dve.tensor_tensor(trow[:, b, 0:4 * D], PS[:, 6 + b, :], b3[:, 0:4 * D], ALU.add)
                            dve.tensor_tensor(trow[:, b, 4 * D:8 * D], PS[:, 2 + b, :], b3[:, 4 * D:8 * D], ALU.add).then_inc(s_take[b], 1)
                    with dve.Fori(0, IT) as it:
                        for b in range(SL):
                            build_onehot((s_scat[b], it + (3 * IT + 1)), it, b, False)
                        for b in range(SL):
                            add_sums(9 + 3 * NI, 3 * IT, it, b, D, acc0)
                    dve.wait_ge(s_acc, 9 + 4 * NI)
                    dve.sem_inc(s_ready, 1)
                    with dve.Fori(0, NJ // 2) as it:
                        for b in range(2):
                            dve.wait_ge(s_prod[b], it + 80)
                            dve.tensor_tensor(wide[:, bass.ds(it * 2 + b, 1), 0:4 * D].rearrange("p o d -> p (o d)"), PS[:, 6 + b, :], gru_b[:, :], ALU.add).then_inc(s_take[b], 1)
                    for b in range(2):
                        dve.wait_ge(s_take[b], 92)
                    dve.sem_inc(s_gate, 1)
                    dve.wait_ge(s_gated, 1)
                    rg3, z, n_in, h_n = (wide[:, :, a * D:(a + 1) * D] for a in range(4))
                    ch.link(dve.tensor_tensor(h_n, h_n, rg3, ALU.mult))
                    dve.tensor_tensor(n_in, n_in, h_n, ALU.add).then_inc(s_gate, 1)
                    dve.wait_ge(s_gated, 2)
                    ch.link(dve.tensor_tensor(Y[:, :, :], X[:, :, :], n_in, ALU.subtract))
                    ch.link(dve.tensor_tensor(Y[:, :, :], Y[:, :, :], z, ALU.mult))
                    ch.link(dve.tensor_tensor(Y[:, :, :], Y[:, :, :], n_in, ALU.add))
                    ch.link(dve.tensor_tensor(Y[:, :, :], Y[:, :, :], X[:, :, :], ALU.add))
                    layer_norm(6, Y[:, :, :], X[:, :, :])
                dve.sem_inc(s_final, 1)


_OUTS = [((3125, 128), "float32")]


def kernel(**inputs):
    import numpy as _np
    import concourse.bacc as _bacc
    from concourse import mybir as _mybir
    from concourse.bass_utils import run_bass_kernel_spmd as _run

    nc = _bacc.Bacc("TRN2", target_bir_lowering=False, num_devices=1)
    arrays, args = {}, {}
    for name in inputs:
        a = _np.ascontiguousarray(inputs[name])
        arrays[f"in_{name}_dram"] = a
        args[name] = nc.dram_tensor(f"in_{name}_dram", a.shape, _mybir.dt.from_np(a.dtype), kind="ExternalInput").ap()
    shape, dtype = _OUTS[0]
    out = nc.dram_tensor("out_0_dram", shape, _mybir.dt.from_np(_np.dtype(dtype)), kind="ExternalOutput").ap()
    gnn_stack(nc, args, out)
    r = _run(nc, [arrays], core_ids=[0])
    return r.results[0]["out_0_dram"]
```

```python
import concourse.bass as bass
from concourse import mybir
from contextlib import ExitStack


class Chain:

    def __init__(self, engine, sem):
        self.engine, self.sem, self.done, self.turn, self.per = engine, sem, 0, None, 0

    def begin(self, turn, per):
        self.turn, self.per, self.first = turn, per, self.done

    def end(self, turns):
        assert self.done - self.first == self.per, (self.done - self.first, self.per)
        self.done, self.turn = self.first + turns * self.per, None

    def link(self, ins):
        ins.then_inc(self.sem, 1)
        self.done += 1
        self.engine.wait_ge(self.sem, self.done if self.turn is None else self.turn * self.per + self.done)


def gnn_stack(nc, t, out, layers=4):
    f32, i32, bf16, f16 = mybir.dt.float32, mybir.dt.int32, mybir.dt.bfloat16, mybir.dt.float16
    ALU, ACT, AX = mybir.AluOpType, mybir.ActivationFunctionType, mybir.AxisListType

    P = 128
    N, D = t["x"].shape
    E = t["src"].shape[0]
    NJ = 26
    NV = -(-N // P)
    LASTN = N - (NV - 1) * P
    Q = -(-E // 512)
    LASTE = E - (Q - 1) * 512
    G = 4
    M2 = P // 4
    NV2 = -(-N // M2)
    SL, K1, NI = 3, 4, 444
    SL2, K2, NI2 = 4, 5, 528
    Q1, Q2 = NI // K1, 104
    assert NI >= 4 * Q + NV - 1 and NI % (SL * G) == 0 and NI == Q1 * K1 and Q1 <= P
    assert NI2 >= Q2 * K2 >= 4 * Q + NV2 - 1 and NI2 % (SL2 * G) == 0 and Q2 <= P
    turns = {"A0": NI // (SL * G), "A1": NI // (SL * G), "B1": NI // (SL * G),
             "A2": NI2 // (SL2 * G), "B2": NI2 // (SL2 * G), "A3": NI // (SL * G)}
    IT, IT2 = turns["A0"], turns["A2"]
    H, C = t["L1_gnn_att_src"].shape
    R = t["L2_gnn_W_R"].shape[0]
    T8 = t["L3_gnn_message_W"].shape[0]
    W1C = D + H
    BIG = 1e30
    FAR = 1e4
    ACC0 = SL * G + 1

    def past(b, *passes):
        return sum(turns[p] for p in passes if b < SL or p in ("A2", "B2"))

    dram = lambda name, shape: nc.dram_tensor(name, shape, f32, kind="Internal").ap()
    table1 = dram("table1", [NJ * P, W1C])
    spill1 = dram("spill1", [NI // G, P, G * W1C])
    table2 = dram("table2", [NJ * P * R, D])
    tableB = dram("tableB", [NJ * P, R * D])
    spill2 = dram("spill2", [NI2 // G, P, G * D])
    table3 = dram("table3", [NJ * P * T8, D])

    with ExitStack() as ctx:
        sb = lambda name, shape, dt=f32: ctx.enter_context(nc.sbuf_tensor(name, shape, dt))
        sem = lambda name: ctx.enter_context(nc.semaphore(name))

        X = sb("X", [P, NJ, D])
        Y = sb("Y", [P, NJ, D])
        wide = sb("wide", [P, NJ, R * (D + 1)])
        wide_flat = wide[:, :, :].rearrange("p j f -> p (j f)")
        big = wide[:, :, 256:256 + D]
        acc0 = wide[:, :, 0:D]
        acc1 = wide[:, :, 0:W1C + H]
        xh = wide[:, :, 384:384 + W1C]
        Btab = wide_flat[:, 0:NV2 * D].rearrange("p (u d) -> p u d", d=D)
        acc2 = wide_flat[:, 0:NV2 * (D + 1)].rearrange("p (u d) -> p u d", d=D + 1)
        own = sb("own", [P, 3, NJ, H])
        relTs = Y[:, 0:SL2 * G, :].rearrange("p (b g) d -> p b g d", g=G)
        ad = sb("ad", [P, NJ, H])
        stats = sb("stats", [P, NJ, 6])
        col = [sb(f"col{n}", [P, NJ]) for n in range(6)]
        den2 = sb("den2", [P, 2, 4 * NJ])

        ROW = max(K1, K2) * P
        region = sb("region", [P, 14 * ROW + 2])
        cells = lambda n, rows, width=ROW: region[0:rows, n * ROW:n * ROW + width]
        ints = {n: cells(m, Q, 512).bitcast(i32) for m, n in enumerate(("src", "dst", "t4", "t8"))}
        rows = {n: cells(4 + m, Q, 512) for m, n in enumerate(("src", "dst", "t4", "t8", "w", "j"))}
        tile_i = sb("tile_i", [Q, 8], i32)
        tile_f = sb("tile_f", [Q, 8, 4])
        spread = wide_flat[0:Q, 0:4 * NI2].rearrange("q (k i) -> q k i", k=4)
        iota = sb("iota", [P, 512])
        iota_items = wide_flat[:, 4 * NI2:5 * NI2]
        ident = sb("ident", [P, P])
        upper = sb("upper", [P, P])
        pick = sb("pick", [P, M2])
        item_i = sb("item_i", [P, 3, NI], i32)
        item_f = sb("item_f", [P, 5, NI])
        tab1 = {"j": item_i[:, 0, :], "src": item_i[:, 1, :], "src8": item_i[:, 2, :],
                "rel": item_f[:, 0, :], "w": item_f[:, 1, :], "dst": item_f[:, 2, :], "ok": item_f[:, 3, :], "jf": item_f[:, 4, :]}
        item_i2 = sb("item_i2", [P, 2, NI2], i32)
        item_f2 = sb("item_f2", [P, 4, NI2])
        tab2 = {"j": item_i2[:, 0, :], "src4": item_i2[:, 1, :],
                "rel": item_f2[:, 0, :], "ok": item_f2[:, 1, :], "dst": item_f2[:, 2, :], "t4": item_f2[:, 3, :],
                "jf": wide_flat[:, 5 * NI2:6 * NI2]}
        score_w = sb("score_w", [P, NI2 * H])
        score = score_w[:, 0:NI * H].rearrange("p (i h) -> p i h", h=H)
        score2 = score_w[:, :].rearrange("p (i h) -> p i h", h=R)
        weight = region[:, 8 * ROW:8 * ROW + NI * H].rearrange("p (i h) -> p i h", h=H)
        weight2 = region[:, 8 * ROW:8 * ROW + NI2]
        ends = sb("ends", [P, 4])
        resets_row = sb("resets_row", [4, P])
        before_row = sb("before_row", [4, P])
        after_row = sb("after_row", [4, P])
        carry = sb("carry", [P, 4])

        def scan_rows(rows_, width):
            c = lambda n: cells(n, rows_, width)
            return {"n": rows_, "width": width, "rv": [c(n) for n in range(4)], "rf": [c(4 + n) for n in range(4)],
                    "g": c(8), "scratch": c(9), "dst": c(10), "aux": c(11),
                    "reset": region[0:rows_, 12 * ROW:12 * ROW + width + 1],
                    "key": region[0:rows_, 13 * ROW + 1:13 * ROW + 2 + width]}
        S1, S2 = scan_rows(Q1, K1 * P), scan_rows(Q2, K2 * P)
        rok2 = S2["dst"]

        ix = sb("ix", [P, SL2, G], i32)
        ring = sb("ring", [P, SL2, G, W1C + H])
        ring2 = sb("ring2", [P, SL2, G, D + 1])
        oneh = sb("oneh", [P, SL2, G, P])
        onehT = sb("onehT", [P, SL2, G, P])
        stg = sb("stg", [P, 2, R + 1, D])
        tT = sb("tT", [P, 2, R + 1, D])
        W0 = sb("W0", [P, 2, D])
        bias0 = sb("bias0", [P, 2, D])
        WX = sb("WX", [P, D + 2 * H])
        r2f = ring2[:, :, :, :].rearrange("p s g f -> p (s g f)")
        rowv = {n: r2f[:, m * D:(m + 1) * D] for m, n in enumerate(("ln1_g", "ln1_b", "gat_b", "ln2_g", "ln2_b", "b2"))}
        w1 = r2f[:, 6 * D:8 * D]
        w2 = r2f[:, 8 * D:10 * D].rearrange("p (n d) -> p n d", n=2)
        b1 = sb("b1", [P, 2])
        att = onehT[:, 0, :, :]
        scaled_w = onehT[:, 1, :, :]
        gelT = sb("gelT", [P, 2, 2, D])
        relT = lambda b: relTs[:, b, :, :]
        trow = wide_flat[:, 0:4 * R * D].rearrange("p (b f) -> p b f", b=2)
        WV = sb("WV", [P, R, D])
        bVx = sb("bVx", [P, D])
        attq = sb("attq", [P, 2, D])
        a_b = sb("a_b", [P, 1])
        u4 = sb("u4", [P, 2, R])
        c4 = sb("c4", [P, 2, R])
        WRs, WRd = (region[:, n * R * D:(n + 1) * R * D].rearrange("p (r d) -> p r d", d=D) for n in range(2))
        bR = region[:, 2 * R * D:3 * R * D]
        WQK = region[:, 3 * R * D:5 * R * D]
        c4q = region[:, 5 * R * D:7 * R * D].rearrange("p (n f) -> p n f", n=2)
        W3 = region[:, 0:T8 * D].rearrange("p (t d) -> p t d", d=D)
        b3 = region[:, T8 * D:2 * T8 * D]
        gru_rows = region[:, 2 * T8 * D:(2 * T8 + 6) * D].rearrange("p (n d) -> p n d", d=D)
        gruT = region[:, (2 * T8 + 6) * D:(2 * T8 + 12) * D].rearrange("p (n d) -> p n d", n=2)
        gru_b = region[:, (2 * T8 + 12) * D:(2 * T8 + 16) * D]
        gru_b2 = region[:, (2 * T8 + 16) * D:(2 * T8 + 18) * D]

        PS = ctx.enter_context(nc.psum_tensor("PS", [P, 8, 512], f32))

        s_in = sem("edges_in")
        s_w = sem("weights_in")
        s_pad = sem("pads_set")
        s_const = sem("constants_made")
        s_pick = sem("pick_steps")
        s_const2 = sem("constants_shaped")
        s_chain = sem("vector_step")
        s_first = sem("tile_counts_summed")
        s_pre = sem("tile_prefix")
        s_spread = sem("spread_ready")
        s_items = sem("items_spread")
        s_tabs = sem("item_tables_ready")
        s_ix = [sem(f"indices_staged{b}") for b in range(SL2)]
        s_rows = [sem(f"rows_gathered{b}") for b in range(SL2)]
        s_oh = [sem(f"onehot_built{b}") for b in range(SL2)]
        s_scat = [sem(f"rows_scattered{b}") for b in range(SL2)]
        s_acc = sem("sums_added")
        s_staged = [sem(f"tile_staged{b}") for b in range(2)]
        s_turned = [sem(f"tile_turned{b}") for b in range(2)]
        s_tcopy = [sem(f"turned_copied{b}") for b in range(2)]
        s_prod = [sem(f"tile_product{b}") for b in range(2)]
        s_take = [sem(f"product_taken{b}") for b in range(2)]
        s_arg = sem("function_arguments_ready")
        s_val = sem("function_values_ready")
        s_var = sem("root_in")
        s_std = sem("root_out")
        s_out = sem("out_written")
        s_w1 = sem("layer1_weights_in")
        s_ready = sem("node_rows_ready")
        s_written = [sem(f"table_rows_written{b}") for b in range(2)]
        s_tfree = [sem(f"table_rows_free{b}") for b in range(2)]
        s_table = sem("table_complete")
        s_ohturn = [sem(f"onehot_turned{b}") for b in range(SL2)]
        s_ohT = [sem(f"turned_onehot_copied{b}") for b in range(SL2)]
        s_spread1 = [sem(f"dst_values_spread{b}") for b in range(SL2)]
        s_scored = [sem(f"scores_stored{b}") for b in range(SL2)]
        s_spill = [sem(f"rows_spilled{b}") for b in range(SL2)]
        s_back = [sem(f"rows_back{b}") for b in range(SL2)]
        s_scaled = [sem(f"rows_weighted{b}") for b in range(SL)]
        s_torow = sem("values_for_rows")
        s_inrow = sem("values_in_rows")
        s_ends = sem("row_ends")
        s_endsT = sem("row_ends_turned")
        s_scan = sem("rows_scanned")
        s_scanT = sem("row_carries")
        s_exin = sem("exponents")
        s_max = sem("maxima_at_starts")
        s_maxT = sem("maxima_turned")
        s_w8 = sem("weights_in_items")
        s_tail = [sem(f"row_tails_set{b}") for b in range(SL2)]
        s_w2 = sem("layer2_weights_in")
        s_w3 = sem("layer3_weights_in")
        s_added = [sem(f"relation_sums{b}") for b in range(SL2)]
        s_relu = [sem(f"relation_rows{b}") for b in range(SL2)]
        s_relT = [sem(f"relation_rows_turned{b}") for b in range(SL2)]
        s_relTc = [sem(f"turned_relation_rows_copied{b}") for b in range(SL2)]
        s_s4 = [sem(f"relation_scores{b}") for b in range(SL2)]
        s_Bback = sem("node_parts_back")
        s_gruT = sem("gru_weights_turned")
        s_ex = sem("exponentials")
        s_exT = sem("exponentials_turned")
        s_mid = [sem(f"gelu_done{b}") for b in range(2)]
        s_prod2 = [sem(f"second_product{b}") for b in range(2)]
        s_final = sem("x_final")

        def window(b, it, slots=SL):
            return it * (slots * G) + b * G

        def four(bank):
            return PS[:, bank, :].rearrange("p (g d) -> p g d", g=G)

        def sums_of(b, k, width):
            return PS[:, 2 * b + k // 2, (k % 2) * 256:(k % 2) * 256 + width]

        def node_tiles(engine, tab, first, count):
            return nc.values_load_multi_w_load_instructions(tab["j"][0:1, bass.ds(first, G)], engines=[engine],
                                                            min_val=0, max_val=count - 1)[1]

        with nc.Block() as block:

            @block.sync
            def _(sp):
                sp.wait_ge(s_pad, 1)
                for name, key in (("src", "src"), ("dst", "dst"), ("t4", "edge_type_4"), ("t8", "edge_type_8")):
                    a = t[key]
                    sp.dma_start(ints[name][0:Q - 1, :], a[0:(Q - 1) * 512].rearrange("(q e) -> q e", e=512)).then_inc(s_in, 16)
                    sp.dma_start(ints[name][Q - 1:Q, 0:LASTE], a[(Q - 1) * 512:E].rearrange("(q e) -> q e", q=1)).then_inc(s_in, 16)
                a = t["edge_weight"]
                sp.dma_start(rows["w"][0:Q - 1, :], a[0:(Q - 1) * 512].rearrange("(q e) -> q e", e=512)).then_inc(s_in, 16)
                sp.dma_start(rows["w"][Q - 1:Q, 0:LASTE], a[(Q - 1) * 512:E].rearrange("(q e) -> q e", q=1)).then_inc(s_in, 16)
                sp.dma_start(X[:, 0:NV - 1, :], t["x"][0:(NV - 1) * P, :].rearrange("(j p) d -> p j d", p=P)).then_inc(s_w, 16)
                sp.dma_start(X[0:LASTN, NV - 1, :], t["x"][(NV - 1) * P:N, :]).then_inc(s_w, 16)
                sp.dma_start(W0[:, 0, :], t["L0_gnn_W1"]).then_inc(s_w, 16)
                sp.dma_start(W0[:, 1, :], t["L0_gnn_W2"]).then_inc(s_w, 16)
                sp.dma_start(bias0[:, 0, :], t["L0_gnn_b1"][0, :].partition_broadcast(P)).then_inc(s_w, 16)
                sp.dma_start(bias0[:, 1, :], t["L0_gnn_b2"][0, :].partition_broadcast(P)).then_inc(s_w, 16)
                if layers > 1:
                    sp.dma_start(WX[:, 0:D], t["L1_gnn_W"]).then_inc(s_w1, 16)
                    for n, name in enumerate(("L1_gnn_att_src", "L1_gnn_att_dst")):
                        sp.dma_start(att[:, n, :], t[name].rearrange("h c -> (h c)").partition_broadcast(P)).then_inc(s_w1, 16)
                    for name, tile in rowv.items():
                        sp.dma_start(tile, t["L1_gnn_" + name].partition_broadcast(P)).then_inc(s_w1, 16)
                    sp.dma_start(w1, t["L1_gnn_w1"]).then_inc(s_w1, 16)
                    sp.dma_start(w2[:, :, :], t["L1_gnn_w2"].rearrange("(a p) d -> p a d", p=P)).then_inc(s_w1, 16)
                    sp.dma_start(b1[:, :], t["L1_gnn_b1"].rearrange("(a p) -> p a", p=P),
                                 allow_slow_non_contiguous=True).then_inc(s_w1, 16)

                    def write_table(base, wbase, tables):
                        with sp.Fori(0, NJ // 2) as it:
                            for b in range(2):
                                sp.wait_ge(s_take[b], it + (base + 2))
                                for table, row in tables(it, b):
                                    sp.dma_start(table.rearrange("(j p) d -> j p d", p=P)[bass.ds(it * 2 + b, 1), :, :]
                                                 .rearrange("o p d -> (o p) d"), row).then_inc(s_written[b], 16)
                            for b in range(2):
                                sp.wait_ge(s_written[b], it * (16 * len(tables(it, b))) + (wbase + len(tables(it, b))) * 16)
                                sp.sem_inc(s_tfree[b], 1)
                        sp.sem_inc(s_table, 1)

                    def spill(p, slots, gathered, ring_tile, width, store):
                        with sp.Fori(0, turns[p]) as it:
                            for b in range(slots):
                                sp.wait_ge(*gathered(b, it))
                                sp.dma_start(store[bass.ds(it * slots + b, 1), :, :].rearrange("o p d -> (o p) d").rearrange("p (g d) -> p g d", g=G),
                                             ring_tile[:, b, :, 0:width]).then_inc(s_spill[b], 16)
                        for b in range(slots):
                            sp.wait_ge(s_spill[b], past(b, *(("A1",) if p == "A1" else ("A1", "A2"))) * 16 + 16)

                    def unspill(p, slots, ring_tile, width, store):
                        with sp.Fori(0, turns[p]) as it:
                            for b in range(slots):
                                sp.wait_ge(s_scat[b], it + (past(b, *(("A0",) if p == "B1" else ("A0", "B1"))) + 1))
                                sp.dma_start(ring_tile[:, b, :, 0:width],
                                             store[bass.ds(it * slots + b, 1), :, :].rearrange("o p d -> (o p) d").rearrange("p (g d) -> p g d", g=G)).then_inc(s_back[b], 16)

                    write_table(13, 0, lambda it, b: [(table1, xh[:, bass.ds(it * 2 + b, 1), :].rearrange("p o d -> p (o d)"))])
                    spill("A1", SL, lambda b, it: (s_rows[b], it * (16 * G) + (IT + 1) * 16 * G), ring, W1C, spill1)
                    for b in range(SL):
                        sp.wait_ge(s_scored[b], 1 + IT)
                    unspill("B1", SL, ring, W1C, spill1)
                if layers > 2:
                    sp.wait_ge(s_maxT, 1)
                    flat2 = lambda a: a.rearrange("a d -> (a d)").partition_broadcast(P)
                    sp.dma_start(WRs[:, :, :], t["L2_gnn_W_R"][:, 0:D, :].rearrange("r k d -> k r d")).then_inc(s_w2, 16)
                    sp.dma_start(WRd[:, :, :], t["L2_gnn_W_R"][:, D:2 * D, :].rearrange("r k d -> k r d")).then_inc(s_w2, 16)
                    sp.dma_start(WV[:, :, :], t["L2_gnn_W_V"].rearrange("r k d -> k r d")).then_inc(s_w2, 16)
                    for n, name in enumerate(("Q", "K")):
                        sp.dma_start(WQK[:, n * R * D:(n + 1) * R * D].rearrange("p (r d) -> p r d", d=D), t["L2_gnn_W_" + name].rearrange("r k d -> k r d")).then_inc(s_w2, 16)
                        sp.dma_start(c4q[:, n, :], flat2(t["L2_gnn_b_" + name])).then_inc(s_w2, 16)
                        sp.dma_start(attq[:, n, :], flat2(t["L2_gnn_a_w"][n * D:(n + 1) * D, :])).then_inc(s_w2, 16)
                    sp.dma_start(bR[:, :], flat2(t["L2_gnn_b_R"])).then_inc(s_w2, 16)
                    for r in range(R):
                        sp.dma_start(bVx[r * M2:(r + 1) * M2, :], t["L2_gnn_b_V"][r, :].partition_broadcast(M2)).then_inc(s_w2, 16)
                    sp.dma_start(a_b[:, :], t["L2_gnn_a_b"].partition_broadcast(P)).then_inc(s_w2, 16)
                    write_table(39, NJ // 2, lambda it, b: [(table2.rearrange("(n r) d -> n (r d)", r=R), trow[:, b, 0:R * D]),
                                                            (tableB, trow[:, b, R * D:2 * R * D])])
                    for r in range(R):
                        sp.dma_start(Btab[r * M2:(r + 1) * M2, :, :],
                                     tableB[0:NV2 * M2, r * D:(r + 1) * D].rearrange("(u m) d -> m u d", m=M2)).then_inc(s_Bback, 16)
                    spill("A2", SL2, lambda b, it: (s_relu[b], it + 1), ring2, D, spill2)
                    for b in range(SL2):
                        sp.wait_ge(s_scored[b], 1 + past(b, "A1", "A2"))
                    unspill("B2", SL2, ring2, D, spill2)
                if layers > 3:
                    sp.wait_ge(s_maxT, 2)
                    sp.dma_start(W3[:, :, :], t["L3_gnn_message_W"].rearrange("t k d -> k t d")).then_inc(s_w3, 16)
                    sp.dma_start(b3[:, :], flat2(t["L3_gnn_message_b"])).then_inc(s_w3, 16)
                    sp.dma_start(gru_rows[:, 0:3, :], t["L3_gnn_gru_w_ih"].rearrange("(a p) d -> p a d", p=P)).then_inc(s_w3, 16)
                    sp.dma_start(gru_rows[:, 3:6, :], t["L3_gnn_gru_w_hh"].rearrange("(a p) d -> p a d", p=P)).then_inc(s_w3, 16)
                    sp.dma_start(gru_b[:, 0:3 * D], t["L3_gnn_gru_b_ih"].partition_broadcast(P)).then_inc(s_w3, 16)
                    sp.dma_start(gru_b[:, 3 * D:4 * D], t["L3_gnn_gru_b_hh"][2 * D:3 * D].partition_broadcast(P)).then_inc(s_w3, 16)
                    sp.dma_start(gru_b2[:, :], t["L3_gnn_gru_b_hh"][0:2 * D].partition_broadcast(P)).then_inc(s_w3, 16)
                    write_table(65, 3 * (NJ // 2), lambda it, b: [(table3.rearrange("(n t) d -> n (t d)", t=T8), trow[:, b, :])])
                sp.wait_ge(s_final, 1)
                sp.dma_start(out[0:(NV - 1) * P, :].rearrange("(j p) d -> p j d", p=P), X[:, 0:NV - 1, :]).then_inc(s_out, 16)
                sp.dma_start(out[(NV - 1) * P:N, :], X[0:LASTN, NV - 1, :]).then_inc(s_out, 16)
                sp.wait_ge(s_out, 32)

            @block.gpsimd
            def _(pool):
                pool.iota(iota[:, :], [[1, 512]], base=0, channel_multiplier=0,
                          allow_small_or_imprecise_dtypes=True)
                pool.iota(iota_items, [[1, NI2]], base=0, channel_multiplier=0,
                          allow_small_or_imprecise_dtypes=True)
                pool.memset(ident[:, :], 0.0)
                pool.memset(pick[:, :], 0.0)
                pool.memset(upper[:, :], 1.0).then_inc(s_const, 1)
                pool.wait_ge(s_const, 1)
                pool.affine_select(out=ident[:, :], in_=ident[:, :], compare_op=ALU.not_equal, fill=1.0,
                                   base=0, pattern=[[-1, P]], channel_multiplier=1)
                for r in range(R):
                    pool.affine_select(out=pick[:, :], in_=pick[:, :], compare_op=ALU.not_equal, fill=1.0,
                                       base=-r * M2, pattern=[[-1, M2]], channel_multiplier=1).then_inc(s_pick, 1)
                    pool.wait_ge(s_pick, r + 1)
                pool.affine_select(out=upper[:, :], in_=upper[:, :], compare_op=ALU.is_gt, fill=0.0,
                                   base=0, pattern=[[1, P]], channel_multiplier=-1).then_inc(s_const2, 1)

                def gather_loop(p, before, slots, table, width, tables=0):
                    if tables:
                        pool.wait_ge(s_table, tables)
                    arm = [pool.alloc_register(f"gather_{p}_{b}") for b in range(slots)]
                    for b in range(slots):
                        pool.reg_mov(arm[b], past(b, *before))
                    with pool.Fori(0, turns[p]) as it:
                        for b in range(slots):
                            pool.reg_add(arm[b], arm[b], 1)
                            pool.wait_ge(s_const2, 1)
                            pool.wait_ge(s_ix[b], arm[b])
                            for k in range(G):
                                pool.indirect_dma_start(
                                    ring[:, b, k, 0:width], None, table,
                                    bass.IndirectOffsetOnAxis(ap=ix[:, b, k:k + 1], axis=0)).then_inc(s_rows[b], 16)

                gather_loop("A0", (), SL, t["x"], D)
                if layers > 1:
                    gather_loop("A1", ("A0",), SL, table1, W1C, 1)
                    pool.wait_ge(s_w8, 1)
                    with pool.Fori(0, IT) as it:
                        for b in range(SL):
                            pool.wait_ge(s_back[b], it * 16 + 16)
                            feats = ring[:, b, :, 0:D].rearrange("p g (h c) -> p g h c", c=C)
                            pool.tensor_tensor(feats, feats, weight[:, bass.ds(window(b, it), G), :].unsqueeze(3).to_broadcast([P, G, H, C]),
                                               ALU.mult).then_inc(s_scaled[b], 1)
                if layers > 2:
                    gather_loop("A2", ("A0", "A1"), SL2, table2, D, 2)
                if layers > 3:
                    gather_loop("A3", ("A0", "A1", "A2"), SL, table3, D, 3)

            @block.scalar
            def _(act):
                chain = 0

                def stage_indices(table, before, it, b):
                    act.wait_ge(s_scat[b], it + (past(b, *before) + 1))
                    act.copy(ix[:, b, :], table[:, bass.ds(window(b, it), G)]).then_inc(s_ix[b], 1)

                def copy_turned(base, it, b, width, n=1):
                    act.wait_ge(s_turned[b], it + (base + 2))
                    act.wait_ge(s_prod[b], it + (base + 1))
                    act.copy(tT[:, b, 0:n, :], PS[:, 4 + b, 0:n * D].rearrange("p (n d) -> p n d", d=D)).then_inc(s_tcopy[b], 1)

                def roots(n):
                    act.wait_ge(s_var, n + 1)
                    act.activation(col[1][:, :], col[0][:, :], ACT.Sqrt).then_inc(s_std, 1)

                act.wait_ge(s_tabs, 1)
                with act.Fori(0, IT) as it:
                    for b in range(SL):
                        stage_indices(tab1["src"], (), it, b)
                with act.Fori(0, NJ // 2) as it:
                    for b in range(2):
                        copy_turned(0, it, b, D, 2)
                act.wait_ge(s_arg, 1)
                act.activation(big, Y[:, :, :], ACT.Square).then_inc(s_val, 1)
                roots(0)
                roots(1)
                if layers > 1:
                    def stage_tile(source, base, it, b):
                        act.wait_ge(s_turned[b], it + (base + 1))
                        act.copy(stg[:, b, 0, :], source[:, bass.ds(it * 2 + b, 1), :].rearrange("p o d -> p (o d)")).then_inc(s_staged[b], 1)

                    roots(2)
                    act.wait_ge(s_ready, 1)
                    with act.Fori(0, NJ // 2) as it:
                        for b in range(2):
                            stage_tile(Y, 13, it, b)
                        for b in range(2):
                            copy_turned(13, it, b, D)
                    with act.Fori(0, IT) as it:
                        for b in range(SL):
                            act.wait_ge(s_scored[b], it + 1)
                            act.wait_ge(s_spill[b], it * 16 + 16)
                            act.copy(ix[:, b, :], tab1["src"][:, bass.ds(window(b, it), G)]).then_inc(s_ix[b], 1)
                        for b in range(SL):
                            act.wait_ge(s_ohturn[b], it + 2)
                            act.wait_ge(s_spread1[b], it + 1)
                            act.copy(onehT[:, b, :, :], four(b)).then_inc(s_ohT[b], 1)

                    def exponentials(n, tiles):
                        for h in range(H):
                            act.wait_ge(s_exin, n * H + h + 1)
                            act.activation(tiles[h], tiles[h], ACT.Exp, scale=-1.0).then_inc(s_ex, 1)

                    exponentials(0, S1["rv"])
                    with act.Fori(0, IT) as it:
                        for b in range(SL):
                            act.wait_ge(s_back[b], it * 16 + 16)
                            act.wait_ge(s_w8, 1)
                            act.copy(ring[:, b, :, W1C:W1C + H], score[:, bass.ds(window(b, it), G), :])
                            act.copy(ring[:, b, :, D:W1C], weight[:, bass.ds(window(b, it), G), :]).then_inc(s_tail[b], 1)
                    act.wait_ge(s_arg, 2)
                    act.activation(own[:, 0:2, :, :], own[:, 0:2, :, :], ACT.Exp, scale=-1.0).then_inc(s_val, 1)
                    roots(3)
                    act.wait_ge(s_ready, 2)
                    with act.Fori(0, NJ // 2) as it:
                        for b in range(2):
                            stage_tile(big, 26, it, b)
                        for b in range(2):
                            copy_turned(26, it, b, D)
                        for b in range(2):
                            act.wait_ge(s_prod[b], it + 28)
                            act.wait_ge(s_prod2[b], it + 1)
                            act.activation(gelT[:, b, 0, :], PS[:, 6 + b, 0:D], ACT.Gelu, bias=b1[:, 0:1])
                            act.activation(gelT[:, b, 1, :], PS[:, 6 + b, D:2 * D], ACT.Gelu, bias=b1[:, 1:2]).then_inc(s_mid[b], 1)
                    roots(4)
                if layers > 2:
                    act.wait_ge(s_ready, 3)
                    with act.Fori(0, NJ // 2) as it:
                        for b in range(2):
                            stage_tile(X, 39, it, b)
                        for b in range(2):
                            copy_turned(39, it, b, D)
                    with act.Fori(0, IT2) as it:
                        for b in range(SL2):
                            act.wait_ge(s_added[b], it + 1)
                            act.copy(ix[:, b, :], tab2["src4"][:, bass.ds(window(b, it, SL2), G)]).then_inc(s_ix[b], 1)
                        for b in range(SL2):
                            act.wait_ge(s_ohturn[b], it + (past(b, "A1") + 2))
                            act.wait_ge(s_spread1[b], it + (past(b, "A1") + 1))
                            act.copy(onehT[:, b, :, :], four(2 * b)).then_inc(s_ohT[b], 1)
                        for b in range(SL2):
                            act.wait_ge(s_relT[b], it + 1)
                            act.copy(relT(b), four(2 * b)).then_inc(s_relTc[b], 1)
                    exponentials(1, S2["rv"])
                    with act.Fori(0, IT2) as it:
                        for b in range(SL2):
                            act.wait_ge(s_back[b], it * 16 + (past(b, "B1") + 1) * 16)
                            act.wait_ge(s_w8, 2)
                            for k in range(G):
                                w = weight2[:, bass.ds(window(b, it, SL2) + k, 1)]
                                act.activation(ring2[:, b, k, 0:D], ring2[:, b, k, 0:D], ACT.Copy, scale=w)
                                ins = act.copy(ring2[:, b, k, D:D + 1], w)
                            ins.then_inc(s_tail[b], 1)
                    with act.Fori(0, NJ // 2) as it:
                        for b in range(2):
                            act.wait_ge(s_turned[b], it + 54)
                            act.wait_ge(s_prod[b], it + 53)
                            act.copy(tT[:, b, 0:R, :].rearrange("p r (u m) -> p u r m", m=M2),
                                     PS[:, 4 + b, :].rearrange("p (u r m) -> p u r m", u=4, m=M2)).then_inc(s_tcopy[b], 1)
                    act.wait_ge(s_arg, 3)
                    act.activation(big, big, ACT.Exp).then_inc(s_val, 1)
                    roots(5)
                if layers > 3:
                    act.wait_ge(s_gruT, 1)
                    for n in range(2):
                        ins = act.copy(gruT[:, n, :], PS[:, n, 0:3 * D])
                    act.wait_ge(s_ready, 4)
                    with act.Fori(0, NJ // 2) as it:
                        for b in range(2):
                            stage_tile(X, 65, it, b)
                        for b in range(2):
                            copy_turned(65, it, b, D)
                    with act.Fori(0, IT) as it:
                        for b in range(SL):
                            stage_indices(tab1["src8"], ("A0", "B1", "B2"), it, b)
                    act.wait_ge(s_ready, 5)
                    with act.Fori(0, NJ // 2) as it:
                        for b in range(2):
                            act.wait_ge(s_turned[b], it + 79)
                            act.copy(stg[:, b, 0, :], X[:, bass.ds(it * 2 + b, 1), :].rearrange("p o d -> p (o d)"))
                            act.copy(stg[:, b, 1, :], Y[:, bass.ds(it * 2 + b, 1), :].rearrange("p o d -> p (o d)")).then_inc(s_staged[b], 1)
                        for b in range(2):
                            copy_turned(78, it, b, D, 2)
                    act.wait_ge(s_arg, 4)
                    act.activation(wide[:, :, 0:2 * D], wide[:, :, 0:2 * D], ACT.Sigmoid).then_inc(s_val, 1)
                    act.wait_ge(s_arg, 5)
                    act.activation(wide[:, :, 2 * D:3 * D], wide[:, :, 2 * D:3 * D], ACT.Tanh).then_inc(s_val, 1)
                    roots(6)

            @block.tensor
            def _(pe):
                pe.wait_ge(s_const2, 1)
                for b in range(2):
                    pe.sem_inc(s_turned[b], 1)
                    pe.sem_inc(s_prod[b], 1)
                    pe.sem_inc(s_prod2[b], 1)
                for b in range(SL2):
                    pe.sem_inc(s_scat[b], 1)
                    pe.sem_inc(s_ohturn[b], 1)
                    pe.sem_inc(s_spread1[b], 1)
                def spread_items(n, names, items):
                    pe.wait_ge(s_first, n + 1)
                    pe.matmul(PS[0:Q, 7, 508:509], upper[0:Q, 0:Q], tile_f[:, 4, 3:4], start=True, stop=True).then_inc(s_pre, 1)
                    pe.wait_ge(s_spread, n + 1)
                    step = items if items <= 512 else items // 2
                    for m, name in enumerate(names):
                        for a in range(0, items, step):
                            bank = m if step == items else 2 * m + a // step
                            for k in range(4):
                                mm = pe.matmul(PS[:, bank, 0:step], rows[name][:, k * P:(k + 1) * P], spread[:, k, a:a + step],
                                               start=k == 0, stop=k == 3)
                    mm.then_inc(s_items, 1)

                spread_items(0, ("src", "dst", "t8", "w", "j"), NI)
                spread_items(1, ("src", "dst", "t4", "j"), NI2)

                def scatter(first, arrived, oh_before, it, b, width):
                    pe.wait_ge(*arrived)
                    pe.wait_ge(s_oh[b], it + (past(b, *oh_before) + 1))
                    pe.wait_ge(s_acc, it * (SL * G) + (first + b * G + G - SL * G))
                    for k in range(G):
                        mm = pe.matmul(sums_of(b, k, width), oneh[:, b, k, :], ring[:, b, k, 0:width],
                                       start=True, stop=True)
                    mm.then_inc(s_scat[b], 1)

                def turn(base, it, b, n=1):
                    pe.wait_ge(s_staged[b], it + (base + 2))
                    pe.wait_ge(s_tcopy[b], it + (base + 1))
                    for m in range(n):
                        mm = pe.transpose(PS[:, 4 + b, m * D:(m + 1) * D], stg[:, b, m, :], ident[:, :])
                    mm.then_inc(s_turned[b], 1)

                def product(base, it, b, outs):
                    pe.wait_ge(s_tcopy[b], it + (base + 2))
                    pe.wait_ge(s_take[b], it + (base + 1))
                    for to, pairs in outs:
                        for n, (lhs, rhs) in enumerate(pairs):
                            mm = pe.matmul(to, lhs, rhs, start=n == 0, stop=n == len(pairs) - 1)
                    mm.then_inc(s_prod[b], 1)

                pe.wait_ge(s_tabs, 1)
                with pe.Fori(0, IT) as it:
                    for b in range(SL):
                        scatter(ACC0, (s_rows[b], it * (16 * G) + 16 * G), (), it, b, D)
                pe.wait_ge(s_w, 96)
                with pe.Fori(0, NJ // 2) as it:
                    for b in range(2):
                        turn(0, it, b, 2)
                    for b in range(2):
                        product(0, it, b, [(PS[:, 6 + b, 0:D], [(tT[:, b, 0, :], W0[:, 0, :]), (tT[:, b, 1, :], W0[:, 1, :])])])
                if layers > 1:
                    def to_rows(n, S, K, tables):
                        pe.wait_ge(s_torow, n + 1)
                        for m, table in enumerate(tables):
                            for k in range(K):
                                at = m * (512 if K <= 4 else 1024) + k * P
                                mm = pe.transpose(PS[0:S["n"], at // 512, at % 512:at % 512 + P], table[:, k:K * S["n"]:K], ident[:, :])
                        mm.then_inc(s_inrow, 1)

                    def turn_ends(n, S):
                        pe.wait_ge(s_ends, n + 1)
                        pe.transpose(PS[0:4, 4, 0:S["n"]], ends[0:S["n"], :], ident[0:S["n"], 0:S["n"]]).then_inc(s_endsT, 1)

                    def turn_carries(n, S, row):
                        pe.wait_ge(s_scan, n + 1)
                        pe.transpose(PS[0:S["n"], 4, 256:260], row, ident[0:4, 0:4]).then_inc(s_scanT, 1)

                    def segment_starts(n, S, K, tables):
                        to_rows(n, S, K, tables)
                        turn_ends(4 * (n // 2), S)
                        turn_carries(3 * (n // 2), S, before_row[:, 0:S["n"]])
                        turn_ends(4 * (n // 2) + 1, S)

                    def segment_maxima(n, S, K, tables):
                        to_rows(2 * n + 1, S, K, tables)
                        turn_ends(4 * n + 2, S)
                        turn_carries(3 * n + 1, S, before_row[:, 0:S["n"]])
                        turn_ends(4 * n + 3, S)
                        turn_carries(3 * n + 2, S, after_row[:, 1:S["n"] + 1])

                    def to_items(S, K, tile, bank):
                        for k in range(K):
                            at = bank + k // 4
                            mm = pe.transpose(PS[:, at, (k % 4) * S["n"]:(k % 4 + 1) * S["n"]], tile[:, k * P:(k + 1) * P],
                                              ident[0:S["n"], 0:S["n"]])
                        return mm

                    segment_starts(0, S1, K1, [tab1[n] for n in ("dst", "ok")])
                    pe.wait_ge(s_ready, 1)
                    with pe.Fori(0, NJ // 2) as it:
                        for b in range(2):
                            turn(13, it, b)
                        for b in range(2):
                            product(13, it, b, [(PS[:, 6 + b, 0:D + 2 * H], [(tT[:, b, 0, :], WX[:, :])])])
                    with pe.Fori(0, IT) as it:
                        for b in range(SL):
                            pe.wait_ge(s_oh[b], it + (IT + 1))
                            pe.wait_ge(s_ohT[b], it + 1)
                            for k in range(G):
                                mm = pe.transpose(four(b)[:, k, :], oneh[:, b, k, :], ident[:, :])
                            mm.then_inc(s_ohturn[b], 1)
                        for b in range(SL):
                            j = node_tiles(mybir.EngineType.PE, tab1, window(b, it), NV)
                            pe.wait_ge(s_ohT[b], it + 2)
                            pe.wait_ge(s_scored[b], it + 1)
                            for k in range(G):
                                mm = pe.matmul(PS[:, SL + b, k * H:(k + 1) * H], onehT[:, b, k, :],
                                               ad[:, bass.ds(j[k], 1), :].rearrange("p o h -> p (o h)"), start=True, stop=True)
                            mm.then_inc(s_spread1[b], 1)
                    segment_maxima(0, S1, K1, [score[:, :, h] for h in range(H)])
                    for h in range(H):
                        pe.wait_ge(s_ex, h + 1)
                        to_items(S1, K1, S1["rv"][h], h).then_inc(s_exT, 1)
                    pe.wait_ge(s_max, 1)
                    for h in range(H):
                        mm = to_items(S1, K1, S1["rf"][h], 4 + h)
                    mm.then_inc(s_maxT, 1)
                    with pe.Fori(0, IT) as it:
                        for b in range(SL):
                            pe.wait_ge(s_tail[b], it + 1)
                            scatter(ACC0 + NI, (s_scaled[b], it + 1), ("A0", "A1"), it, b, W1C + H)
                    pe.wait_ge(s_ready, 2)
                    with pe.Fori(0, NJ // 2) as it:
                        for b in range(2):
                            turn(26, it, b)
                        for b in range(2):
                            pe.wait_ge(s_mid[b], it + 1)
                            product(26, it, b, [(PS[:, 6 + b, a * D:(a + 1) * D], [(w1[:, a * D:(a + 1) * D], tT[:, b, 0, :])]) for a in range(2)])
                        for b in range(2):
                            pe.wait_ge(s_mid[b], it + 2)
                            for a in range(2):
                                mm = pe.matmul(PS[:, 2 + b, 0:D], gelT[:, b, a, :], w2[:, a, :], start=a == 0, stop=a == 1)
                            mm.then_inc(s_prod2[b], 1)

                if layers > 2:
                    pe.wait_ge(s_ready, 3)
                    with pe.Fori(0, NJ // 2) as it:
                        for b in range(2):
                            turn(39, it, b)
                        for b in range(2):
                            product(39, it, b, [(PS[:, 6 + b, :], [(tT[:, b, 0, :], WRs[:, :, :].rearrange("p r d -> p (r d)"))]),
                                                (PS[:, 2 + b, :], [(tT[:, b, 0, :], WRd[:, :, :].rearrange("p r d -> p (r d)"))])])
                    segment_starts(2, S2, K2, [tab2["dst"], tab2["ok"], tab2["t4"]])
                    pe.wait_ge(s_Bback, R * 16)
                    with pe.Fori(0, IT2) as it:
                        for b in range(SL2):
                            pe.wait_ge(s_oh[b], it + (past(b, "A0", "A1", "B1") + 1))
                            pe.wait_ge(s_ohT[b], it + (past(b, "A1") + 1))
                            pe.wait_ge(s_scored[b], it + (past(b, "A1") + 1))
                            for k in range(G):
                                mm = pe.transpose(four(2 * b)[:, k, :], oneh[:, b, k, :], ident[:, :])
                            mm.then_inc(s_ohturn[b], 1)
                        for b in range(SL2):
                            j = node_tiles(mybir.EngineType.PE, tab2, window(b, it, SL2), NV2)
                            pe.wait_ge(s_ohT[b], it + (past(b, "A1") + 2))
                            pe.wait_ge(s_added[b], it + 1)
                            for k in range(G):
                                mm = pe.matmul(four(2 * b + 1)[:, k, :], onehT[:, b, k, :],
                                               Btab[:, bass.ds(j[k], 1), :].rearrange("p o d -> p (o d)"), start=True, stop=True)
                            mm.then_inc(s_spread1[b], 1)
                        for b in range(SL2):
                            pe.wait_ge(s_relu[b], it + 1)
                            for k in range(G):
                                mm = pe.transpose(four(2 * b)[:, k, :], ring2[:, b, k, 0:D], ident[:, :])
                            mm.then_inc(s_relT[b], 1)
                        for b in range(SL2):
                            pe.wait_ge(s_relTc[b], it + 1)
                            for k in range(G):
                                mm = pe.matmul(PS[:, 2 * b, k * R:(k + 1) * R], relT(b)[:, k, :], u4[:, 0, :], start=True, stop=True)
                            mm.then_inc(s_s4[b], 1)
                    segment_maxima(1, S2, K2, [score2[:, :, r] for r in range(R)])
                    pe.wait_ge(s_max, 2)
                    to_items(S2, K2, S2["rv"][0], 0).then_inc(s_maxT, 1)
                    with pe.Fori(0, IT2) as it:
                        for b in range(SL2):
                            pe.wait_ge(s_tail[b], it + (past(b, "B1") + 1))
                            pe.wait_ge(s_oh[b], it + (past(b, "A0", "A1", "B1", "A2") + 1))
                            pe.wait_ge(s_acc, it * (SL2 * G) + (ACC0 + 2 * NI + b * G + G - SL2 * G))
                            for k in range(G):
                                mm = pe.matmul(sums_of(b, k, D + 1), oneh[:, b, k, :], ring2[:, b, k, :], start=True, stop=True)
                            mm.then_inc(s_scat[b], 1)
                    with pe.Fori(0, NJ // 2) as it:
                        for b in range(2):
                            pe.wait_ge(s_staged[b], it + 54)
                            pe.wait_ge(s_tcopy[b], it + 53)
                            for r in range(R):
                                mm = pe.transpose(PS[:, 4 + b, r * D:(r + 1) * D], stg[:, b, r, :], ident[:, :])
                            mm.then_inc(s_turned[b], 1)
                        for b in range(2):
                            product(52, it, b, [(PS[:, 6 + b, 0:D], [(tT[:, b, r, :], WV[:, r, :]) for r in range(R)] + [(stg[:, b, R, :], bVx[:, :])])])
                if layers > 3:
                    pe.wait_ge(s_w3, 7 * 16)
                    pe.wait_ge(s_acc, ACC0 + 2 * NI + NI2)
                    for n in range(2):
                        for a in range(3):
                            mm = pe.transpose(PS[:, n, a * D:(a + 1) * D], gru_rows[:, 3 * n + a, :], ident[:, :])
                    mm.then_inc(s_gruT, 1)
                    pe.wait_ge(s_ready, 4)
                    with pe.Fori(0, NJ // 2) as it:
                        for b in range(2):
                            turn(65, it, b)
                        for b in range(2):
                            product(65, it, b, [(PS[:, (6, 2)[a] + b, :], [(tT[:, b, 0, :], W3[:, 4 * a:4 * a + 4, :].rearrange("p r d -> p (r d)"))]) for a in range(2)])
                    with pe.Fori(0, IT) as it:
                        for b in range(SL):
                            scatter(ACC0 + 2 * NI + NI2, (s_rows[b], it * (16 * G) + (past(b, "A0", "A1", "A2") + 1) * 16 * G),
                                    ("A0", "A1", "B1", "A2", "B2"), it, b, D)
                    pe.wait_ge(s_ready, 5)
                    with pe.Fori(0, NJ // 2) as it:
                        for b in range(2):
                            turn(78, it, b, 2)
                        for b in range(2):
                            hT, mT = tT[:, b, 0, :], tT[:, b, 1, :]
                            product(78, it, b, [(PS[:, 6 + b, 0:2 * D], [(mT, gruT[:, 0, 0:2 * D]), (hT, gruT[:, 1, 0:2 * D])]),
                                                (PS[:, 6 + b, 2 * D:3 * D], [(mT, gruT[:, 0, 2 * D:3 * D])]),
                                                (PS[:, 6 + b, 3 * D:4 * D], [(hT, gruT[:, 1, 2 * D:3 * D])])])

            @block.vector
            def _(dve):
                ch = Chain(dve, s_chain)
                for name, value in (("src", 0), ("dst", 4095), ("t4", 0), ("t8", 0)):
                    dve.memset(ints[name][96:Q, :], value)
                dve.memset(X[:, NV - 1:NJ, :], 0.0)
                dve.memset(rows["w"][96:Q, :], 0.0).then_inc(s_pad, 1)
                for b in range(2):
                    dve.sem_inc(s_staged[b], 1)
                    dve.sem_inc(s_take[b], 1)
                    dve.sem_inc(s_tcopy[b], 1)
                    dve.sem_inc(s_mid[b], 1)
                    dve.sem_inc(s_tfree[b], 1)
                for b in range(SL2):
                    dve.sem_inc(s_ohT[b], 1)
                    dve.sem_inc(s_scored[b], 1)
                    dve.sem_inc(s_added[b], 1)
                    dve.sem_inc(s_spill[b], 16)
                dve.wait_ge(s_const2, 1)
                dve.wait_ge(s_in, 160)
                for name in ("src", "dst", "t4"):
                    dve.tensor_copy(rows[name], ints[name])
                ch.link(dve.tensor_copy(rows["t8"], ints["t8"]))
                first, last, cnt, ones, incl, off, end, delta = (tile_f[:, n, :] for n in range(8))

                def spread_items(n, tab, shift, tiles, items, parts):
                    dve.tensor_single_scalar(tile_i[:, 0:4], ints["dst"][:, 0:512:P], shift, ALU.arith_shift_right)
                    ch.link(dve.tensor_single_scalar(tile_i[:, 4:8], ints["dst"][:, P - 1:512:P], shift, ALU.arith_shift_right))
                    dve.tensor_copy(first, tile_i[:, 0:4])
                    dve.memset(ones, 1.0)
                    ch.link(dve.tensor_single_scalar(last, tile_i[:, 4:8], float(tiles - 1), ALU.min))
                    ch.link(dve.scalar_tensor_tensor(cnt, last, 1.0, first, ALU.add, ALU.subtract))
                    dve.tensor_tensor_scan(incl, ones, cnt, 0.0, ALU.mult, ALU.add).then_inc(s_first, 1)
                    dve.wait_ge(s_first, n + 1)
                    ch.link(dve.tensor_tensor(off, incl, cnt, ALU.subtract))
                    dve.wait_ge(s_pre, n + 1)
                    ch.link(dve.tensor_scalar(off, off, PS[0:Q, 7, 508:509], None, ALU.add))
                    dve.tensor_tensor(end, off, cnt, ALU.add)
                    ch.link(dve.tensor_tensor(delta, first, off, ALU.subtract))
                    for k in range(4):
                        dve.tensor_scalar(spread[:, k, 0:items], iota_items[0:Q, 0:items], off[:, k:k + 1], None, ALU.is_ge)
                    ch.link(dve.tensor_copy(rows["j"].rearrange("q (k e) -> q k e", e=P),
                                            delta.unsqueeze(2).to_broadcast([Q, 4, P])))
                    for k in range(4):
                        ins = dve.scalar_tensor_tensor(spread[:, k, 0:items], iota_items[0:Q, 0:items], end[:, k:k + 1],
                                                       spread[:, k, 0:items], ALU.is_lt, ALU.mult)
                    ins.then_inc(s_spread, 1)
                    dve.wait_ge(s_items, n + 1)
                    step = items if items <= 512 else items // 2
                    whole = lambda v, m: v
                    for a in range(0, items, step):
                        cols = slice(a, a + step)
                        from_psum = {name: PS[:, m if step == items else 2 * m + a // step, 0:step] for m, name in enumerate(parts)}
                        for name in ("w", "t4"):
                            if name in from_psum and name in tab:
                                dve.tensor_copy(tab[name][:, cols], from_psum[name])
                        if "src" in tab:
                            dve.tensor_copy(tab["src"][:, cols], from_psum["src"])
                        ch.link(dve.tensor_copy(score_w[:, cols], from_psum["src"]))
                        ch.link(dve.tensor_tensor(tab["jf"][:, cols], iota_items[:, cols], from_psum["j"], ALU.add))
                        dve.tensor_single_scalar(tab["j"][:, cols], tab["jf"][:, cols], float(tiles - 1), ALU.min)
                        if "src8" in tab:
                            dve.scalar_tensor_tensor(tab["src8"][:, cols], score_w[:, cols], float(T8), from_psum["t8"], ALU.mult, ALU.add)
                        else:
                            dve.scalar_tensor_tensor(tab["src4"][:, cols], score_w[:, cols], float(R), from_psum["t4"], ALU.mult, ALU.add)
                        dve.tensor_copy(tab["dst"][:, cols], from_psum["dst"])
                        ch.link(dve.scalar_tensor_tensor(tab["rel"][:, cols], tab["jf"][:, cols], -float(2 ** shift), from_psum["dst"], ALU.mult, ALU.add))
                    rel, ok, dst = tab["rel"], tab["ok"], tab["dst"]
                    ch.link(dve.tensor_single_scalar(ok, rel, 0.0, ALU.is_ge))
                    ch.link(dve.scalar_tensor_tensor(ok, rel, float(2 ** shift), ok, ALU.is_lt, ALU.mult))
                    if "src4" in tab:
                        ch.link(dve.scalar_tensor_tensor(rel, tab["t4"], float(M2), rel, ALU.mult, ALU.add))
                    ch.link(dve.scalar_tensor_tensor(rel, rel, FAR, ok, ALU.add, ALU.mult))
                    ch.link(dve.tensor_single_scalar(rel, rel, -FAR, ALU.add))
                    ch.link(dve.scalar_tensor_tensor(dst, dst, 1.0, ok, ALU.add, ALU.mult))
                    dve.tensor_single_scalar(dst, dst, -1.0, ALU.add).then_inc(s_tabs, 1)

                spread_items(0, tab1, 7, NV, NI, ("src", "dst", "t8", "w", "j"))
                spread_items(1, tab2, 5, NV2, NI2, ("src", "dst", "t4", "j"))
                dve.sem_inc(s_acc, ACC0 - 1)
                dve.wait_ge(s_tabs, 2)
                dve.memset(acc0, 0.0).then_inc(s_acc, 1)

                def add_sums(first, before, slots, tab, it, b, width, target, nodes):
                    j = node_tiles(mybir.EngineType.DVE, tab, window(b, it, slots), nodes)
                    dve.wait_ge(s_scat[b], it + (past(b, *before) + 2))
                    for k in range(G):
                        a = target[:, bass.ds(j[k], 1), :].rearrange("p o d -> p (o d)")
                        dve.wait_ge(s_acc, it * (slots * G) + (first + b * G + k))
                        dve.tensor_tensor(a, a, sums_of(b, k, width), ALU.add).then_inc(s_acc, 1)

                def layer_norm(n, source, target):
                    with dve.Fori(0, NJ) as j:
                        dve.bn_stats(stats[:, bass.ds(j, 1), :].rearrange("p o d -> p (o d)"),
                                     source[:, bass.ds(j, 1), :].rearrange("p o d -> p (o d)"))
                    ch.link(dve.memset(col[5][:, :], 0.0))
                    me, ve, mo, vo = (stats[:, :, m] for m in (1, 2, 4, 5))
                    dve.tensor_tensor(col[2][:, :], me, mo, ALU.add)
                    dve.tensor_tensor(col[3][:, :], me, mo, ALU.subtract)
                    ch.link(dve.tensor_tensor(col[0][:, :], ve, vo, ALU.add))
                    ch.link(dve.tensor_tensor(col[3][:, :], col[3][:, :], col[3][:, :], ALU.mult))
                    dve.tensor_single_scalar(col[2][:, :], col[2][:, :], 0.5, ALU.mult)
                    ch.link(dve.tensor_scalar(col[3][:, :], col[3][:, :], 0.25, 1e-5, ALU.mult, ALU.add))
                    dve.scalar_tensor_tensor(col[0][:, :], col[0][:, :], 1.0 / D, col[3][:, :], ALU.mult, ALU.add).then_inc(s_var, 1)
                    ch.link(dve.tensor_tensor(target, source, col[2][:, :].unsqueeze(2).to_broadcast([P, NJ, D]), ALU.subtract))
                    dve.wait_ge(s_std, n + 1)
                    ch.link(dve.reciprocal(col[1][:, :], col[1][:, :]))
                    ch.link(dve.tensor_tensor(target, target, col[1][:, :].unsqueeze(2).to_broadcast([P, NJ, D]), ALU.mult))

                def build_onehots(free, slots, tab, it, b):
                    dve.wait_ge(*free)
                    dve.tensor_tensor(oneh[:, b, :, :], iota[:, 0:P].unsqueeze(1).to_broadcast([P, G, P]),
                                      tab["rel"][:, bass.ds(window(b, it, slots), G)].unsqueeze(2).to_broadcast([P, G, P]),
                                      ALU.is_equal).then_inc(s_oh[b], 1)

                with dve.Fori(0, IT) as it:
                    for b in range(SL):
                        dve.wait_ge(s_scat[b], it + 1)
                        for k in range(G):
                            i = window(b, it) + k
                            ins = dve.tensor_scalar(oneh[:, b, k, :], iota[:, 0:P], tab1["rel"][:, bass.ds(i, 1)],
                                                    tab1["w"][:, bass.ds(i, 1)], ALU.is_equal, ALU.mult)
                        ins.then_inc(s_oh[b], 1)
                    for b in range(SL):
                        add_sums(ACC0, (), SL, tab1, it, b, D, acc0, NV)
                dve.wait_ge(s_acc, ACC0 + NI)
                dve.wait_ge(s_w, 96)
                ch.link(dve.tensor_tensor(bias0[:, 0, :], bias0[:, 0, :], bias0[:, 1, :], ALU.add))

                with dve.Fori(0, NJ // 2) as it:
                    ch.begin(it, 2)
                    for b in range(2):
                        j = it * 2 + b
                        xj = X[:, bass.ds(j, 1), :].rearrange("p o d -> p (o d)")
                        lj = acc0[:, bass.ds(j, 1), :].rearrange("p o d -> p (o d)")
                        dve.wait_ge(s_turned[b], it + 1)
                        dve.tensor_tensor(stg[:, b, 0, :], xj, lj, ALU.add)
                        dve.tensor_tensor(stg[:, b, 1, :], xj, lj, ALU.mult).then_inc(s_staged[b], 1)
                    for b in range(2):
                        j = it * 2 + b
                        yj = Y[:, bass.ds(j, 1), :].rearrange("p o d -> p (o d)")
                        dve.wait_ge(s_prod[b], it + 2)
                        ch.link(dve.tensor_tensor(yj, PS[:, 6 + b, 0:D], bias0[:, 0, :], ALU.add))
                        dve.scalar_tensor_tensor(yj, yj, 0.2, yj, ALU.mult, ALU.max).then_inc(s_take[b], 1)
                    ch.end(NJ // 2)
                dve.wait_ge(s_take[0], 1 + NJ // 2)
                dve.wait_ge(s_take[1], 1 + NJ // 2)
                dve.sem_inc(s_arg, 1)
                dve.wait_ge(s_val, 1)
                ch.link(dve.tensor_reduce(col[0][:, :], big, AX.X, ALU.add))
                dve.tensor_single_scalar(col[0][:, :], col[0][:, :], 1e-24, ALU.max).then_inc(s_var, 1)
                dve.wait_ge(s_std, 1)
                ch.link(dve.reciprocal(col[1][:, :], col[1][:, :]))
                ch.link(dve.tensor_tensor(Y[:, :, :], Y[:, :, :], col[1][:, :].unsqueeze(2).to_broadcast([P, NJ, D]), ALU.mult))
                ch.link(dve.tensor_tensor(Y[:, :, :], Y[:, :, :], X[:, :, :], ALU.add))
                layer_norm(1, Y[:, :, :], X[:, :, :])
                if layers > 1:
                    everyone = lambda v: v.unsqueeze(1).to_broadcast([P, NJ, D])
                    dve.wait_ge(s_w1, 12 * 16)

                    def scale_shift(target, gain, shift):
                        ch.link(dve.tensor_tensor(target, target, everyone(gain), ALU.mult))
                        ch.link(dve.tensor_tensor(target, target, everyone(shift), ALU.add))

                    for n in range(2):
                        dve.tensor_tensor(scaled_w[:, n, :], WX[:, 0:D], att[:, n, :], ALU.mult)
                    ch.link(dve.memset(before_row[:, :], -BIG))
                    for n in range(2):
                        dve.tensor_reduce(WX[:, D + n * H:D + (n + 1) * H], scaled_w[:, n, :].rearrange("p (h c) -> p h c", c=C), AX.X, ALU.add)
                    ch.link(dve.memset(after_row[:, :], -BIG))

                    def segment_starts(n, S):
                        Qn, W = S["n"], S["width"]
                        key, reset, rdst = S["key"], S["reset"], S["dst"]
                        ch.link(dve.memset(ends[:, :], 0.0))
                        dve.tensor_reduce(ends[0:Qn, 0:1], rdst, AX.X, ALU.max).then_inc(s_ends, 1)
                        dve.wait_ge(s_endsT, 4 * n + 1)
                        ch.link(dve.tensor_copy(resets_row[:, 0:Qn], PS[0:4, 4, 0:Qn]))
                        dve.tensor_tensor_scan(before_row[:, 1:Qn + 1], resets_row[:, 0:Qn], resets_row[:, 0:Qn], -1.0, ALU.max, ALU.max).then_inc(s_scan, 1)
                        dve.wait_ge(s_scanT, 3 * n + 1)
                        ch.link(dve.tensor_single_scalar(key[:, 0:1], PS[0:Qn, 4, 256:257], -1.0, ALU.max))
                        ch.link(dve.tensor_tensor_scan(key[:, 1:W + 1], rdst, rdst, key[:, 0:1], ALU.max, ALU.max))
                        ch.link(dve.tensor_tensor(reset[:, 0:W], rdst, key[:, 0:W], ALU.is_gt))
                        dve.memset(reset[:, W:W + 1], 0.0)
                        ch.link(dve.tensor_single_scalar(reset[:, 0:W], reset[:, 0:W], -BIG, ALU.mult))
                        for m in range(4):
                            ins = dve.tensor_reduce(ends[0:Qn, m:m + 1], reset[:, 0:W], AX.X, ALU.add)
                        ins.then_inc(s_ends, 1)
                        dve.wait_ge(s_endsT, 4 * n + 2)
                        ch.link(dve.tensor_copy(resets_row[:, 0:Qn], PS[0:4, 4, 0:Qn]))

                    dve.sem_inc(s_torow, 1)
                    dve.wait_ge(s_inrow, 1)
                    dve.tensor_scalar(S1["aux"], PS[0:Q1, 1, :], BIG, -BIG, ALU.mult, ALU.add)
                    ch.link(dve.tensor_copy(S1["dst"], PS[0:Q1, 0, :]))
                    segment_starts(0, S1)

                    def segment_max(n, S, starts_too):
                        Qn, W = S["n"], S["width"]
                        reset, rv, rf, rg, scratch = S["reset"], S["rv"], S["rf"], S["g"], S["scratch"]
                        for h in range(H):
                            ch.link(dve.tensor_tensor_scan(scratch, reset[:, 0:W], rv[h], -BIG, ALU.add, ALU.max))
                            ch.link(dve.tensor_copy(ends[0:Qn, h:h + 1], scratch[:, W - 1:W]))
                        dve.sem_inc(s_ends, 1)
                        dve.wait_ge(s_endsT, 4 * n + 3)
                        dve.tensor_tensor_scan(before_row[:, 1:Qn + 1], resets_row[:, 0:Qn], PS[0:4, 4, 0:Qn], -BIG, ALU.add, ALU.max).then_inc(s_scan, 1)
                        dve.wait_ge(s_scanT, 3 * n + 2)
                        ch.link(dve.tensor_copy(carry[0:Qn, :], PS[0:Qn, 4, 256:260]))
                        for h in range(H):
                            ins = dve.tensor_tensor_scan(rf[h], reset[:, 0:W], rv[h], carry[0:Qn, h:h + 1], ALU.add, ALU.max)
                        ch.link(ins)
                        for h in range(H):
                            ch.link(dve.tensor_tensor_scan(scratch[:, ::-1], reset[:, 1:W + 1][:, ::-1], rf[h][:, ::-1], -BIG, ALU.add, ALU.max))
                            ch.link(dve.tensor_tensor(ends[0:Qn, h:h + 1], scratch[:, 0:1], reset[:, 0:1], ALU.add))
                        ch.link(dve.memset(after_row[:, Qn:Qn + 1], -BIG))
                        dve.sem_inc(s_ends, 1)
                        dve.wait_ge(s_endsT, 4 * n + 4)
                        dve.tensor_tensor_scan(after_row[:, 0:Qn][:, ::-1], resets_row[:, 0:Qn][:, ::-1], PS[0:4, 4, 0:Qn][:, ::-1], -BIG, ALU.add, ALU.max).then_inc(s_scan, 1)
                        dve.wait_ge(s_scanT, 3 * n + 3)
                        ch.link(dve.tensor_copy(carry[0:Qn, :], PS[0:Qn, 4, 256:260]))
                        for h in range(H):
                            ch.link(dve.tensor_tensor_scan(rg[:, ::-1], reset[:, 1:W + 1][:, ::-1], rf[h][:, ::-1], carry[0:Qn, h:h + 1], ALU.add, ALU.max))
                            dve.scalar_tensor_tensor(rv[h], rg, -0.1 * BIG, rv[h], ALU.max, ALU.subtract).then_inc(s_exin, 1)
                            dve.wait_ge(s_exin, n * H + h + 1)
                            if starts_too:
                                ch.link(dve.scalar_tensor_tensor(rf[h], reset[:, 0:W], 0.0, rg, ALU.is_lt, ALU.mult))

                    layer_norm(2, X[:, :, :], Y[:, :, :])
                    scale_shift(Y[:, :, :], rowv["ln1_g"][:, :], rowv["ln1_b"])
                    dve.sem_inc(s_ready, 1)
                    with dve.Fori(0, NJ // 2) as it:
                        for b in range(2):
                            dve.wait_ge(s_prod[b], it + 15)
                            dve.tensor_copy(ad[:, bass.ds(it * 2 + b, 1), :].rearrange("p o h -> p (o h)"), PS[:, 6 + b, W1C:W1C + H])
                            dve.tensor_copy(xh[:, bass.ds(it * 2 + b, 1), :].rearrange("p o d -> p (o d)"), PS[:, 6 + b, 0:W1C]).then_inc(s_take[b], 1)
                    with dve.Fori(0, IT) as it:
                        for b in range(SL):
                            build_onehots((s_ohturn[b], it + 1), SL, tab1, it, b)
                        for b in range(SL):
                            dve.wait_ge(s_spread1[b], it + 2)
                            dve.wait_ge(s_rows[b], it * (16 * G) + (IT + 1) * 16 * G)
                            dve.tensor_tensor(score[:, bass.ds(window(b, it), G), :],
                                              PS[:, SL + b, 0:G * H].rearrange("p (g h) -> p g h", g=G),
                                              ring[:, b, :, D:W1C], ALU.add).then_inc(s_scored[b], 1)
                    for b in range(SL):
                        dve.wait_ge(s_scored[b], 1 + IT)
                    dve.memset(acc1, 0.0)
                    dve.scalar_tensor_tensor(score[:, :, :], score[:, :, :], 0.2, score[:, :, :], ALU.mult, ALU.max).then_inc(s_torow, 1)
                    dve.wait_ge(s_inrow, 2)
                    for h in range(H):
                        ins = dve.tensor_tensor(S1["rv"][h], PS[0:Q1, h, :], S1["aux"], ALU.add)
                    ch.link(ins)
                    segment_max(0, S1, True)
                    dve.sem_inc(s_max, 1)
                    for h in range(H):
                        dve.wait_ge(s_exT, h + 1)
                        dve.tensor_copy(weight[:, :, h].rearrange("p (q k) -> p k q", k=K1),
                                        PS[:, h, 0:NI].rearrange("p (k q) -> p k q", k=K1))
                    dve.wait_ge(s_maxT, 1)
                    for h in range(H):
                        ins = dve.tensor_copy(score[:, :, h].rearrange("p (q k) -> p k q", k=K1),
                                              PS[:, 4 + h, 0:NI].rearrange("p (k q) -> p k q", k=K1))
                    ins.then_inc(s_w8, 1)
                    dve.wait_ge(s_w8, 1)
                    with dve.Fori(0, IT) as it:
                        for b in range(SL):
                            build_onehots((s_scat[b], it + (past(b, "A0") + 1)), SL, tab1, it, b)
                        for b in range(SL):
                            add_sums(ACC0 + NI, ("A0",), SL, tab1, it, b, W1C + H, acc1, NV)
                    dve.wait_ge(s_acc, ACC0 + 2 * NI)
                    sums, peak = acc1[:, :, D:W1C], acc1[:, :, W1C:W1C + H]
                    edge_exp, own_exp, top = (own[:, n, :, :] for n in range(3))
                    ch.link(dve.tensor_tensor(own_exp, xh[:, :, D:W1C], ad[:, :, :], ALU.add))
                    ch.link(dve.scalar_tensor_tensor(own_exp, own_exp, 0.2, own_exp, ALU.mult, ALU.max))
                    ch.link(dve.tensor_scalar(edge_exp, sums, 0.5, -BIG, ALU.is_lt, ALU.mult))
                    ch.link(dve.tensor_tensor(edge_exp, edge_exp, peak, ALU.add))
                    ch.link(dve.tensor_tensor(top, edge_exp, own_exp, ALU.max))
                    dve.tensor_tensor(edge_exp, top, edge_exp, ALU.subtract)
                    dve.tensor_tensor(own_exp, top, own_exp, ALU.subtract).then_inc(s_arg, 1)
                    dve.wait_ge(s_val, 2)
                    ch.link(dve.tensor_tensor(top, sums, edge_exp, ALU.mult))
                    ch.link(dve.tensor_tensor(top, top, own_exp, ALU.add))
                    ch.link(dve.reciprocal(top, top))
                    dve.tensor_tensor(edge_exp, edge_exp, top, ALU.mult)
                    ch.link(dve.tensor_tensor(own_exp, own_exp, top, ALU.mult))
                    for h in range(H):
                        part = slice(h * C, (h + 1) * C)
                        dve.tensor_tensor(Y[:, :, part], acc1[:, :, part], edge_exp[:, :, h:h + 1].to_broadcast([P, NJ, C]), ALU.mult)
                        ins = dve.tensor_tensor(xh[:, :, part], xh[:, :, part], own_exp[:, :, h:h + 1].to_broadcast([P, NJ, C]), ALU.mult)
                    ch.link(ins)
                    ch.link(dve.tensor_tensor(Y[:, :, :], Y[:, :, :], xh[:, :, 0:D], ALU.add))
                    ch.link(dve.tensor_tensor(Y[:, :, :], Y[:, :, :], everyone(rowv["gat_b"]), ALU.add))
                    ch.link(dve.tensor_tensor(Y[:, :, :], Y[:, :, :], X[:, :, :], ALU.add))
                    layer_norm(3, Y[:, :, :], big)
                    scale_shift(big, rowv["ln2_g"][:, :], rowv["ln2_b"])
                    dve.sem_inc(s_ready, 1)
                    with dve.Fori(0, NJ // 2) as it:
                        for b in range(2):
                            yj = Y[:, bass.ds(it * 2 + b, 1), :].rearrange("p o d -> p (o d)")
                            dve.wait_ge(s_prod2[b], it + 2)
                            dve.tensor_tensor(yj, yj, PS[:, 2 + b, 0:D], ALU.add).then_inc(s_take[b], 1)
                    dve.wait_ge(s_take[0], 1 + 3 * (NJ // 2))
                    dve.wait_ge(s_take[1], 1 + 3 * (NJ // 2))
                    ch.link(dve.tensor_tensor(Y[:, :, :], Y[:, :, :], everyone(rowv["b2"]), ALU.add))
                    ch.link(dve.tensor_tensor(Y[:, :, :], Y[:, :, :], X[:, :, :], ALU.add))
                    layer_norm(4, Y[:, :, :], X[:, :, :])
                if layers > 2:
                    dve.wait_ge(s_w2, 15 * 16)
                    for n in range(2):
                        for r in range(R):
                            ch.link(dve.tensor_tensor(stg[:, 0, 1, :], WQK[:, (n * R + r) * D:(n * R + r + 1) * D], attq[:, n, :], ALU.mult))
                            dve.tensor_tensor(c4q[:, n, r * D:(r + 1) * D], c4q[:, n, r * D:(r + 1) * D], attq[:, n, :], ALU.mult)
                            ch.link(dve.tensor_reduce(u4[:, n, r:r + 1], stg[:, 0, 1, :], AX.X, ALU.add))
                        ch.link(dve.tensor_reduce(c4[:, n, :], c4q[:, n, :].rearrange("p (r d) -> p r d", d=D), AX.X, ALU.add))
                    dve.tensor_tensor(u4[:, 0, :], u4[:, 0, :], u4[:, 1, :], ALU.add)
                    ch.link(dve.tensor_tensor(c4[:, 0, :], c4[:, 0, :], c4[:, 1, :], ALU.add))
                    ch.link(dve.tensor_scalar(c4[:, 0, :], c4[:, 0, :], a_b[:, 0:1], None, ALU.add))
                    dve.sem_inc(s_ready, 1)
                    with dve.Fori(0, NJ // 2) as it:
                        for b in range(2):
                            dve.wait_ge(s_prod[b], it + 41)
                            dve.wait_ge(s_tfree[b], it + (NJ // 2 + 1))
                            dve.tensor_copy(trow[:, b, 0:R * D], PS[:, 6 + b, :])
                            dve.tensor_tensor(trow[:, b, R * D:2 * R * D], PS[:, 2 + b, :], bR, ALU.add).then_inc(s_take[b], 1)
                    for b in range(2):
                        dve.wait_ge(s_take[b], 53)
                    dve.sem_inc(s_torow, 1)
                    dve.wait_ge(s_inrow, 3)
                    fold = lambda m: PS[0:Q2, 2 * m:2 * m + 2, :].rearrange("q n f -> q (n f)")[:, 0:K2 * P]
                    dve.tensor_copy(S2["aux"], fold(2))
                    ch.link(dve.tensor_copy(S2["dst"], fold(0)))
                    ch.link(dve.tensor_copy(S2["g"], fold(1)))
                    segment_starts(1, S2)
                    ch.link(dve.tensor_copy(rok2, S2["g"]))
                    with dve.Fori(0, IT2) as it:
                        for b in range(SL2):
                            build_onehots((s_ohturn[b], it + (past(b, "A1") + 1)), SL2, tab2, it, b)
                        for b in range(SL2):
                            dve.wait_ge(s_spread1[b], it + (past(b, "A1") + 2))
                            dve.wait_ge(s_rows[b], it * (16 * G) + (past(b, "A0", "A1") + 1) * 16 * G)
                            dve.wait_ge(s_spill[b], it * 16 + (past(b, "A1") + 1) * 16)
                            dve.tensor_tensor(ring2[:, b, :, 0:D], four(2 * b + 1),
                                              ring[:, b, :, 0:D], ALU.add).then_inc(s_added[b], 1)
                        for b in range(SL2):
                            dve.wait_ge(s_added[b], it + 2)
                            dve.scalar_tensor_tensor(ring2[:, b, :, 0:D], ring2[:, b, :, 0:D], 0.2, ring2[:, b, :, 0:D],
                                                     ALU.mult, ALU.max).then_inc(s_relu[b], 1)
                        for b in range(SL2):
                            dve.wait_ge(s_s4[b], it + 1)
                            dve.tensor_copy(score2[:, bass.ds(window(b, it, SL2), G), :],
                                            PS[:, 2 * b, 0:G * R].rearrange("p (g r) -> p g r", g=G)).then_inc(s_scored[b], 1)
                    for b in range(SL2):
                        dve.wait_ge(s_scored[b], 1 + past(b, "A1", "A2"))
                    dve.memset(wide_flat, 0.0)
                    ch.link(dve.tensor_tensor(score2, score2, c4[:, 0, :].unsqueeze(1).to_broadcast([P, NI2, R]), ALU.add))
                    dve.scalar_tensor_tensor(score2, score2, 0.2, score2, ALU.mult, ALU.max).then_inc(s_torow, 1)
                    dve.wait_ge(s_inrow, 4)
                    for r in range(R):
                        ch.link(dve.scalar_tensor_tensor(S2["scratch"], S2["aux"], float(r), rok2, ALU.is_equal, ALU.mult))
                        ch.link(dve.tensor_scalar(S2["scratch"], S2["scratch"], BIG, -BIG, ALU.mult, ALU.add))
                        ch.link(dve.tensor_tensor(S2["rv"][r], fold(r), S2["scratch"], ALU.add))
                    segment_max(1, S2, False)
                    dve.wait_ge(s_ex, 2 * H)
                    rv = S2["rv"]
                    dve.tensor_tensor(rv[2], rv[2], rv[3], ALU.add)
                    ch.link(dve.tensor_tensor(rv[0], rv[0], rv[1], ALU.add))
                    dve.tensor_tensor(rv[0], rv[0], rv[2], ALU.add).then_inc(s_max, 1)
                    dve.wait_ge(s_maxT, 2)
                    by_row = weight2[:, 0:Q2 * K2].rearrange("p (q k) -> p k q", k=K2)
                    dve.memset(weight2[:, Q2 * K2:NI2], 0.0)
                    dve.tensor_copy(by_row[:, 0:4, :], PS[:, 0, 0:4 * Q2].rearrange("p (k q) -> p k q", k=4))
                    dve.tensor_copy(by_row[:, 4, :], PS[:, 1, 0:Q2]).then_inc(s_w8, 1)
                    with dve.Fori(0, IT2) as it:
                        for b in range(SL2):
                            build_onehots((s_scat[b], it + (past(b, "A0", "B1") + 1)), SL2, tab2, it, b)
                        for b in range(SL2):
                            add_sums(ACC0 + 2 * NI, ("A0", "B1"), SL2, tab2, it, b, D + 1, acc2, NV2)
                    dve.wait_ge(s_acc, ACC0 + 2 * NI + NI2)
                    ch.link(dve.memset(den2[:, :, :], 0.0))
                    rden, flag = den2[:, 0, 0:NV2], den2[:, 1, 0:NV2]
                    ch.link(dve.tensor_single_scalar(rden, acc2[:, :, D], 1e-16, ALU.max))
                    ch.link(dve.reciprocal(rden, rden))
                    ch.link(dve.tensor_tensor(flag, rden, acc2[:, :, D], ALU.mult))
                    with dve.Fori(0, NJ // 2) as it:
                        for b in range(2):
                            u = (it * 2 + b) * 4
                            dve.wait_ge(s_turned[b], it + 53)
                            dve.wait_ge(s_prod[b], it + 53)
                            dve.tensor_tensor(stg[:, b, R, :].rearrange("p (u m) -> p u m", m=M2), pick[:, :].unsqueeze(1).to_broadcast([P, 4, M2]),
                                              den2[:, 1, bass.ds(u, 4)].unsqueeze(2).to_broadcast([P, 4, M2]), ALU.mult)
                            dve.tensor_tensor(stg[:, b, 0:4, :], wide_flat[:, bass.ds(u * (D + 1), 4 * (D + 1))].rearrange("p (u d) -> p u d", d=D + 1)[:, :, 0:D],
                                              den2[:, 0, bass.ds(u, 4)].unsqueeze(2).to_broadcast([P, 4, D]), ALU.mult).then_inc(s_staged[b], 1)
                        for b in range(2):
                            dve.wait_ge(s_prod[b], it + 54)
                            dve.tensor_copy(Y[:, bass.ds(it * 2 + b, 1), :].rearrange("p o d -> p (o d)"), PS[:, 6 + b, 0:D]).then_inc(s_take[b], 1)
                    for b in range(2):
                        dve.wait_ge(s_take[b], 66)
                    dve.tensor_single_scalar(big, Y[:, :, :], 0.0, ALU.min).then_inc(s_arg, 1)
                    ch.link(dve.scalar_tensor_tensor(Y[:, :, :], Y[:, :, :], 0.0, X[:, :, :], ALU.max, ALU.add))
                    dve.wait_ge(s_val, 3)
                    ch.link(dve.scalar_tensor_tensor(Y[:, :, :], big, -1.0, Y[:, :, :], ALU.add, ALU.add))
                    layer_norm(5, Y[:, :, :], X[:, :, :])
                if layers > 3:
                    dve.memset(Y[:, :, :], 0.0)
                    dve.wait_ge(s_w3, 7 * 16)
                    ch.link(dve.tensor_tensor(gru_b[:, 0:2 * D], gru_b[:, 0:2 * D], gru_b2[:, :], ALU.add))
                    dve.sem_inc(s_ready, 1)
                    with dve.Fori(0, NJ // 2) as it:
                        for b in range(2):
                            dve.wait_ge(s_prod[b], it + 67)
                            dve.wait_ge(s_tfree[b], it + (NJ + 1))
                            dve.tensor_tensor(trow[:, b, 0:4 * D], PS[:, 6 + b, :], b3[:, 0:4 * D], ALU.add)
                            dve.tensor_tensor(trow[:, b, 4 * D:8 * D], PS[:, 2 + b, :], b3[:, 4 * D:8 * D], ALU.add).then_inc(s_take[b], 1)
                    with dve.Fori(0, IT) as it:
                        for b in range(SL):
                            build_onehots((s_scat[b], it + (past(b, "A0", "B1", "B2") + 1)), SL, tab1, it, b)
                        for b in range(SL):
                            add_sums(ACC0 + 2 * NI + NI2, ("A0", "B1", "B2"), SL, tab1, it, b, D, Y, NV)
                    dve.wait_ge(s_acc, ACC0 + 3 * NI + NI2)
                    dve.sem_inc(s_ready, 1)
                    with dve.Fori(0, NJ // 2) as it:
                        for b in range(2):
                            dve.wait_ge(s_prod[b], it + 80)
                            dve.tensor_tensor(wide[:, bass.ds(it * 2 + b, 1), 0:4 * D].rearrange("p o d -> p (o d)"), PS[:, 6 + b, :], gru_b[:, :], ALU.add).then_inc(s_take[b], 1)
                    for b in range(2):
                        dve.wait_ge(s_take[b], 92)
                    dve.sem_inc(s_arg, 1)
                    dve.wait_ge(s_val, 4)
                    rg3, z, n_in, h_n = (wide[:, :, a * D:(a + 1) * D] for a in range(4))
                    ch.link(dve.tensor_tensor(h_n, h_n, rg3, ALU.mult))
                    dve.tensor_tensor(n_in, n_in, h_n, ALU.add).then_inc(s_arg, 1)
                    dve.wait_ge(s_val, 5)
                    ch.link(dve.tensor_tensor(Y[:, :, :], X[:, :, :], n_in, ALU.subtract))
                    ch.link(dve.tensor_tensor(Y[:, :, :], Y[:, :, :], z, ALU.mult))
                    ch.link(dve.tensor_tensor(Y[:, :, :], Y[:, :, :], n_in, ALU.add))
                    ch.link(dve.tensor_tensor(Y[:, :, :], Y[:, :, :], X[:, :, :], ALU.add))
                    layer_norm(6, Y[:, :, :], X[:, :, :])
                dve.sem_inc(s_final, 1)


_OUTS = [((3125, 128), "float32")]


def kernel(**inputs):
    import numpy as _np
    import concourse.bacc as _bacc
    from concourse import mybir as _mybir
    from concourse.bass_utils import run_bass_kernel_spmd as _run

    nc = _bacc.Bacc("TRN2", target_bir_lowering=False, num_devices=1)
    arrays, args = {}, {}
    for name in inputs:
        a = _np.ascontiguousarray(inputs[name])
        arrays[f"in_{name}_dram"] = a
        args[name] = nc.dram_tensor(f"in_{name}_dram", a.shape, _mybir.dt.from_np(a.dtype), kind="ExternalInput").ap()
    shape, dtype = _OUTS[0]
    out = nc.dram_tensor("out_0_dram", shape, _mybir.dt.from_np(_np.dtype(dtype)), kind="ExternalOutput").ap()
    gnn_stack(nc, args, out)
    r = _run(nc, [arrays], core_ids=[0])
    return r.results[0]["out_0_dram"]
```

```python
import concourse.bass as bass
from concourse import mybir
from contextlib import ExitStack


class Chain:

    def __init__(self, engine, sem):
        self.engine, self.sem, self.done, self.turn, self.per = engine, sem, 0, None, 0

    def begin(self, turn, per):
        self.turn, self.per, self.first = turn, per, self.done

    def end(self, turns):
        assert self.done - self.first == self.per, (self.done - self.first, self.per)
        self.done, self.turn = self.first + turns * self.per, None

    def link(self, ins):
        ins.then_inc(self.sem, 1)
        self.done += 1
        self.engine.wait_ge(self.sem, self.done if self.turn is None else self.turn * self.per + self.done)


def gnn_stack(nc, t, out):
    f32, i32 = mybir.dt.float32, mybir.dt.int32
    ALU, ACT, AX = mybir.AluOpType, mybir.ActivationFunctionType, mybir.AxisListType

    P = 128
    N, D = t["x"].shape
    E = t["src"].shape[0]
    NJ = 26
    NV = -(-N // P)
    LASTN = N - (NV - 1) * P
    Q = -(-E // 512)
    LASTE = E - (Q - 1) * 512
    G = 4
    M2 = P // 4
    NV2 = -(-N // M2)
    SL = 4
    K1, NI = 4, 448
    K2, NI2 = 5, 528
    Q1, Q2 = NI // K1, 104
    assert NI >= 4 * Q + NV - 1 and NI % (SL * G) == 0 and NI == Q1 * K1 and Q1 <= P
    assert NI2 >= Q2 * K2 >= 4 * Q + NV2 - 1 and NI2 % (SL * G) == 0 and Q2 <= P
    turns = {"A0": NI // (SL * G), "A1": NI // (SL * G), "B1": NI // (SL * G),
             "A2": NI2 // (SL * G), "B2": NI2 // (SL * G), "A3": NI // (SL * G)}
    IT, IT2 = turns["A0"], turns["A2"]
    H, C = t["L1_gnn_att_src"].shape
    R = t["L2_gnn_W_R"].shape[0]
    T8 = t["L3_gnn_message_W"].shape[0]
    W1C = D + H
    BIG = 1e30
    FAR = 1e4
    ACC0 = SL * G + 1

    NODE0, TABLE1, FFN, TABLE2, NODE2, TABLE3, GRU = (n * (NJ // 2) for n in range(7))

    def past(*passes):
        return sum(turns[p] for p in passes)

    def idle_at_last(p, b):
        return b * G >= 4 * Q + (NV2 if p == "A2" else NV) - 1 - (turns[p] - 1) * SL * G

    dram = lambda name, shape: nc.dram_tensor(name, shape, f32, kind="Internal").ap()
    table1 = dram("table1", [NJ * P, W1C])
    spill1 = dram("spill1", [NI // G, P, G * W1C])
    table2 = dram("table2", [NJ * P * R, D])
    tableB = dram("tableB", [NJ * P, R * D])
    spill2 = dram("spill2", [NI2 // G, P, G * (D + 1)])
    table3 = dram("table3", [NJ * P * T8, D])

    with ExitStack() as ctx:
        sb = lambda name, shape, dt=f32: ctx.enter_context(nc.sbuf_tensor(name, shape, dt))
        sem = lambda name: ctx.enter_context(nc.semaphore(name))

        X = sb("X", [P, NJ, D])
        Y = sb("Y", [P, NJ, D])
        wide = sb("wide", [P, NJ, R * (D + 1)])
        wide_flat = wide[:, :, :].rearrange("p j f -> p (j f)")
        big = wide[:, :, 256:256 + D]
        acc0 = wide[:, :, 0:D]
        acc1, acc1b = (wide[:, :, n * (W1C + H):(n + 1) * (W1C + H)] for n in range(2))
        xh = wide[:, :, 384:384 + W1C]
        Btab = wide_flat[:, 0:NV2 * D].rearrange("p (u d) -> p u d", d=D)
        acc2 = wide_flat[:, 0:NV2 * (D + 1)].rearrange("p (u d) -> p u d", d=D + 1)
        own = sb("own", [P, 3, NJ, H])
        relTs = Y[:, 0:SL * G, :].rearrange("p (b g) d -> p b g d", g=G)
        ad = sb("ad", [P, NJ, H])
        stats = sb("stats", [P, NJ, 6])
        col = [sb(f"col{n}", [P, NJ]) for n in range(6)]
        den2 = sb("den2", [P, 2, 4 * NJ])

        ROW = max(K1, K2) * P
        region = sb("region", [P, 14 * ROW + 2])
        cells = lambda n, rows, width=ROW: region[0:rows, n * ROW:n * ROW + width]
        ints = {n: cells(m, Q, 512).bitcast(i32) for m, n in enumerate(("src", "dst", "t4", "t8"))}
        rows = {n: cells(4 + m, Q, 512) for m, n in enumerate(("src", "dst", "t4", "t8", "w", "j"))}
        tile_i = sb("tile_i", [Q, 8], i32)
        tile_f = sb("tile_f", [Q, 8, 4])
        spread = wide_flat[0:Q, 0:4 * NI2].rearrange("q (k i) -> q k i", k=4)
        iota = sb("iota", [P, 512])
        iota_items = wide_flat[:, 4 * NI2:5 * NI2]
        ident = sb("ident", [P, P])
        upper = sb("upper", [P, P])
        pick = sb("pick", [P, M2])
        item_i = sb("item_i", [P, 3, NI], i32)
        item_f = sb("item_f", [P, 5, NI])
        tab1 = {"j": item_i[:, 0, :], "src": item_i[:, 1, :], "src8": item_i[:, 2, :],
                "rel": item_f[:, 0, :], "w": item_f[:, 1, :], "dst": item_f[:, 2, :], "ok": item_f[:, 3, :], "jf": item_f[:, 4, :]}
        item_i2 = sb("item_i2", [P, 2, NI2], i32)
        item_f2 = sb("item_f2", [P, 4, NI2])
        tab2 = {"j": item_i2[:, 0, :], "src4": item_i2[:, 1, :],
                "rel": item_f2[:, 0, :], "ok": item_f2[:, 1, :], "dst": item_f2[:, 2, :], "t4": item_f2[:, 3, :],
                "jf": wide_flat[:, 5 * NI2:6 * NI2]}
        score_w = sb("score_w", [P, NI2 * H])
        score = score_w[:, 0:NI * H].rearrange("p (i h) -> p i h", h=H)
        score2 = score_w[:, :].rearrange("p (i h) -> p i h", h=R)
        weight = region[:, 8 * ROW:8 * ROW + NI * H].rearrange("p (i h) -> p i h", h=H)
        weight2 = region[:, 8 * ROW:8 * ROW + NI2]
        ends = sb("ends", [P, 4])
        resets_row = sb("resets_row", [4, P])
        before_row = sb("before_row", [4, P])
        after_row = sb("after_row", [4, P])
        carry = sb("carry", [P, 4])

        def scan_rows(rows_, width):
            c = lambda n: cells(n, rows_, width)
            return {"n": rows_, "width": width, "rv": [c(n) for n in range(4)], "rf": [c(4 + n) for n in range(4)],
                    "g": c(8), "scratch": c(9), "dst": c(10), "aux": c(11),
                    "reset": region[0:rows_, 12 * ROW:12 * ROW + width + 1],
                    "key": region[0:rows_, 13 * ROW + 1:13 * ROW + 2 + width]}
        S1, S2 = scan_rows(Q1, K1 * P), scan_rows(Q2, K2 * P)
        rok2 = S2["dst"]

        ix = sb("ix", [P, SL, G], i32)
        ring = sb("ring", [P, SL, G, W1C + H])
        ring2 = sb("ring2", [P, SL, G, W1C + H])
        oneh = sb("oneh", [P, SL, G, P])
        onehT = sb("onehT", [P, SL, G, P])
        stg = sb("stg", [P, 2, R + 1, D])
        tT = sb("tT", [P, 2, R + 1, D])
        WV = sb("WV", [P, R, D])
        W0, bias0 = WV[:, 0:2, :], WV[:, 2:4, :]
        WX = sb("WX", [P, D + 2 * H])
        r2f, late = ring2[:, :, :, :].rearrange("p s g f -> p (s g f)"), region[:, 8 * ROW + NI * H:8 * ROW + NI * H + 8 * D]
        rowv = {n: r2f[:, m * D:(m + 1) * D] for m, n in enumerate(("ln1_g", "ln1_b"))}
        rowv2 = {n: late[:, m * D:(m + 1) * D] for m, n in enumerate(("gat_b", "ln2_g", "ln2_b", "b2"))}
        w1 = late[:, 4 * D:6 * D]
        w2 = late[:, 6 * D:8 * D].rearrange("p (n d) -> p n d", n=2)
        b1 = sb("b1", [P, 2])
        att = onehT[:, 0, :, :]
        scaled_w = onehT[:, 1, :, :]
        gelT = sb("gelT", [P, 2, 2, D])
        relT = lambda b: relTs[:, b, :, :]
        trow = wide_flat[:, 0:8 * R * D].rearrange("p (b f) -> p b f", b=4)
        bVx = sb("bVx", [P, D])
        attq = sb("attq", [P, 2, D])
        a_b = sb("a_b", [P, 1])
        ones_col = sb("ones_col", [P, 1])
        u4 = sb("u4", [P, 2, R])
        c4 = sb("c4", [P, 2, R])
        WRs, WRd = (region[:, n * R * D:(n + 1) * R * D].rearrange("p (r d) -> p r d", d=D) for n in range(2))
        bR = region[:, 2 * R * D:3 * R * D]
        WQK = region[:, 3 * R * D:5 * R * D]
        c4q = region[:, 5 * R * D:7 * R * D].rearrange("p (n f) -> p n f", n=2)
        W3 = region[:, 0:T8 * D].rearrange("p (t d) -> p t d", d=D)
        b3 = region[:, T8 * D:2 * T8 * D]
        gru_rows = region[:, 2 * T8 * D:(2 * T8 + 6) * D].rearrange("p (n d) -> p n d", d=D)
        gruT = region[:, (2 * T8 + 6) * D:(2 * T8 + 12) * D].rearrange("p (n d) -> p n d", n=2)
        gru_b = region[:, (2 * T8 + 12) * D:(2 * T8 + 16) * D]
        gru_b2 = region[:, (2 * T8 + 16) * D:(2 * T8 + 18) * D]

        PS = ctx.enter_context(nc.psum_tensor("PS", [P, 8, 512], f32))

        s_in = sem("edges_in")
        s_w = sem("weights_in")
        s_pad = sem("pads_set")
        s_const = sem("constants_made")
        s_pick = sem("pick_steps")
        s_const2 = sem("constants_shaped")
        s_chain = sem("vector_step")
        s_first = sem("tile_counts_summed")
        s_pre = sem("tile_prefix")
        s_spread = sem("spread_ready")
        s_items = sem("items_spread")
        s_tabs = sem("item_tables_ready")
        s_ix = [sem(f"indices_staged{b}") for b in range(SL)]
        s_rows = [sem(f"rows_gathered{b}") for b in range(SL)]
        s_oh = [sem(f"onehot_built{b}") for b in range(SL)]
        s_scat = [sem(f"rows_scattered{b}") for b in range(SL)]
        s_acc = sem("sums_added")
        s_staged = [sem(f"tile_staged{b}") for b in range(2)]
        s_turned = [sem(f"tile_turned{b}") for b in range(2)]
        s_tcopy = [sem(f"turned_copied{b}") for b in range(2)]
        s_prod = [sem(f"tile_product{b}") for b in range(2)]
        s_take = [sem(f"product_taken{b}") for b in range(2)]
        s_arg = sem("function_arguments_ready")
        s_val = sem("function_values_ready")
        s_var = sem("root_in")
        s_std = sem("root_out")
        s_out = sem("out_written")
        s_w1 = sem("layer1_weights_in")
        s_w1b = sem("layer1_late_weights_in")
        s_ready = sem("node_rows_ready")
        s_written = [sem(f"table_rows_written{b}") for b in range(2)]
        s_rowdone = [sem(f"row_buffer_written{n}") for n in range(4)]
        s_table = sem("table_complete")
        s_ohturn = [sem(f"onehot_turned{b}") for b in range(SL)]
        s_ohT = [sem(f"turned_onehot_copied{b}") for b in range(SL)]
        s_spread1 = [sem(f"dst_values_spread{b}") for b in range(SL)]
        s_scored = [sem(f"scores_stored{b}") for b in range(SL)]
        s_spill = [sem(f"rows_spilled{b}") for b in range(SL)]
        s_back = [sem(f"rows_back{b}") for b in range(SL)]
        s_scaled = [sem(f"rows_weighted{b}") for b in range(SL)]
        s_torow = sem("values_for_rows")
        s_inrow = sem("values_in_rows")
        s_ends = sem("row_ends")
        s_endsT = sem("row_ends_turned")
        s_scan = sem("rows_scanned")
        s_scanT = sem("row_carries")
        s_exin = sem("exponents")
        s_max = sem("maxima_at_starts")
        s_maxT = sem("maxima_turned")
        s_ohsq = [sem(f"onehot_squares{b}") for b in range(SL)]
        s_w8 = sem("weights_in_items")
        s_tail = [sem(f"row_tails_set{b}") for b in range(SL)]
        s_w2 = sem("layer2_weights_in")
        s_w3 = sem("layer3_weights_in")
        s_added = [sem(f"relation_sums{b}") for b in range(SL)]
        s_relu = [sem(f"relation_rows{b}") for b in range(SL)]
        s_relT = [sem(f"relation_rows_turned{b}") for b in range(SL)]
        s_relTc = [sem(f"turned_relation_rows_copied{b}") for b in range(SL)]
        s_s4 = [sem(f"relation_scores{b}") for b in range(SL)]
        s_Bback = sem("node_parts_back")
        s_gruT = sem("gru_weights_turned")
        s_ex = sem("exponentials")
        s_exT = sem("exponentials_turned")
        s_mid = [sem(f"gelu_done{b}") for b in range(2)]
        s_prod2 = [sem(f"second_product{b}") for b in range(2)]
        s_final = sem("x_final")

        def rows_due(p, b, it, last=False):
            passes = ("A0", "A1", "A2", "A3")
            before = sum(turns[q] - idle_at_last(q, b) for q in passes[:passes.index(p)])
            if last and idle_at_last(p, b):
                return s_ix[b], past(*passes[:passes.index(p) + 1])
            return s_rows[b], it * (16 * G) + (before + 1) * 16 * G

        def window(b, it):
            return it * (SL * G) + b * G

        def four(bank):
            return PS[:, bank, :].rearrange("p (g d) -> p g d", g=G)

        def sums_of(b, k, width):
            return PS[:, 2 * b + k // 2, (k % 2) * 256:(k % 2) * 256 + width]

        def node_tiles(engine, tab, first, count):
            return nc.values_load_multi_w_load_instructions(tab["j"][0:1, bass.ds(first, G)], engines=[engine],
                                                            min_val=0, max_val=count - 1,
                                                            skip_runtime_bounds_check_because="the table is clamped to the tiles when it is made")[1]

        with nc.Block() as block:

            @block.sync
            def _(sp):
                sp.wait_ge(s_pad, 1)
                for name, key in (("src", "src"), ("dst", "dst"), ("t4", "edge_type_4"), ("t8", "edge_type_8")):
                    a = t[key]
                    sp.dma_start(ints[name][0:Q - 1, :], a[0:(Q - 1) * 512].rearrange("(q e) -> q e", e=512)).then_inc(s_in, 16)
                    sp.dma_start(ints[name][Q - 1:Q, 0:LASTE], a[(Q - 1) * 512:E].rearrange("(q e) -> q e", q=1)).then_inc(s_in, 16)
                a = t["edge_weight"]
                sp.dma_start(rows["w"][0:Q - 1, :], a[0:(Q - 1) * 512].rearrange("(q e) -> q e", e=512)).then_inc(s_in, 16)
                sp.dma_start(rows["w"][Q - 1:Q, 0:LASTE], a[(Q - 1) * 512:E].rearrange("(q e) -> q e", q=1)).then_inc(s_in, 16)
                sp.dma_start(X[:, 0:NV - 1, :], t["x"][0:(NV - 1) * P, :].rearrange("(j p) d -> p j d", p=P)).then_inc(s_w, 16)
                sp.dma_start(X[0:LASTN, NV - 1, :], t["x"][(NV - 1) * P:N, :]).then_inc(s_w, 16)
                sp.dma_start(W0[:, 0, :], t["L0_gnn_W1"]).then_inc(s_w, 16)
                sp.dma_start(W0[:, 1, :], t["L0_gnn_W2"]).then_inc(s_w, 16)
                sp.dma_start(bias0[:, 0, :], t["L0_gnn_b1"][0, :].partition_broadcast(P)).then_inc(s_w, 16)
                sp.dma_start(bias0[:, 1, :], t["L0_gnn_b2"][0, :].partition_broadcast(P)).then_inc(s_w, 16)
                sp.dma_start(WX[:, 0:D], t["L1_gnn_W"]).then_inc(s_w1, 16)
                for n, name in enumerate(("L1_gnn_att_src", "L1_gnn_att_dst")):
                    sp.dma_start(att[:, n, :], t[name].rearrange("h c -> (h c)").partition_broadcast(P)).then_inc(s_w1, 16)
                for name, tile in rowv.items():
                    sp.dma_start(tile, t["L1_gnn_" + name].partition_broadcast(P)).then_inc(s_w1, 16)
                def write_table(base, wbase, tables):
                    with sp.Fori(0, NJ // 2) as it:
                        for b in range(2):
                            sp.wait_ge(s_take[b], it + (base + 2))
                            for table, row in tables(it, b):
                                sp.dma_start(table.rearrange("(j p) d -> j p d", p=P)[bass.ds(it * 2 + b, 1), :, :]
                                             .rearrange("o p d -> (o p) d"), row).then_inc(s_written[b], 16)
                    writes = len(tables(0, 0)) * (NJ // 2)
                    for b in range(2):
                        sp.wait_ge(s_written[b], (wbase + writes) * 16)
                    sp.sem_inc(s_table, 1)

                def write_rows(base, before, tables):
                    def rows_of(it, u, turn):
                        for b in range(2):
                            sp.wait_ge(s_take[b], turn + (base + 2))
                            for table, row in tables(2 * u + b):
                                sp.dma_start(table.rearrange("(j p) d -> j p d", p=P)[bass.ds(turn * 2 + b, 1), :, :]
                                             .rearrange("o p d -> (o p) d"), row).then_inc(s_rowdone[2 * u + b], 16)

                    with sp.Fori(0, NJ // 4) as it:
                        for u in range(2):
                            rows_of(it, u, it * 2 + u)
                    rows_of(NJ // 4, 0, NJ // 2 - 1)
                    for n in range(4):
                        sp.wait_ge(s_rowdone[n], (1 + before[n // 2] + len(tables(0)) * (NJ // 4 + 1 - n // 2)) * 16)
                    sp.sem_inc(s_table, 1)

                def spill(p, ready, ring_tile, width, store):
                    def spill_turn(it, last):
                        for b in range(SL):
                            sp.wait_ge(*ready(b, it, last))
                            sp.dma_start(store[bass.ds(it * SL + b, 1), :, :].rearrange("o p d -> (o p) d").rearrange("p (g d) -> p g d", g=G),
                                         ring_tile[:, b, :, 0:width]).then_inc(s_spill[b], 16)

                    with sp.Fori(0, turns[p] - 1) as it:
                        spill_turn(it, False)
                    spill_turn(turns[p] - 1, True)
                    for b in range(SL):
                        sp.wait_ge(s_spill[b], past(*(("A1",) if p == "A1" else ("A1", "A2"))) * 16 + 16)

                def unspill(p, ring_tile, width, store):
                    with sp.Fori(0, turns[p]) as it:
                        for b in range(SL):
                            sp.wait_ge(s_scaled[b], it + (past(*(("B1",) if p == "B2" else ())) + 1))
                            sp.dma_start(ring_tile[:, b, :, 0:width],
                                         store[bass.ds(it * SL + b, 1), :, :].rearrange("o p d -> (o p) d").rearrange("p (g d) -> p g d", g=G)).then_inc(s_back[b], 16)

                write_table(TABLE1, 0, lambda it, b: [(table1, xh[:, bass.ds(it * 2 + b, 1), :].rearrange("p o d -> p (o d)"))])
                spill("A1", lambda b, it, last: rows_due("A1", b, it, last), ring, W1C, spill1)
                for b in range(SL):
                    sp.wait_ge(s_scored[b], 1 + IT)
                sp.wait_ge(s_maxT, 1)
                for name, tile in rowv2.items():
                    sp.dma_start(tile, t["L1_gnn_" + name].partition_broadcast(P)).then_inc(s_w1b, 16)
                sp.dma_start(w1, t["L1_gnn_w1"]).then_inc(s_w1b, 16)
                sp.dma_start(w2[:, :, :], t["L1_gnn_w2"].rearrange("(a p) d -> p a d", p=P)).then_inc(s_w1b, 16)
                sp.dma_start(b1[:, :], t["L1_gnn_b1"].rearrange("(a p) -> p a", p=P),
                             allow_slow_non_contiguous=True).then_inc(s_w1b, 16)
                unspill("B1", ring, W1C, spill1)
                flat2 = lambda a: a.rearrange("a d -> (a d)").partition_broadcast(P)
                sp.dma_start(WRs[:, :, :], t["L2_gnn_W_R"][:, 0:D, :].rearrange("r k d -> k r d")).then_inc(s_w2, 16)
                sp.dma_start(WRd[:, :, :], t["L2_gnn_W_R"][:, D:2 * D, :].rearrange("r k d -> k r d")).then_inc(s_w2, 16)
                sp.dma_start(WV[:, :, :], t["L2_gnn_W_V"].rearrange("r k d -> k r d")).then_inc(s_w2, 16)
                for n, name in enumerate(("Q", "K")):
                    sp.dma_start(WQK[:, n * R * D:(n + 1) * R * D].rearrange("p (r d) -> p r d", d=D), t["L2_gnn_W_" + name].rearrange("r k d -> k r d")).then_inc(s_w2, 16)
                    sp.dma_start(c4q[:, n, :], flat2(t["L2_gnn_b_" + name])).then_inc(s_w2, 16)
                    sp.dma_start(attq[:, n, :], flat2(t["L2_gnn_a_w"][n * D:(n + 1) * D, :])).then_inc(s_w2, 16)
                sp.dma_start(bR[:, :], flat2(t["L2_gnn_b_R"])).then_inc(s_w2, 16)
                for r in range(R):
                    sp.dma_start(bVx[r * M2:(r + 1) * M2, :], t["L2_gnn_b_V"][r, :].partition_broadcast(M2)).then_inc(s_w2, 16)
                sp.dma_start(a_b[:, :], t["L2_gnn_a_b"].partition_broadcast(P)).then_inc(s_w2, 16)
                write_rows(TABLE2, (0, 0), lambda n: [(table2.rearrange("(n r) d -> n (r d)", r=R), trow[:, n, 0:R * D]),
                                                  (tableB, trow[:, n, R * D:2 * R * D])])
                for r in range(R):
                    sp.dma_start(Btab[r * M2:(r + 1) * M2, :, :],
                                 tableB[0:NV2 * M2, r * D:(r + 1) * D].rearrange("(u m) d -> m u d", m=M2)).then_inc(s_Bback, 16)
                spill("A2", lambda b, it, last: (s_relu[b], it + 1), ring2, D + 1, spill2)
                for b in range(SL):
                    sp.wait_ge(s_scored[b], 1 + past("A1", "A2"))
                unspill("B2", ring, D + 1, spill2)
                sp.wait_ge(s_maxT, 2)
                sp.dma_start(W3[:, :, :], t["L3_gnn_message_W"].rearrange("t k d -> k t d")).then_inc(s_w3, 16)
                sp.dma_start(b3[:, :], flat2(t["L3_gnn_message_b"])).then_inc(s_w3, 16)
                sp.dma_start(gru_rows[:, 0:3, :], t["L3_gnn_gru_w_ih"].rearrange("(a p) d -> p a d", p=P)).then_inc(s_w3, 16)
                sp.dma_start(gru_rows[:, 3:6, :], t["L3_gnn_gru_w_hh"].rearrange("(a p) d -> p a d", p=P)).then_inc(s_w3, 16)
                sp.dma_start(gru_b[:, 0:3 * D], t["L3_gnn_gru_b_ih"].partition_broadcast(P)).then_inc(s_w3, 16)
                sp.dma_start(gru_b[:, 3 * D:4 * D], t["L3_gnn_gru_b_hh"][2 * D:3 * D].partition_broadcast(P)).then_inc(s_w3, 16)
                sp.dma_start(gru_b2[:, :], t["L3_gnn_gru_b_hh"][0:2 * D].partition_broadcast(P)).then_inc(s_w3, 16)
                write_rows(TABLE3, (2 * (NJ // 4 + 1), 2 * (NJ // 4)), lambda n: [(table3.rearrange("(n t) d -> n (t d)", t=T8), trow[:, n, :])])
                sp.wait_ge(s_final, 1)
                sp.dma_start(out[0:(NV - 1) * P, :].rearrange("(j p) d -> p j d", p=P), X[:, 0:NV - 1, :]).then_inc(s_out, 16)
                sp.dma_start(out[(NV - 1) * P:N, :], X[0:LASTN, NV - 1, :]).then_inc(s_out, 16)
                sp.wait_ge(s_out, 32)

            @block.gpsimd
            def _(pool):
                pool.iota(iota[:, :], [[1, 512]], base=0, channel_multiplier=0,
                          allow_small_or_imprecise_dtypes=True)
                pool.iota(iota_items, [[1, NI2]], base=0, channel_multiplier=0,
                          allow_small_or_imprecise_dtypes=True)
                pool.memset(ident[:, :], 0.0)
                pool.memset(pick[:, :], 0.0)
                pool.memset(upper[:, :], 1.0).then_inc(s_const, 1)
                pool.wait_ge(s_const, 1)
                pool.affine_select(out=ident[:, :], in_=ident[:, :], compare_op=ALU.not_equal, fill=1.0,
                                   base=0, pattern=[[-1, P]], channel_multiplier=1)
                for r in range(R):
                    pool.affine_select(out=pick[:, :], in_=pick[:, :], compare_op=ALU.not_equal, fill=1.0,
                                       base=-r * M2, pattern=[[-1, M2]], channel_multiplier=1).then_inc(s_pick, 1)
                    pool.wait_ge(s_pick, r + 1)
                pool.affine_select(out=upper[:, :], in_=upper[:, :], compare_op=ALU.is_gt, fill=0.0,
                                   base=0, pattern=[[1, P]], channel_multiplier=-1).then_inc(s_const2, 1)

                def gather_loop(p, before, table, width, tables=0):
                    if tables:
                        pool.wait_ge(s_table, tables)
                    arm = [pool.alloc_register(f"gather_{p}_{b}") for b in range(SL)]
                    for b in range(SL):
                        pool.reg_mov(arm[b], past(*before))

                    def gather(b):
                        pool.reg_add(arm[b], arm[b], 1)
                        pool.wait_ge(s_const2, 1)
                        pool.wait_ge(s_ix[b], arm[b])
                        for k in range(G):
                            pool.indirect_dma_start(
                                ring[:, b, k, 0:width], None, table,
                                bass.IndirectOffsetOnAxis(ap=ix[:, b, k:k + 1], axis=0)).then_inc(s_rows[b], 16)

                    with pool.Fori(0, turns[p] - 1) as it:
                        for b in range(SL):
                            gather(b)
                    for b in range(SL):
                        if not idle_at_last(p, b):
                            gather(b)

                gather_loop("A0", (), t["x"], D)
                gather_loop("A1", ("A0",), table1, W1C, 1)
                pool.memset(wide[:, :, 0:2 * (W1C + H)], 0.0)
                pool.wait_ge(s_w8, 1)
                with pool.Fori(0, IT) as it:
                    for b in range(SL):
                        pool.wait_ge(s_back[b], it * 16 + 16)
                        pool.wait_ge(s_scat[b], it + (past("A0") + 1))
                        feats, products = (r[:, b, :, 0:D].rearrange("p g (h c) -> p g h c", c=C) for r in (ring, ring2))
                        pool.tensor_tensor(products, feats, weight[:, bass.ds(window(b, it), G), :].unsqueeze(3).to_broadcast([P, G, H, C]),
                                           ALU.mult).then_inc(s_scaled[b], 1)
                gather_loop("A2", ("A0", "A1"), table2, D, 2)
                for b in range(SL):
                    pool.wait_ge(s_scored[b], 1 + past("A1", "A2"))
                pool.memset(wide_flat, 0.0)
                pool.wait_ge(s_w8, 2)
                with pool.Fori(0, IT2) as it:
                    for b in range(SL):
                        pool.wait_ge(s_back[b], it * 16 + (past("B1") + 1) * 16)
                        pool.wait_ge(s_scat[b], it + (past("A0", "B1") + 1))
                        pool.tensor_tensor(ring2[:, b, :, 0:D + 1], ring[:, b, :, 0:D + 1],
                                           weight2[:, bass.ds(window(b, it), G)].unsqueeze(2).to_broadcast([P, G, D + 1]),
                                           ALU.mult).then_inc(s_scaled[b], 1)
                gather_loop("A3", ("A0", "A1", "A2"), table3, D, 3)

            @block.scalar
            def _(act):
                def stage_indices(table, before, it, b):
                    act.wait_ge(s_scat[b], it + (past(*before) + 1))
                    act.copy(ix[:, b, :], table[:, bass.ds(window(b, it), G)]).then_inc(s_ix[b], 1)

                def copy_turned(base, it, b, width, n=1):
                    act.wait_ge(s_turned[b], it + (base + 2))
                    act.wait_ge(s_prod[b], it + (base + 1))
                    act.copy(tT[:, b, 0:n, :], PS[:, 4 + b, 0:n * D].rearrange("p (n d) -> p n d", d=D)).then_inc(s_tcopy[b], 1)

                def roots(n):
                    act.wait_ge(s_var, n + 1)
                    act.activation(col[1][:, :], col[0][:, :], ACT.Sqrt).then_inc(s_std, 1)

                act.wait_ge(s_tabs, 1)
                with act.Fori(0, IT) as it:
                    for b in range(SL):
                        stage_indices(tab1["src"], (), it, b)
                with act.Fori(0, NJ // 2) as it:
                    for b in range(2):
                        copy_turned(NODE0, it, b, D, 2)
                act.wait_ge(s_arg, 1)
                act.activation(big, Y[:, :, :], ACT.Square).then_inc(s_val, 1)
                roots(0)
                roots(1)
                def stage_tile(source, base, it, b):
                    act.wait_ge(s_turned[b], it + (base + 1))
                    act.copy(stg[:, b, 0, :], source[:, bass.ds(it * 2 + b, 1), :].rearrange("p o d -> p (o d)")).then_inc(s_staged[b], 1)

                roots(2)
                act.wait_ge(s_ready, 1)
                with act.Fori(0, NJ // 2) as it:
                    for b in range(2):
                        stage_tile(Y, TABLE1, it, b)
                    for b in range(2):
                        copy_turned(TABLE1, it, b, D)
                with act.Fori(0, IT) as it:
                    for b in range(SL):
                        act.wait_ge(s_scored[b], it + 1)
                        act.wait_ge(s_spill[b], it * 16 + 16)
                        act.copy(ix[:, b, :], tab1["src"][:, bass.ds(window(b, it), G)]).then_inc(s_ix[b], 1)
                    for b in range(SL):
                        act.wait_ge(s_ohturn[b], it + 2)
                        act.wait_ge(s_spread1[b], it + 1)
                        act.copy(onehT[:, b, :, :], four(b)).then_inc(s_ohT[b], 1)

                def exponentials(n, tiles):
                    for h in range(H):
                        act.wait_ge(s_exin, n * H + h + 1)
                        act.activation(tiles[h], tiles[h], ACT.Exp, scale=-1.0).then_inc(s_ex, 1)

                exponentials(0, S1["rv"])
                with act.Fori(0, IT) as it:
                    for b in range(SL):
                        act.wait_ge(s_scat[b], it + (past("A0") + 1))
                        act.wait_ge(s_w8, 1)
                        act.copy(ring2[:, b, :, W1C:W1C + H], score[:, bass.ds(window(b, it), G), :])
                        act.copy(ring2[:, b, :, D:W1C], weight[:, bass.ds(window(b, it), G), :]).then_inc(s_tail[b], 1)
                act.wait_ge(s_arg, 2)
                act.activation(own[:, 0:2, :, :], own[:, 0:2, :, :], ACT.Exp, scale=-1.0).then_inc(s_val, 1)
                roots(3)
                act.wait_ge(s_ready, 2)
                def gelus(it):
                    for b in range(2):
                        act.wait_ge(s_prod[b], it + (FFN + 2))
                        act.wait_ge(s_prod2[b], it + 1)
                        act.activation(gelT[:, b, 0, :], PS[:, 6 + b, 0:D], ACT.Gelu, bias=b1[:, 0:1])
                        act.activation(gelT[:, b, 1, :], PS[:, 6 + b, D:2 * D], ACT.Gelu, bias=b1[:, 1:2]).then_inc(s_mid[b], 1)

                with act.Fori(0, NJ // 8) as four_turns:
                    for m in range(4):
                        gelus(four_turns * 4 + m)
                gelus(NJ // 2 - 1)
                roots(4)
                act.wait_ge(s_ready, 3)
                with act.Fori(0, NJ // 2) as it:
                    for b in range(2):
                        stage_tile(X, TABLE2, it, b)
                    for b in range(2):
                        copy_turned(TABLE2, it, b, D)
                def stage_sources(it, b):
                    act.wait_ge(s_added[b], it + 1)
                    act.copy(ix[:, b, :], tab2["src4"][:, bass.ds(window(b, it), G)]).then_inc(s_ix[b], 1)

                def copy_onehot(it, b):
                    act.wait_ge(s_ohturn[b], it + (past("A1") + 2))
                    act.wait_ge(s_spread1[b], it + (past("A1") + 1))
                    act.copy(onehT[:, b, :, :], four(2 * b)).then_inc(s_ohT[b], 1)

                def relation_turn(it, more):
                    for b in range(SL):
                        if more:
                            stage_sources(it + 1, b)
                    for b in range(SL):
                        act.wait_ge(s_relT[b], it + 1)
                        act.copy(relT(b), four(2 * b)).then_inc(s_relTc[b], 1)
                    for b in range(SL):
                        if more:
                            copy_onehot(it + 1, b)

                for b in range(SL):
                    stage_sources(0, b)
                for b in range(SL):
                    copy_onehot(0, b)
                with act.Fori(0, IT2 - 1) as it:
                    relation_turn(it, True)
                relation_turn(IT2 - 1, False)
                exponentials(1, S2["rv"])
                with act.Fori(0, IT2) as it:
                    for b in range(SL):
                        act.wait_ge(s_scat[b], it + (past("A0", "B1") + 1))
                        for k in range(G):
                            ins = act.activation(oneh[:, b, k, :], iota[:, 0:P], ACT.Square, scale=-1.0,
                                                 bias=tab2["rel"][:, bass.ds(window(b, it) + k, 1)])
                        ins.then_inc(s_ohsq[b], 1)
                        act.wait_ge(s_ohsq[b], it + 1)
                        act.activation(oneh[:, b, :, :], oneh[:, b, :, :], ACT.Relu, scale=-1.0, bias=ones_col[:, 0:1]).then_inc(s_oh[b], 1)
                with act.Fori(0, NJ // 2) as it:
                    for b in range(2):
                        act.wait_ge(s_turned[b], it + (NODE2 + 2))
                        act.wait_ge(s_prod[b], it + (NODE2 + 1))
                        act.copy(tT[:, b, 0:R, :].rearrange("p r (u m) -> p u r m", m=M2),
                                 PS[:, 4 + b, :].rearrange("p (u r m) -> p u r m", u=4, m=M2)).then_inc(s_tcopy[b], 1)
                act.wait_ge(s_arg, 3)
                act.activation(big, big, ACT.Exp).then_inc(s_val, 1)
                roots(5)
                act.wait_ge(s_gruT, 1)
                for n in range(2):
                    ins = act.copy(gruT[:, n, :], PS[:, n, 0:3 * D])
                act.wait_ge(s_ready, 4)
                with act.Fori(0, NJ // 2) as it:
                    for b in range(2):
                        stage_tile(X, TABLE3, it, b)
                    for b in range(2):
                        copy_turned(TABLE3, it, b, D)
                with act.Fori(0, IT) as it:
                    for b in range(SL):
                        stage_indices(tab1["src8"], ("A0", "B1", "B2"), it, b)
                act.wait_ge(s_ready, 5)
                with act.Fori(0, NJ // 2) as it:
                    for b in range(2):
                        act.wait_ge(s_turned[b], it + (GRU + 1))
                        act.copy(stg[:, b, 0, :], X[:, bass.ds(it * 2 + b, 1), :].rearrange("p o d -> p (o d)"))
                        act.copy(stg[:, b, 1, :], Y[:, bass.ds(it * 2 + b, 1), :].rearrange("p o d -> p (o d)")).then_inc(s_staged[b], 1)
                    for b in range(2):
                        copy_turned(GRU, it, b, D, 2)
                act.wait_ge(s_arg, 4)
                act.activation(wide[:, :, 0:2 * D], wide[:, :, 0:2 * D], ACT.Sigmoid).then_inc(s_val, 1)
                act.wait_ge(s_arg, 5)
                act.activation(wide[:, :, 2 * D:3 * D], wide[:, :, 2 * D:3 * D], ACT.Tanh).then_inc(s_val, 1)
                roots(6)

            @block.tensor
            def _(pe):
                pe.wait_ge(s_const2, 1)
                for b in range(2):
                    pe.sem_inc(s_turned[b], 1)
                    pe.sem_inc(s_prod[b], 1)
                    pe.sem_inc(s_prod2[b], 1)
                for b in range(SL):
                    pe.sem_inc(s_scat[b], 1)
                    pe.sem_inc(s_ohturn[b], 1)
                    pe.sem_inc(s_spread1[b], 1)
                def spread_items(n, names, items):
                    pe.wait_ge(s_first, n + 1)
                    pe.matmul(PS[0:Q, 7, 508:509], upper[0:Q, 0:Q], tile_f[:, 4, 3:4], start=True, stop=True).then_inc(s_pre, 1)
                    pe.wait_ge(s_spread, n + 1)
                    step = items if items <= 512 else items // 2
                    for m, name in enumerate(names):
                        for a in range(0, items, step):
                            bank = m if step == items else 2 * m + a // step
                            for k in range(4):
                                mm = pe.matmul(PS[:, bank, 0:step], rows[name][:, k * P:(k + 1) * P], spread[:, k, a:a + step],
                                               start=k == 0, stop=k == 3)
                    mm.then_inc(s_items, 1)

                spread_items(0, ("src", "dst", "t8", "w", "j"), NI)
                spread_items(1, ("src", "dst", "t4", "j"), NI2)

                def scatter(first, arrived, oh_before, it, b, width, rows_=ring):
                    pe.wait_ge(*arrived)
                    pe.wait_ge(s_oh[b], it + (past(*oh_before) + 1))
                    pe.wait_ge(s_acc, it * (SL * G) + (first + b * G + G - SL * G))
                    for k in range(G):
                        mm = pe.matmul(sums_of(b, k, width), oneh[:, b, k, :], rows_[:, b, k, 0:width],
                                       start=True, stop=True)
                    mm.then_inc(s_scat[b], 1)

                def node_tiles_loop(base, n, outs):
                    def step(it, more):
                        for b in range(2):
                            if more:
                                turn(base, it + 1, b, n)
                        for b in range(2):
                            product(base, it, b, outs(b))

                    for b in range(2):
                        turn(base, 0, b, n)
                    with pe.Fori(0, NJ // 2 - 1) as it:
                        step(it, True)
                    step(NJ // 2 - 1, False)

                def turn(base, it, b, n=1):
                    pe.wait_ge(s_staged[b], it + (base + 2))
                    pe.wait_ge(s_tcopy[b], it + (base + 1))
                    for m in range(n):
                        mm = pe.transpose(PS[:, 4 + b, m * D:(m + 1) * D], stg[:, b, m, :], ident[:, :])
                    mm.then_inc(s_turned[b], 1)

                def product(base, it, b, outs):
                    pe.wait_ge(s_tcopy[b], it + (base + 2))
                    pe.wait_ge(s_take[b], it + (base + 1))
                    for to, pairs in outs:
                        for n, (lhs, rhs) in enumerate(pairs):
                            mm = pe.matmul(to, lhs, rhs, start=n == 0, stop=n == len(pairs) - 1)
                    mm.then_inc(s_prod[b], 1)

                pe.wait_ge(s_tabs, 1)
                def scatter_gathered(p, first, oh_before):
                    with pe.Fori(0, IT - 1) as it:
                        for b in range(SL):
                            scatter(first, rows_due(p, b, it), oh_before, it, b, D)
                    for b in range(SL):
                        scatter(first, rows_due(p, b, IT - 1, True), oh_before, IT - 1, b, D)

                scatter_gathered("A0", ACC0, ())
                pe.wait_ge(s_w, 96)
                node_tiles_loop(NODE0, 2, lambda b: [(PS[:, 6 + b, 0:D], [(tT[:, b, 0, :], W0[:, 0, :]), (tT[:, b, 1, :], W0[:, 1, :])])])
                def to_rows(n, S, K, tables):
                    pe.wait_ge(s_torow, n + 1)
                    for m, table in enumerate(tables):
                        for k in range(K):
                            at = m * (512 if K <= 4 else 1024) + k * P
                            mm = pe.transpose(PS[0:S["n"], at // 512, at % 512:at % 512 + P], table[:, k:K * S["n"]:K], ident[:, :])
                    mm.then_inc(s_inrow, 1)

                def turn_ends(n, S):
                    pe.wait_ge(s_ends, n + 1)
                    pe.transpose(PS[0:4, 4, 0:S["n"]], ends[0:S["n"], :], ident[0:S["n"], 0:S["n"]]).then_inc(s_endsT, 1)

                def turn_carries(n, S, row):
                    pe.wait_ge(s_scan, n + 1)
                    pe.transpose(PS[0:S["n"], 4, 256:260], row, ident[0:4, 0:4]).then_inc(s_scanT, 1)

                def segment_starts(n, S, K, tables):
                    to_rows(n, S, K, tables)
                    turn_ends(4 * (n // 2), S)
                    turn_carries(3 * (n // 2), S, before_row[:, 0:S["n"]])
                    turn_ends(4 * (n // 2) + 1, S)

                def segment_maxima(n, S, K, tables):
                    to_rows(2 * n + 1, S, K, tables)
                    turn_ends(4 * n + 2, S)
                    turn_carries(3 * n + 1, S, before_row[:, 0:S["n"]])
                    turn_ends(4 * n + 3, S)
                    turn_carries(3 * n + 2, S, after_row[:, 1:S["n"] + 1])

                def to_items(S, K, tile, bank):
                    for k in range(K):
                        at = bank + k // 4
                        mm = pe.transpose(PS[:, at, (k % 4) * S["n"]:(k % 4 + 1) * S["n"]], tile[:, k * P:(k + 1) * P],
                                          ident[0:S["n"], 0:S["n"]])
                    return mm

                segment_starts(0, S1, K1, [tab1[n] for n in ("dst", "ok")])
                pe.wait_ge(s_ready, 1)
                node_tiles_loop(TABLE1, 1, lambda b: [(PS[:, 6 + b, 0:D + 2 * H], [(tT[:, b, 0, :], WX[:, :])])])
                with pe.Fori(0, IT) as it:
                    for b in range(SL):
                        pe.wait_ge(s_oh[b], it + (IT + 1))
                        pe.wait_ge(s_ohT[b], it + 1)
                        for k in range(G):
                            mm = pe.transpose(four(b)[:, k, :], oneh[:, b, k, :], ident[:, :])
                        mm.then_inc(s_ohturn[b], 1)
                    for b in range(SL):
                        j = node_tiles(mybir.EngineType.PE, tab1, window(b, it), NV)
                        pe.wait_ge(s_ohT[b], it + 2)
                        pe.wait_ge(s_scored[b], it + 1)
                        for k in range(G):
                            mm = pe.matmul(PS[:, SL + b, k * H:(k + 1) * H], onehT[:, b, k, :],
                                           ad[:, bass.ds(j[k], 1), :].rearrange("p o h -> p (o h)"), start=True, stop=True)
                        mm.then_inc(s_spread1[b], 1)
                segment_maxima(0, S1, K1, [score[:, :, h] for h in range(H)])
                for h in range(H):
                    pe.wait_ge(s_ex, h + 1)
                    to_items(S1, K1, S1["rv"][h], h).then_inc(s_exT, 1)
                pe.wait_ge(s_max, 1)
                for h in range(H):
                    mm = to_items(S1, K1, S1["rf"][h], 4 + h)
                mm.then_inc(s_maxT, 1)
                with pe.Fori(0, IT) as it:
                    for b in range(SL):
                        pe.wait_ge(s_tail[b], it + 1)
                        scatter(ACC0 + NI, (s_scaled[b], it + 2), ("A0", "A1"), it, b, W1C + H, ring2)
                pe.wait_ge(s_ready, 2)
                def feed_forward(it, more):
                    for b in range(2):
                        pe.wait_ge(s_mid[b], it + 1)
                        product(FFN, it, b, [(PS[:, 6 + b, a * D:(a + 1) * D], [(w1[:, a * D:(a + 1) * D], tT[:, b, 0, :])]) for a in range(2)])
                    for b in range(2):
                        if more:
                            turn(FFN, it + 1, b)
                    for b in range(2):
                        pe.wait_ge(s_mid[b], it + 2)
                        for a in range(2):
                            mm = pe.matmul(PS[:, 2 + b, 0:D], gelT[:, b, a, :], w2[:, a, :], start=a == 0, stop=a == 1)
                        mm.then_inc(s_prod2[b], 1)

                for b in range(2):
                    turn(FFN, 0, b)
                with pe.Fori(0, NJ // 2 - 1) as it:
                    feed_forward(it, True)
                feed_forward(NJ // 2 - 1, False)
                pe.wait_ge(s_ready, 3)
                node_tiles_loop(TABLE2, 1, lambda b: [(PS[:, 6 + b, :], [(tT[:, b, 0, :], WRs[:, :, :].rearrange("p r d -> p (r d)"))]),
                                              (PS[:, 2 + b, :], [(tT[:, b, 0, :], WRd[:, :, :].rearrange("p r d -> p (r d)"))])])
                segment_starts(2, S2, K2, [tab2["dst"], tab2["ok"], tab2["t4"]])
                pe.wait_ge(s_Bback, R * 16)
                def turn_onehots(it, b):
                    pe.wait_ge(s_oh[b], it + (past("A0", "A1", "B1") + 1))
                    for k in range(G):
                        mm = pe.transpose(four(2 * b)[:, k, :], oneh[:, b, k, :], ident[:, :])
                    mm.then_inc(s_ohturn[b], 1)

                def relation_turn(it, more):
                    for b in range(SL):
                        j = node_tiles(mybir.EngineType.PE, tab2, window(b, it), NV2)
                        pe.wait_ge(s_ohT[b], it + (past("A1") + 2))
                        pe.wait_ge(s_scored[b], it + (past("A1") + 1))
                        for k in range(G):
                            mm = pe.matmul(four(2 * b + 1)[:, k, :], onehT[:, b, k, :],
                                           Btab[:, bass.ds(j[k], 1), :].rearrange("p o d -> p (o d)"), start=True, stop=True)
                        mm.then_inc(s_spread1[b], 1)
                    for b in range(SL):
                        pe.wait_ge(s_relu[b], it + 1)
                        for k in range(G):
                            mm = pe.transpose(four(2 * b)[:, k, :], ring2[:, b, k, 0:D], ident[:, :])
                        mm.then_inc(s_relT[b], 1)
                    for b in range(SL):
                        pe.wait_ge(s_relTc[b], it + 1)
                        for k in range(G):
                            mm = pe.matmul(PS[:, 2 * b + 1, k * R:(k + 1) * R], relT(b)[:, k, :], u4[:, 0, :], start=True, stop=True)
                        mm.then_inc(s_s4[b], 1)
                        if more:
                            turn_onehots(it + 1, b)

                for b in range(SL):
                    turn_onehots(0, b)
                with pe.Fori(0, IT2 - 1) as it:
                    relation_turn(it, True)
                relation_turn(IT2 - 1, False)
                segment_maxima(1, S2, K2, [score2[:, :, r] for r in range(R)])
                pe.wait_ge(s_max, 2)
                to_items(S2, K2, S2["rv"][0], 0).then_inc(s_maxT, 1)
                with pe.Fori(0, IT2) as it:
                    for b in range(SL):
                        scatter(ACC0 + 2 * NI, (s_scaled[b], it + (past("B1") + 2)), ("A0", "A1", "B1", "A2"), it, b, D + 1, ring2)
                def turn_relations(it, b):
                    pe.wait_ge(s_staged[b], it + (NODE2 + 2))
                    pe.wait_ge(s_tcopy[b], it + (NODE2 + 1))
                    for r in range(R):
                        mm = pe.transpose(PS[:, 4 + b, r * D:(r + 1) * D], stg[:, b, r, :], ident[:, :])
                    mm.then_inc(s_turned[b], 1)

                def relation_values(it, more):
                    for b in range(2):
                        product(NODE2, it, b, [(PS[:, 6 + b, 0:D], [(tT[:, b, r, :], WV[:, r, :]) for r in range(R)] + [(stg[:, b, R, :], bVx[:, :])])])
                    for b in range(2):
                        if more:
                            turn_relations(it + 1, b)

                for b in range(2):
                    turn_relations(0, b)
                with pe.Fori(0, NJ // 2 - 1) as it:
                    relation_values(it, True)
                relation_values(NJ // 2 - 1, False)
                pe.wait_ge(s_w3, 7 * 16)
                pe.wait_ge(s_acc, ACC0 + 2 * NI + NI2)
                for n in range(2):
                    for a in range(3):
                        mm = pe.transpose(PS[:, n, a * D:(a + 1) * D], gru_rows[:, 3 * n + a, :], ident[:, :])
                mm.then_inc(s_gruT, 1)
                pe.wait_ge(s_ready, 4)
                node_tiles_loop(TABLE3, 1, lambda b: [(PS[:, (6, 2)[a] + b, :], [(tT[:, b, 0, :], W3[:, 4 * a:4 * a + 4, :].rearrange("p r d -> p (r d)"))])
                                              for a in range(2)])
                scatter_gathered("A3", ACC0 + 2 * NI + NI2, ("A0", "A1", "B1", "A2", "B2"))
                pe.wait_ge(s_ready, 5)
                node_tiles_loop(GRU, 2, lambda b: [(PS[:, 6 + b, 0:2 * D], [(tT[:, b, 1, :], gruT[:, 0, 0:2 * D]), (tT[:, b, 0, :], gruT[:, 1, 0:2 * D])]),
                                              (PS[:, 6 + b, 2 * D:3 * D], [(tT[:, b, 1, :], gruT[:, 0, 2 * D:3 * D])]),
                                              (PS[:, 6 + b, 3 * D:4 * D], [(tT[:, b, 0, :], gruT[:, 1, 2 * D:3 * D])])])
            @block.vector
            def _(dve):
                ch = Chain(dve, s_chain)
                for name, value in (("src", 0), ("dst", 4095), ("t4", 0), ("t8", 0)):
                    dve.memset(ints[name][96:Q, :], value)
                dve.memset(X[:, NV - 1:NJ, :], 0.0)
                dve.memset(ones_col[:, :], 1.0)
                dve.memset(rows["w"][96:Q, :], 0.0).then_inc(s_pad, 1)
                for b in range(2):
                    dve.sem_inc(s_staged[b], 1)
                    dve.sem_inc(s_take[b], 1)
                    dve.sem_inc(s_tcopy[b], 1)
                    dve.sem_inc(s_mid[b], 1)
                for b in range(SL):
                    dve.sem_inc(s_rowdone[b], 16)
                    dve.sem_inc(s_ohT[b], 1)
                    dve.sem_inc(s_scaled[b], 1)
                    dve.sem_inc(s_scored[b], 1)
                    dve.sem_inc(s_added[b], 1)
                    dve.sem_inc(s_spill[b], 16)
                dve.wait_ge(s_const2, 1)
                dve.wait_ge(s_in, 160)
                for name in ("src", "dst", "t4"):
                    dve.tensor_copy(rows[name], ints[name])
                ch.link(dve.tensor_copy(rows["t8"], ints["t8"]))
                first, last, cnt, ones, incl, off, end, delta = (tile_f[:, n, :] for n in range(8))

                def spread_items(n, tab, shift, tiles, items, parts):
                    dve.tensor_single_scalar(tile_i[:, 0:4], ints["dst"][:, 0:512:P], shift, ALU.arith_shift_right)
                    ch.link(dve.tensor_single_scalar(tile_i[:, 4:8], ints["dst"][:, P - 1:512:P], shift, ALU.arith_shift_right))
                    dve.tensor_copy(first, tile_i[:, 0:4])
                    dve.memset(ones, 1.0)
                    ch.link(dve.tensor_single_scalar(last, tile_i[:, 4:8], float(tiles - 1), ALU.min))
                    ch.link(dve.scalar_tensor_tensor(cnt, last, 1.0, first, ALU.add, ALU.subtract))
                    dve.tensor_tensor_scan(incl, ones, cnt, 0.0, ALU.mult, ALU.add).then_inc(s_first, 1)
                    dve.wait_ge(s_first, n + 1)
                    ch.link(dve.tensor_tensor(off, incl, cnt, ALU.subtract))
                    dve.wait_ge(s_pre, n + 1)
                    ch.link(dve.tensor_scalar(off, off, PS[0:Q, 7, 508:509], None, ALU.add))
                    dve.tensor_tensor(end, off, cnt, ALU.add)
                    ch.link(dve.tensor_tensor(delta, first, off, ALU.subtract))
                    for k in range(4):
                        dve.tensor_scalar(spread[:, k, 0:items], iota_items[0:Q, 0:items], off[:, k:k + 1], None, ALU.is_ge)
                    ch.link(dve.tensor_copy(rows["j"].rearrange("q (k e) -> q k e", e=P),
                                            delta.unsqueeze(2).to_broadcast([Q, 4, P])))
                    for k in range(4):
                        ins = dve.scalar_tensor_tensor(spread[:, k, 0:items], iota_items[0:Q, 0:items], end[:, k:k + 1],
                                                       spread[:, k, 0:items], ALU.is_lt, ALU.mult)
                    ins.then_inc(s_spread, 1)
                    dve.wait_ge(s_items, n + 1)
                    step = items if items <= 512 else items // 2
                    for a in range(0, items, step):
                        cols = slice(a, a + step)
                        from_psum = {name: PS[:, m if step == items else 2 * m + a // step, 0:step] for m, name in enumerate(parts)}
                        for name in ("w", "t4"):
                            if name in from_psum and name in tab:
                                dve.tensor_copy(tab[name][:, cols], from_psum[name])
                        if "src" in tab:
                            dve.tensor_copy(tab["src"][:, cols], from_psum["src"])
                        ch.link(dve.tensor_copy(score_w[:, cols], from_psum["src"]))
                        ch.link(dve.tensor_tensor(tab["jf"][:, cols], iota_items[:, cols], from_psum["j"], ALU.add))
                        dve.tensor_scalar(tab["j"][:, cols], tab["jf"][:, cols], float(tiles - 1), 0.0, ALU.min, ALU.max)
                        if "src8" in tab:
                            dve.scalar_tensor_tensor(tab["src8"][:, cols], score_w[:, cols], float(T8), from_psum["t8"], ALU.mult, ALU.add)
                        else:
                            dve.scalar_tensor_tensor(tab["src4"][:, cols], score_w[:, cols], float(R), from_psum["t4"], ALU.mult, ALU.add)
                        dve.tensor_copy(tab["dst"][:, cols], from_psum["dst"])
                        ch.link(dve.scalar_tensor_tensor(tab["rel"][:, cols], tab["jf"][:, cols], -float(2 ** shift), from_psum["dst"], ALU.mult, ALU.add))
                    rel, ok, dst = tab["rel"], tab["ok"], tab["dst"]
                    ch.link(dve.tensor_single_scalar(ok, rel, 0.0, ALU.is_ge))
                    ch.link(dve.scalar_tensor_tensor(ok, rel, float(2 ** shift), ok, ALU.is_lt, ALU.mult))
                    if "src4" in tab:
                        ch.link(dve.scalar_tensor_tensor(rel, tab["t4"], float(M2), rel, ALU.mult, ALU.add))
                    ch.link(dve.scalar_tensor_tensor(rel, rel, FAR, ok, ALU.add, ALU.mult))
                    ch.link(dve.tensor_single_scalar(rel, rel, -FAR, ALU.add))
                    ch.link(dve.scalar_tensor_tensor(dst, dst, 1.0, ok, ALU.add, ALU.mult))
                    dve.tensor_single_scalar(dst, dst, -1.0, ALU.add).then_inc(s_tabs, 1)

                spread_items(0, tab1, 7, NV, NI, ("src", "dst", "t8", "w", "j"))
                spread_items(1, tab2, 5, NV2, NI2, ("src", "dst", "t4", "j"))
                dve.sem_inc(s_acc, ACC0 - 1)
                dve.wait_ge(s_tabs, 2)
                dve.memset(acc0, 0.0).then_inc(s_acc, 1)

                def add_sums(first, before, tab, it, b, width, targets, nodes):
                    j = node_tiles(mybir.EngineType.DVE, tab, window(b, it), nodes)
                    dve.wait_ge(s_scat[b], it + (past(*before) + 2))
                    for k in range(G):
                        a = targets[k % len(targets)][:, bass.ds(j[k], 1), :].rearrange("p o d -> p (o d)")
                        dve.wait_ge(s_acc, it * (SL * G) + (first + b * G + k + 1 - len(targets)))
                        dve.tensor_tensor(a, a, sums_of(b, k, width), ALU.add).then_inc(s_acc, 1)

                def layer_norm(n, source, target):
                    with dve.Fori(0, 2) as half:
                        for m in range(NJ // 2):
                            j = half * (NJ // 2) + m
                            dve.bn_stats(stats[:, bass.ds(j, 1), :].rearrange("p o d -> p (o d)"),
                                         source[:, bass.ds(j, 1), :].rearrange("p o d -> p (o d)"))
                    ch.link(dve.memset(col[5][:, :], 0.0))
                    me, ve, mo, vo = (stats[:, :, m] for m in (1, 2, 4, 5))
                    dve.tensor_tensor(col[2][:, :], me, mo, ALU.add)
                    dve.tensor_tensor(col[3][:, :], me, mo, ALU.subtract)
                    ch.link(dve.tensor_tensor(col[0][:, :], ve, vo, ALU.add))
                    ch.link(dve.tensor_tensor(col[3][:, :], col[3][:, :], col[3][:, :], ALU.mult))
                    dve.tensor_single_scalar(col[2][:, :], col[2][:, :], 0.5, ALU.mult)
                    ch.link(dve.tensor_scalar(col[3][:, :], col[3][:, :], 0.25, 1e-5, ALU.mult, ALU.add))
                    dve.scalar_tensor_tensor(col[0][:, :], col[0][:, :], 1.0 / D, col[3][:, :], ALU.mult, ALU.add).then_inc(s_var, 1)
                    ch.link(dve.tensor_tensor(target, source, col[2][:, :].unsqueeze(2).to_broadcast([P, NJ, D]), ALU.subtract))
                    dve.wait_ge(s_std, n + 1)
                    ch.link(dve.reciprocal(col[1][:, :], col[1][:, :]))
                    ch.link(dve.tensor_tensor(target, target, col[1][:, :].unsqueeze(2).to_broadcast([P, NJ, D]), ALU.mult))

                def build_onehots(free, tab, it, b):
                    dve.wait_ge(*free)
                    dve.tensor_tensor(oneh[:, b, :, :], iota[:, 0:P].unsqueeze(1).to_broadcast([P, G, P]),
                                      tab["rel"][:, bass.ds(window(b, it), G)].unsqueeze(2).to_broadcast([P, G, P]),
                                      ALU.is_equal).then_inc(s_oh[b], 1)

                with dve.Fori(0, IT) as it:
                    for b in range(SL):
                        dve.wait_ge(s_scat[b], it + 1)
                        for k in range(G):
                            i = window(b, it) + k
                            ins = dve.tensor_scalar(oneh[:, b, k, :], iota[:, 0:P], tab1["rel"][:, bass.ds(i, 1)],
                                                    tab1["w"][:, bass.ds(i, 1)], ALU.is_equal, ALU.mult)
                        ins.then_inc(s_oh[b], 1)
                    for b in range(SL):
                        add_sums(ACC0, (), tab1, it, b, D, [acc0], NV)
                dve.wait_ge(s_acc, ACC0 + NI)
                dve.wait_ge(s_w, 96)
                ch.link(dve.tensor_tensor(bias0[:, 0, :], bias0[:, 0, :], bias0[:, 1, :], ALU.add))

                def stage_sums(it, b):
                    j = it * 2 + b
                    xj = X[:, bass.ds(j, 1), :].rearrange("p o d -> p (o d)")
                    lj = acc0[:, bass.ds(j, 1), :].rearrange("p o d -> p (o d)")
                    dve.wait_ge(s_turned[b], it + 1)
                    dve.tensor_tensor(stg[:, b, 0, :], xj, lj, ALU.add)
                    dve.tensor_tensor(stg[:, b, 1, :], xj, lj, ALU.mult).then_inc(s_staged[b], 1)

                def take_sums(it, more):
                    for b in range(2):
                        if more:
                            stage_sums(it + 1, b)
                    for b in range(2):
                        yj = Y[:, bass.ds(it * 2 + b, 1), :].rearrange("p o d -> p (o d)")
                        dve.wait_ge(s_prod[b], it + 2)
                        dve.tensor_tensor(yj, PS[:, 6 + b, 0:D], bias0[:, 0, :], ALU.add).then_inc(s_take[b], 1)

                for b in range(2):
                    stage_sums(0, b)
                with dve.Fori(0, NJ // 2 - 1) as it:
                    take_sums(it, True)
                take_sums(NJ // 2 - 1, False)
                dve.wait_ge(s_take[0], TABLE1 + 1)
                dve.wait_ge(s_take[1], TABLE1 + 1)
                ch.link(dve.scalar_tensor_tensor(Y[:, :, :], Y[:, :, :], 0.2, Y[:, :, :], ALU.mult, ALU.max))
                dve.sem_inc(s_arg, 1)
                dve.wait_ge(s_val, 1)
                ch.link(dve.tensor_reduce(col[0][:, :], big, AX.X, ALU.add))
                dve.tensor_single_scalar(col[0][:, :], col[0][:, :], 1e-24, ALU.max).then_inc(s_var, 1)
                dve.wait_ge(s_std, 1)
                ch.link(dve.reciprocal(col[1][:, :], col[1][:, :]))
                ch.link(dve.tensor_tensor(Y[:, :, :], Y[:, :, :], col[1][:, :].unsqueeze(2).to_broadcast([P, NJ, D]), ALU.mult))
                ch.link(dve.tensor_tensor(Y[:, :, :], Y[:, :, :], X[:, :, :], ALU.add))
                layer_norm(1, Y[:, :, :], X[:, :, :])
                everyone = lambda v: v.unsqueeze(1).to_broadcast([P, NJ, D])
                dve.wait_ge(s_w1, 5 * 16)

                def scale_shift(target, gain, shift):
                    ch.link(dve.tensor_tensor(target, target, everyone(gain), ALU.mult))
                    ch.link(dve.tensor_tensor(target, target, everyone(shift), ALU.add))

                for n in range(2):
                    dve.tensor_tensor(scaled_w[:, n, :], WX[:, 0:D], att[:, n, :], ALU.mult)
                ch.link(dve.memset(before_row[:, :], -BIG))
                for n in range(2):
                    dve.tensor_reduce(WX[:, D + n * H:D + (n + 1) * H], scaled_w[:, n, :].rearrange("p (h c) -> p h c", c=C), AX.X, ALU.add)
                ch.link(dve.memset(after_row[:, :], -BIG))

                def segment_starts(n, S):
                    Qn, W = S["n"], S["width"]
                    key, reset, rdst = S["key"], S["reset"], S["dst"]
                    ch.link(dve.memset(ends[:, :], 0.0))
                    dve.tensor_reduce(ends[0:Qn, 0:1], rdst, AX.X, ALU.max).then_inc(s_ends, 1)
                    dve.wait_ge(s_endsT, 4 * n + 1)
                    ch.link(dve.tensor_copy(resets_row[:, 0:Qn], PS[0:4, 4, 0:Qn]))
                    dve.tensor_tensor_scan(before_row[:, 1:Qn + 1], resets_row[:, 0:Qn], resets_row[:, 0:Qn], -1.0, ALU.max, ALU.max).then_inc(s_scan, 1)
                    dve.wait_ge(s_scanT, 3 * n + 1)
                    ch.link(dve.tensor_single_scalar(key[:, 0:1], PS[0:Qn, 4, 256:257], -1.0, ALU.max))
                    ch.link(dve.tensor_tensor_scan(key[:, 1:W + 1], rdst, rdst, key[:, 0:1], ALU.max, ALU.max))
                    ch.link(dve.tensor_tensor(reset[:, 0:W], rdst, key[:, 0:W], ALU.is_gt))
                    dve.memset(reset[:, W:W + 1], 0.0)
                    ch.link(dve.tensor_single_scalar(reset[:, 0:W], reset[:, 0:W], -BIG, ALU.mult))
                    for m in range(4):
                        ins = dve.tensor_reduce(ends[0:Qn, m:m + 1], reset[:, 0:W], AX.X, ALU.add)
                    ins.then_inc(s_ends, 1)
                    dve.wait_ge(s_endsT, 4 * n + 2)
                    ch.link(dve.tensor_copy(resets_row[:, 0:Qn], PS[0:4, 4, 0:Qn]))

                dve.sem_inc(s_torow, 1)
                dve.wait_ge(s_inrow, 1)
                dve.tensor_scalar(S1["aux"], PS[0:Q1, 1, :], BIG, -BIG, ALU.mult, ALU.add)
                ch.link(dve.tensor_copy(S1["dst"], PS[0:Q1, 0, :]))
                segment_starts(0, S1)

                def segment_max(n, S, starts_too):
                    Qn, W = S["n"], S["width"]
                    reset, rv, rf, rg, scratch = S["reset"], S["rv"], S["rf"], S["g"], S["scratch"]
                    for h in range(H):
                        ch.link(dve.tensor_tensor_scan(scratch, reset[:, 0:W], rv[h], -BIG, ALU.add, ALU.max))
                        ch.link(dve.tensor_copy(ends[0:Qn, h:h + 1], scratch[:, W - 1:W]))
                    dve.sem_inc(s_ends, 1)
                    dve.wait_ge(s_endsT, 4 * n + 3)
                    dve.tensor_tensor_scan(before_row[:, 1:Qn + 1], resets_row[:, 0:Qn], PS[0:4, 4, 0:Qn], -BIG, ALU.add, ALU.max).then_inc(s_scan, 1)
                    dve.wait_ge(s_scanT, 3 * n + 2)
                    ch.link(dve.tensor_copy(carry[0:Qn, :], PS[0:Qn, 4, 256:260]))
                    for h in range(H):
                        ins = dve.tensor_tensor_scan(rf[h], reset[:, 0:W], rv[h], carry[0:Qn, h:h + 1], ALU.add, ALU.max)
                    ch.link(ins)
                    for h in range(H):
                        ch.link(dve.tensor_tensor_scan(scratch[:, ::-1], reset[:, 1:W + 1][:, ::-1], rf[h][:, ::-1], -BIG, ALU.add, ALU.max))
                        ch.link(dve.tensor_tensor(ends[0:Qn, h:h + 1], scratch[:, 0:1], reset[:, 0:1], ALU.add))
                    ch.link(dve.memset(after_row[:, Qn:Qn + 1], -BIG))
                    dve.sem_inc(s_ends, 1)
                    dve.wait_ge(s_endsT, 4 * n + 4)
                    dve.tensor_tensor_scan(after_row[:, 0:Qn][:, ::-1], resets_row[:, 0:Qn][:, ::-1], PS[0:4, 4, 0:Qn][:, ::-1], -BIG, ALU.add, ALU.max).then_inc(s_scan, 1)
                    dve.wait_ge(s_scanT, 3 * n + 3)
                    ch.link(dve.tensor_copy(carry[0:Qn, :], PS[0:Qn, 4, 256:260]))
                    for h in range(H):
                        ch.link(dve.tensor_tensor_scan(rg[:, ::-1], reset[:, 1:W + 1][:, ::-1], rf[h][:, ::-1], carry[0:Qn, h:h + 1], ALU.add, ALU.max))
                        dve.scalar_tensor_tensor(rv[h], rg, -0.1 * BIG, rv[h], ALU.max, ALU.subtract).then_inc(s_exin, 1)
                        dve.wait_ge(s_exin, n * H + h + 1)
                        if starts_too:
                            ch.link(dve.scalar_tensor_tensor(rf[h], reset[:, 0:W], 0.0, rg, ALU.is_lt, ALU.mult))

                layer_norm(2, X[:, :, :], Y[:, :, :])
                scale_shift(Y[:, :, :], rowv["ln1_g"][:, :], rowv["ln1_b"])
                dve.sem_inc(s_ready, 1)
                with dve.Fori(0, NJ // 2) as it:
                    for b in range(2):
                        dve.wait_ge(s_prod[b], it + (TABLE1 + 2))
                        dve.tensor_copy(ad[:, bass.ds(it * 2 + b, 1), :].rearrange("p o h -> p (o h)"), PS[:, 6 + b, W1C:W1C + H])
                        dve.tensor_copy(xh[:, bass.ds(it * 2 + b, 1), :].rearrange("p o d -> p (o d)"), PS[:, 6 + b, 0:W1C]).then_inc(s_take[b], 1)
                def score_turn(it, last):
                    for b in range(SL):
                        build_onehots((s_ohturn[b], it + 1), tab1, it, b)
                    for b in range(SL):
                        dve.wait_ge(s_spread1[b], it + 2)
                        dve.wait_ge(*rows_due("A1", b, it, last))
                        dve.tensor_tensor(score[:, bass.ds(window(b, it), G), :],
                                          PS[:, SL + b, 0:G * H].rearrange("p (g h) -> p g h", g=G),
                                          ring[:, b, :, D:W1C], ALU.add).then_inc(s_scored[b], 1)

                with dve.Fori(0, IT - 1) as it:
                    score_turn(it, False)
                score_turn(IT - 1, True)
                for b in range(SL):
                    dve.wait_ge(s_scored[b], 1 + IT)
                dve.scalar_tensor_tensor(score[:, :, :], score[:, :, :], 0.2, score[:, :, :], ALU.mult, ALU.max).then_inc(s_torow, 1)
                dve.wait_ge(s_inrow, 2)
                for h in range(H):
                    ins = dve.tensor_tensor(S1["rv"][h], PS[0:Q1, h, :], S1["aux"], ALU.add)
                ch.link(ins)
                segment_max(0, S1, True)
                dve.sem_inc(s_max, 1)
                for h in range(H):
                    dve.wait_ge(s_exT, h + 1)
                    dve.tensor_copy(weight[:, :, h].rearrange("p (q k) -> p k q", k=K1),
                                    PS[:, h, 0:NI].rearrange("p (k q) -> p k q", k=K1))
                dve.wait_ge(s_maxT, 1)
                for h in range(H):
                    ins = dve.tensor_copy(score[:, :, h].rearrange("p (q k) -> p k q", k=K1),
                                          PS[:, 4 + h, 0:NI].rearrange("p (k q) -> p k q", k=K1))
                ins.then_inc(s_w8, 1)
                dve.wait_ge(s_w8, 1)
                def weighted_pass(p, before, first, tab, width, targets, nodes, builds):
                    def turn(it, more):
                        for b in range(SL):
                            add_sums(first, before, tab, it, b, width, targets, nodes)
                            if builds and more:
                                build_onehots((s_scat[b], it + (past(*before) + 2)), tab, it + 1, b)

                    if builds:
                        for b in range(SL):
                            build_onehots((s_scat[b], past(*before) + 1), tab, 0, b)
                    with dve.Fori(0, turns[p] - 1) as it:
                        turn(it, True)
                    turn(turns[p] - 1, False)

                weighted_pass("B1", ("A0",), ACC0 + NI, tab1, W1C + H, [acc1, acc1b], NV, True)
                dve.wait_ge(s_acc, ACC0 + 2 * NI)
                dve.wait_ge(s_w1b, 7 * 16)
                ch.link(dve.tensor_tensor(acc1, acc1, acc1b, ALU.add))
                sums, peak = acc1[:, :, D:W1C], acc1[:, :, W1C:W1C + H]
                edge_exp, own_exp, top = (own[:, n, :, :] for n in range(3))
                ch.link(dve.tensor_tensor(own_exp, xh[:, :, D:W1C], ad[:, :, :], ALU.add))
                ch.link(dve.scalar_tensor_tensor(own_exp, own_exp, 0.2, own_exp, ALU.mult, ALU.max))
                ch.link(dve.tensor_scalar(edge_exp, sums, 0.5, -BIG, ALU.is_lt, ALU.mult))
                ch.link(dve.tensor_tensor(edge_exp, edge_exp, peak, ALU.add))
                ch.link(dve.tensor_tensor(top, edge_exp, own_exp, ALU.max))
                dve.tensor_tensor(edge_exp, top, edge_exp, ALU.subtract)
                dve.tensor_tensor(own_exp, top, own_exp, ALU.subtract).then_inc(s_arg, 1)
                dve.wait_ge(s_val, 2)
                ch.link(dve.tensor_tensor(top, sums, edge_exp, ALU.mult))
                ch.link(dve.tensor_tensor(top, top, own_exp, ALU.add))
                ch.link(dve.reciprocal(top, top))
                dve.tensor_tensor(edge_exp, edge_exp, top, ALU.mult)
                ch.link(dve.tensor_tensor(own_exp, own_exp, top, ALU.mult))
                for h in range(H):
                    part = slice(h * C, (h + 1) * C)
                    dve.tensor_tensor(Y[:, :, part], acc1[:, :, part], edge_exp[:, :, h:h + 1].to_broadcast([P, NJ, C]), ALU.mult)
                    ins = dve.tensor_tensor(xh[:, :, part], xh[:, :, part], own_exp[:, :, h:h + 1].to_broadcast([P, NJ, C]), ALU.mult)
                ch.link(ins)
                ch.link(dve.tensor_tensor(Y[:, :, :], Y[:, :, :], xh[:, :, 0:D], ALU.add))
                ch.link(dve.tensor_tensor(Y[:, :, :], Y[:, :, :], everyone(rowv2["gat_b"]), ALU.add))
                ch.link(dve.tensor_tensor(Y[:, :, :], Y[:, :, :], X[:, :, :], ALU.add))
                layer_norm(3, Y[:, :, :], big)
                scale_shift(big, rowv2["ln2_g"][:, :], rowv2["ln2_b"])
                dve.sem_inc(s_ready, 1)
                def stage_normed(it, b):
                    dve.wait_ge(s_turned[b], it + (FFN + 1))
                    dve.tensor_copy(stg[:, b, 0, :], big[:, bass.ds(it * 2 + b, 1), :].rearrange("p o d -> p (o d)")).then_inc(s_staged[b], 1)

                def copy_normed(it, b):
                    dve.wait_ge(s_turned[b], it + (FFN + 2))
                    dve.wait_ge(s_prod[b], it + (FFN + 1))
                    dve.tensor_copy(tT[:, b, 0, :], PS[:, 4 + b, 0:D]).then_inc(s_tcopy[b], 1)

                def add_ffn(it, more):
                    for b in range(2):
                        if more:
                            stage_normed(it + 1, b)
                    for b in range(2):
                        if more:
                            copy_normed(it + 1, b)
                    for b in range(2):
                        yj = Y[:, bass.ds(it * 2 + b, 1), :].rearrange("p o d -> p (o d)")
                        dve.wait_ge(s_prod2[b], it + 2)
                        dve.tensor_tensor(yj, yj, PS[:, 2 + b, 0:D], ALU.add).then_inc(s_take[b], 1)

                for b in range(2):
                    stage_normed(0, b)
                for b in range(2):
                    copy_normed(0, b)
                with dve.Fori(0, NJ // 2 - 1) as it:
                    add_ffn(it, True)
                add_ffn(NJ // 2 - 1, False)
                dve.wait_ge(s_take[0], TABLE2 + 1)
                dve.wait_ge(s_take[1], TABLE2 + 1)
                ch.link(dve.tensor_tensor(Y[:, :, :], Y[:, :, :], everyone(rowv2["b2"]), ALU.add))
                ch.link(dve.tensor_tensor(Y[:, :, :], Y[:, :, :], X[:, :, :], ALU.add))
                layer_norm(4, Y[:, :, :], X[:, :, :])
                dve.wait_ge(s_w2, 15 * 16)
                for n in range(2):
                    for r in range(R):
                        ch.link(dve.tensor_tensor(stg[:, 0, 1, :], WQK[:, (n * R + r) * D:(n * R + r + 1) * D], attq[:, n, :], ALU.mult))
                        dve.tensor_tensor(c4q[:, n, r * D:(r + 1) * D], c4q[:, n, r * D:(r + 1) * D], attq[:, n, :], ALU.mult)
                        ch.link(dve.tensor_reduce(u4[:, n, r:r + 1], stg[:, 0, 1, :], AX.X, ALU.add))
                    ch.link(dve.tensor_reduce(c4[:, n, :], c4q[:, n, :].rearrange("p (r d) -> p r d", d=D), AX.X, ALU.add))
                dve.tensor_tensor(u4[:, 0, :], u4[:, 0, :], u4[:, 1, :], ALU.add)
                ch.link(dve.tensor_tensor(c4[:, 0, :], c4[:, 0, :], c4[:, 1, :], ALU.add))
                ch.link(dve.tensor_scalar(c4[:, 0, :], c4[:, 0, :], a_b[:, 0:1], None, ALU.add))
                dve.sem_inc(s_ready, 1)
                def table_rows(base, before, writes, take):
                    def two_tiles(it, u, turn):
                        for b in range(2):
                            dve.wait_ge(s_prod[b], turn + (base + 2))
                            dve.wait_ge(s_rowdone[2 * u + b], it * (writes * 16) + (1 + before[u]) * 16)
                            take(b, 2 * u + b).then_inc(s_take[b], 1)

                    with dve.Fori(0, NJ // 4) as it:
                        for u in range(2):
                            two_tiles(it, u, it * 2 + u)
                    two_tiles(NJ // 4, 0, NJ // 2 - 1)

                def take_relation_rows(b, n):
                    dve.tensor_copy(trow[:, n, 0:R * D], PS[:, 6 + b, :])
                    return dve.tensor_tensor(trow[:, n, R * D:2 * R * D], PS[:, 2 + b, :], bR, ALU.add)

                table_rows(TABLE2, (0, 0), 2, take_relation_rows)
                for b in range(2):
                    dve.wait_ge(s_take[b], NODE2 + 1)
                dve.sem_inc(s_torow, 1)
                dve.wait_ge(s_inrow, 3)
                fold = lambda m: PS[0:Q2, 2 * m:2 * m + 2, :].rearrange("q n f -> q (n f)")[:, 0:K2 * P]
                dve.tensor_copy(S2["aux"], fold(2))
                ch.link(dve.tensor_copy(S2["dst"], fold(0)))
                ch.link(dve.tensor_copy(S2["g"], fold(1)))
                segment_starts(1, S2)
                ch.link(dve.tensor_copy(rok2, S2["g"]))
                dve.memset(ring2[:, :, :, D:D + 1], 1.0)
                def relation_turn(it, more):
                    for b in range(SL):
                        dve.wait_ge(s_spread1[b], it + (past("A1") + 2))
                        dve.wait_ge(*rows_due("A2", b, it, not more))
                        dve.wait_ge(s_spill[b], it * 16 + (past("A1") + 1) * 16)
                        dve.tensor_tensor(ring2[:, b, :, 0:D], four(2 * b + 1), ring[:, b, :, 0:D], ALU.add).then_inc(s_added[b], 1)
                    for b in range(SL):
                        dve.wait_ge(s_added[b], it + 2)
                        dve.scalar_tensor_tensor(ring2[:, b, :, 0:D], ring2[:, b, :, 0:D], 0.2, ring2[:, b, :, 0:D],
                                                 ALU.mult, ALU.max).then_inc(s_relu[b], 1)
                    for b in range(SL):
                        if more:
                            build_onehots((s_ohturn[b], it + (past("A1") + 2)), tab2, it + 1, b)
                    for b in range(SL):
                        dve.wait_ge(s_s4[b], it + 1)
                        dve.tensor_copy(score2[:, bass.ds(window(b, it), G), :],
                                        PS[:, 2 * b + 1, 0:G * R].rearrange("p (g r) -> p g r", g=G)).then_inc(s_scored[b], 1)

                for b in range(SL):
                    build_onehots((s_ohturn[b], past("A1") + 1), tab2, 0, b)
                with dve.Fori(0, IT2 - 1) as it:
                    relation_turn(it, True)
                relation_turn(IT2 - 1, False)
                for b in range(SL):
                    dve.wait_ge(s_scored[b], 1 + past("A1", "A2"))
                ch.link(dve.tensor_tensor(score2, score2, c4[:, 0, :].unsqueeze(1).to_broadcast([P, NI2, R]), ALU.add))
                dve.scalar_tensor_tensor(score2, score2, 0.2, score2, ALU.mult, ALU.max).then_inc(s_torow, 1)
                dve.wait_ge(s_inrow, 4)
                for r in range(R):
                    ch.link(dve.scalar_tensor_tensor(S2["scratch"], S2["aux"], float(r), rok2, ALU.is_equal, ALU.mult))
                    ch.link(dve.tensor_scalar(S2["scratch"], S2["scratch"], BIG, -BIG, ALU.mult, ALU.add))
                    ch.link(dve.tensor_tensor(S2["rv"][r], fold(r), S2["scratch"], ALU.add))
                segment_max(1, S2, False)
                dve.wait_ge(s_ex, 2 * H)
                rv = S2["rv"]
                dve.tensor_tensor(rv[2], rv[2], rv[3], ALU.add)
                ch.link(dve.tensor_tensor(rv[0], rv[0], rv[1], ALU.add))
                dve.tensor_tensor(rv[0], rv[0], rv[2], ALU.add).then_inc(s_max, 1)
                dve.wait_ge(s_maxT, 2)
                by_row = weight2[:, 0:Q2 * K2].rearrange("p (q k) -> p k q", k=K2)
                dve.memset(weight2[:, Q2 * K2:NI2], 0.0)
                dve.tensor_copy(by_row[:, 0:4, :], PS[:, 0, 0:4 * Q2].rearrange("p (k q) -> p k q", k=4))
                dve.tensor_copy(by_row[:, 4, :], PS[:, 1, 0:Q2]).then_inc(s_w8, 1)
                weighted_pass("B2", ("A0", "B1"), ACC0 + 2 * NI, tab2, D + 1, [acc2], NV2, False)
                dve.wait_ge(s_acc, ACC0 + 2 * NI + NI2)
                ch.link(dve.memset(den2[:, :, :], 0.0))
                rden, flag = den2[:, 0, 0:NV2], den2[:, 1, 0:NV2]
                ch.link(dve.tensor_single_scalar(rden, acc2[:, :, D], 1e-16, ALU.max))
                ch.link(dve.reciprocal(rden, rden))
                ch.link(dve.tensor_tensor(flag, rden, acc2[:, :, D], ALU.mult))
                def stage_relations(it, b):
                    u = (it * 2 + b) * 4
                    dve.wait_ge(s_turned[b], it + (NODE2 + 1))
                    dve.wait_ge(s_prod[b], it + (NODE2 + 1))
                    dve.tensor_tensor(stg[:, b, R, :].rearrange("p (u m) -> p u m", m=M2), pick[:, :].unsqueeze(1).to_broadcast([P, 4, M2]),
                                      den2[:, 1, bass.ds(u, 4)].unsqueeze(2).to_broadcast([P, 4, M2]), ALU.mult)
                    dve.tensor_tensor(stg[:, b, 0:4, :], wide_flat[:, bass.ds(u * (D + 1), 4 * (D + 1))].rearrange("p (u d) -> p u d", d=D + 1)[:, :, 0:D],
                                      den2[:, 0, bass.ds(u, 4)].unsqueeze(2).to_broadcast([P, 4, D]), ALU.mult).then_inc(s_staged[b], 1)

                def take_relations(it, more):
                    for b in range(2):
                        if more:
                            stage_relations(it + 1, b)
                    for b in range(2):
                        dve.wait_ge(s_prod[b], it + (NODE2 + 2))
                        dve.tensor_copy(Y[:, bass.ds(it * 2 + b, 1), :].rearrange("p o d -> p (o d)"), PS[:, 6 + b, 0:D]).then_inc(s_take[b], 1)

                for b in range(2):
                    stage_relations(0, b)
                with dve.Fori(0, NJ // 2 - 1) as it:
                    take_relations(it, True)
                take_relations(NJ // 2 - 1, False)
                for b in range(2):
                    dve.wait_ge(s_take[b], TABLE3 + 1)
                dve.tensor_single_scalar(big, Y[:, :, :], 0.0, ALU.min).then_inc(s_arg, 1)
                ch.link(dve.scalar_tensor_tensor(Y[:, :, :], Y[:, :, :], 0.0, X[:, :, :], ALU.max, ALU.add))
                dve.wait_ge(s_val, 3)
                ch.link(dve.scalar_tensor_tensor(Y[:, :, :], big, -1.0, Y[:, :, :], ALU.add, ALU.add))
                layer_norm(5, Y[:, :, :], X[:, :, :])
                dve.wait_ge(s_w3, 7 * 16)
                ch.link(dve.tensor_tensor(gru_b[:, 0:2 * D], gru_b[:, 0:2 * D], gru_b2[:, :], ALU.add))
                dve.sem_inc(s_ready, 1)
                dve.memset(Y[:, :, :], 0.0)
                def take_messages(b, n):
                    dve.tensor_tensor(trow[:, n, 0:4 * D], PS[:, 6 + b, :], b3[:, 0:4 * D], ALU.add)
                    return dve.tensor_tensor(trow[:, n, 4 * D:8 * D], PS[:, 2 + b, :], b3[:, 4 * D:8 * D], ALU.add)

                table_rows(TABLE3, (2 * (NJ // 4 + 1), 2 * (NJ // 4)), 1, take_messages)
                with dve.Fori(0, IT) as it:
                    for b in range(SL):
                        build_onehots((s_scat[b], it + (past("A0", "B1", "B2") + 1)), tab1, it, b)
                    for b in range(SL):
                        add_sums(ACC0 + 2 * NI + NI2, ("A0", "B1", "B2"), tab1, it, b, D, [Y], NV)
                dve.wait_ge(s_acc, ACC0 + 3 * NI + NI2)
                dve.sem_inc(s_ready, 1)
                with dve.Fori(0, NJ // 2) as it:
                    for b in range(2):
                        dve.wait_ge(s_prod[b], it + (GRU + 2))
                        dve.tensor_tensor(wide[:, bass.ds(it * 2 + b, 1), 0:4 * D].rearrange("p o d -> p (o d)"), PS[:, 6 + b, :], gru_b[:, :], ALU.add).then_inc(s_take[b], 1)
                for b in range(2):
                    dve.wait_ge(s_take[b], GRU + NJ // 2 + 1)
                dve.sem_inc(s_arg, 1)
                dve.wait_ge(s_val, 4)
                rg3, z, n_in, h_n = (wide[:, :, a * D:(a + 1) * D] for a in range(4))
                ch.link(dve.tensor_tensor(h_n, h_n, rg3, ALU.mult))
                dve.tensor_tensor(n_in, n_in, h_n, ALU.add).then_inc(s_arg, 1)
                dve.wait_ge(s_val, 5)
                ch.link(dve.tensor_tensor(Y[:, :, :], X[:, :, :], n_in, ALU.subtract))
                ch.link(dve.tensor_tensor(Y[:, :, :], Y[:, :, :], z, ALU.mult))
                ch.link(dve.tensor_tensor(Y[:, :, :], Y[:, :, :], n_in, ALU.add))
                ch.link(dve.tensor_tensor(Y[:, :, :], Y[:, :, :], X[:, :, :], ALU.add))
                layer_norm(6, Y[:, :, :], X[:, :, :])
                dve.sem_inc(s_final, 1)


_OUTS = [((3125, 128), "float32")]


def kernel(**inputs):
    import numpy as _np
    import concourse.bacc as _bacc
    from concourse import mybir as _mybir
    from concourse.bass_utils import run_bass_kernel_spmd as _run

    nc = _bacc.Bacc("TRN2", target_bir_lowering=False, num_devices=1)
    arrays, args = {}, {}
    for name in inputs:
        a = _np.ascontiguousarray(inputs[name])
        arrays[f"in_{name}_dram"] = a
        args[name] = nc.dram_tensor(f"in_{name}_dram", a.shape, _mybir.dt.from_np(a.dtype), kind="ExternalInput").ap()
    shape, dtype = _OUTS[0]
    out = nc.dram_tensor("out_0_dram", shape, _mybir.dt.from_np(_np.dtype(dtype)), kind="ExternalOutput").ap()
    gnn_stack(nc, args, out)
    r = _run(nc, [arrays], core_ids=[0])
    return r.results[0]["out_0_dram"]
```
